# Optimizing a Trainium2 kernel written in Bass

```python
import numpy as np
import jax
import jax.numpy as jnp

def _softmax(x, axis=-1):
    return jax.nn.softmax(x, axis=axis)

def _gelu(x):
    return jax.nn.gelu(x, approximate=True)

def _silu(x):
    return jax.nn.silu(x)

def _sigmoid(x):
    return jax.nn.sigmoid(x)

def _layernorm(x, axis=-1, eps=1e-05):
    m = jnp.mean(x, axis=axis, keepdims=True)
    v = jnp.var(x, axis=axis, keepdims=True)
    return (x - m) / jnp.sqrt(v + eps)

def _scatter_add(tgt, idx, src, axis=0):
    return tgt.at[idx].add(src)

def _segment_sum(src, seg, n):
    return jax.ops.segment_sum(src, seg, n)
kernel_name = 'mk_hybrid_d1_jaxref_r8_e53339'

def setup_inputs(seed: int=0):
    np.random.seed(seed)
    _w = jnp.asarray

    def _L0_attn_a_setup():
        import jax, jax.numpy as jnp
        import numpy as np
        B, S, D = (2, 256, 128)
        N_HEADS = 16
        HEAD_DIM = D // N_HEADS
        WINDOW = 128
        STRIDE = 64

        def _sparse_mask(s):
            row = jnp.arange(s)[:, None]
            col = jnp.arange(s)[None, :]
            causal = col <= row
            in_window = (col >= row - WINDOW + 1) & causal
            is_global = (col % STRIDE == 0) & causal
            return in_window | is_global
        key = jax.random.key(seed)
        k1, k2, k3 = jax.random.split(key, 3)
        x = jax.random.normal(k1, (B, S, D), dtype=jnp.float32)
        Wqkv = jax.random.normal(k2, (D, 3 * D), dtype=jnp.float32) * 0.02
        Wproj = jax.random.normal(k3, (D, D), dtype=jnp.float32) * 0.02
        return {'x': x, 'Wqkv': Wqkv, 'Wproj': Wproj}
    _L0_attn_a_in = _L0_attn_a_setup()

    def _L0_attn_b_setup():
        import jax, jax.numpy as jnp
        import numpy as np
        import math
        B, N, DIM, H, DH, NNULL = (2, 256, 128, 16, 64, 2)
        SCALE = 8.0
        LN_EPS = 1e-05

        def _alibi_slopes(heads):
            start = 2.0 ** (-2.0 ** (-(math.log2(heads) - 3)))
            return np.array([start * start ** i for i in range(heads)], dtype=np.float32)

        def _l2norm(t):
            n = jnp.sqrt(jnp.sum(t * t, axis=-1, keepdims=True))
            return t / jnp.maximum(n, 1e-12)
        key = jax.random.key(seed)
        ks = jax.random.split(key, 6)
        inner = H * DH
        return {'x': jax.random.normal(ks[0], (B, N, DIM), dtype=jnp.float32), 'norm_g': jnp.ones((DIM,), jnp.float32), 'norm_b': jnp.zeros((DIM,), jnp.float32), 'Wq': jax.random.normal(ks[1], (DIM, inner), jnp.float32) * 0.02, 'Wkv': jax.random.normal(ks[2], (DIM, 2 * inner), jnp.float32) * 0.02, 'q_scale': jnp.ones((DH,), jnp.float32), 'k_scale': jnp.ones((DH,), jnp.float32), 'null_kv': jax.random.normal(ks[3], (H, 2 * NNULL, DH), jnp.float32), 'Wout': jax.random.normal(ks[4], (inner, DIM), jnp.float32) * 0.02}
    _L0_attn_b_in = _L0_attn_b_setup()

    def _L0_ffn_setup():
        import jax, jax.numpy as jnp
        import numpy as np
        DIM = 128

        def _reference_tuple_inner(x, W_r, W_k, W_v, mu_r, mu_k):
            B, T, C = x.shape
            x_prev = jnp.concatenate([jnp.zeros((B, 1, C), x.dtype), x[:, :-1, :]], axis=1)
            xr = mu_r * x + (1.0 - mu_r) * x_prev
            xk = mu_k * x + (1.0 - mu_k) * x_prev
            r = jax.nn.sigmoid(jnp.einsum('btc,dc->btd', xr, W_r))
            k = jnp.einsum('btc,dc->btd', xk, W_k)
            k_act = jnp.square(jax.nn.relu(k))
            out = r * jnp.einsum('btc,dc->btd', k_act, W_v)
            new_state = x[:, -1, :]
            return (out, new_state)
        key = jax.random.key(seed)
        ks = jax.random.split(key, 6)
        B, T, C = (8, 256, DIM)
        x = jax.random.normal(ks[0], (B, T, C), dtype=jnp.float32)
        s = 1.0 / np.sqrt(C)
        W_r = jax.random.uniform(ks[1], (C, C), jnp.float32, -s, s)
        W_k = jax.random.uniform(ks[2], (C, C), jnp.float32, -s, s)
        W_v = jax.random.uniform(ks[3], (C, C), jnp.float32, -s, s)
        mu_r = jax.random.uniform(ks[4], (C,), jnp.float32)
        mu_k = jax.random.uniform(ks[5], (C,), jnp.float32)
        return {'x': x, 'W_r': W_r, 'W_k': W_k, 'W_v': W_v, 'mu_r': mu_r, 'mu_k': mu_k}
    _L0_ffn_in = _L0_ffn_setup()
    _d = {'L0_attn_a_x': _L0_attn_a_in['x'], 'L0_attn_a_Wqkv': _L0_attn_a_in['Wqkv'], 'L0_attn_a_Wproj': _L0_attn_a_in['Wproj'], 'L0_attn_b_norm_g': _L0_attn_b_in['norm_g'], 'L0_attn_b_norm_b': _L0_attn_b_in['norm_b'], 'L0_attn_b_Wq': _L0_attn_b_in['Wq'], 'L0_attn_b_Wkv': _L0_attn_b_in['Wkv'], 'L0_attn_b_q_scale': _L0_attn_b_in['q_scale'], 'L0_attn_b_k_scale': _L0_attn_b_in['k_scale'], 'L0_attn_b_null_kv': _L0_attn_b_in['null_kv'], 'L0_attn_b_Wout': _L0_attn_b_in['Wout'], 'L0_ffn_W_r': _L0_ffn_in['W_r'], 'L0_ffn_W_k': _L0_ffn_in['W_k'], 'L0_ffn_W_v': _L0_ffn_in['W_v'], 'L0_ffn_mu_r': _L0_ffn_in['mu_r'], 'L0_ffn_mu_k': _L0_ffn_in['mu_k']}
    _x0 = _d['L0_attn_a_x']
    _d['L0_attn_a_x'] = jax.random.normal(jax.random.fold_in(jax.random.key(seed), 1), (16, 512, 128), dtype=_x0.dtype)
    del _x0
    return _d

def reference(L0_attn_a_x, L0_attn_a_Wqkv, L0_attn_a_Wproj, L0_attn_b_norm_g, L0_attn_b_norm_b, L0_attn_b_Wq, L0_attn_b_Wkv, L0_attn_b_q_scale, L0_attn_b_k_scale, L0_attn_b_null_kv, L0_attn_b_Wout, L0_ffn_W_r, L0_ffn_W_k, L0_ffn_W_v, L0_ffn_mu_r, L0_ffn_mu_k):

    def _L0_attn_a_ref(x, Wqkv, Wproj):
        import jax, jax.numpy as jnp
        import numpy as np
        B, S, D = (2, 256, 128)
        N_HEADS = 16
        HEAD_DIM = D // N_HEADS
        WINDOW = 128
        STRIDE = 64

        def _sparse_mask(s):
            row = jnp.arange(s)[:, None]
            col = jnp.arange(s)[None, :]
            causal = col <= row
            in_window = (col >= row - WINDOW + 1) & causal
            is_global = (col % STRIDE == 0) & causal
            return in_window | is_global
        b, s, d = x.shape
        qkv = (x @ Wqkv).reshape(b, s, 3, N_HEADS, HEAD_DIM)
        q, k, v = (qkv[:, :, 0], qkv[:, :, 1], qkv[:, :, 2])
        scale = 1.0 / HEAD_DIM ** 0.5
        att = jnp.einsum('bshd,bthd->bhst', q, k) * scale
        can_attend = _sparse_mask(s)
        att = jnp.where(can_attend[None, None], att, -jnp.inf)
        att = jax.nn.softmax(att, axis=-1)
        att = jnp.nan_to_num(att, nan=0.0)
        y = jnp.einsum('bhst,bthd->bshd', att, v).reshape(b, s, d)
        return y @ Wproj

    def _L0_attn_b_ref(x, norm_g, norm_b, Wq, Wkv, q_scale, k_scale, null_kv, Wout):
        import jax, jax.numpy as jnp
        import numpy as np
        import math
        B, N, DIM, H, DH, NNULL = (2, 256, 128, 16, 64, 2)
        SCALE = 8.0
        LN_EPS = 1e-05

        def _alibi_slopes(heads):
            start = 2.0 ** (-2.0 ** (-(math.log2(heads) - 3)))
            return np.array([start * start ** i for i in range(heads)], dtype=np.float32)

        def _l2norm(t):
            n = jnp.sqrt(jnp.sum(t * t, axis=-1, keepdims=True))
            return t / jnp.maximum(n, 1e-12)
        b, n, dim = x.shape
        h, dh, nn = (H, DH, NNULL)
        j = n + nn
        mu = jnp.mean(x, axis=-1, keepdims=True)
        var = jnp.mean((x - mu) ** 2, axis=-1, keepdims=True)
        xn = (x - mu) * jax.lax.rsqrt(var + LN_EPS) * norm_g + norm_b
        q = (xn @ Wq).reshape(b, n, h, dh).transpose(0, 2, 1, 3)
        kv = x @ Wkv
        k, v = jnp.split(kv, 2, axis=-1)
        k = k.reshape(b, n, h, dh).transpose(0, 2, 1, 3)
        v = v.reshape(b, n, h, dh).transpose(0, 2, 1, 3)
        null = null_kv.reshape(h, nn, 2, dh)
        nk = jnp.broadcast_to(null[:, :, 0, :][None], (b, h, nn, dh))
        nv = jnp.broadcast_to(null[:, :, 1, :][None], (b, h, nn, dh))
        k = jnp.concatenate([nk, k], axis=2)
        v = jnp.concatenate([nv, v], axis=2)
        q = _l2norm(q) * q_scale
        k = _l2norm(k) * k_scale
        sim = jnp.einsum('bhid,bhjd->bhij', q, k) * SCALE
        irow = jnp.arange(j - n, j)
        jcol = jnp.arange(j)
        bias = -jnp.abs(jcol[None, :] - irow[:, None]).astype(sim.dtype)
        slopes = jnp.asarray(_alibi_slopes(h))[:, None, None]
        sim = sim + slopes * bias
        causal = jnp.triu(jnp.ones((n, j), dtype=bool), k=j - n + 1)
        neg = jnp.finfo(sim.dtype).max
        sim = jnp.where(causal[None, None], -neg, sim)
        attn = jax.nn.softmax(sim, axis=-1)
        out = jnp.einsum('bhij,bhjd->bhid', attn, v)
        out = out.transpose(0, 2, 1, 3).reshape(b, n, h * dh)
        return out @ Wout

    def _L0_ffn_ref(x, W_r, W_k, W_v, mu_r, mu_k):
        import jax, jax.numpy as jnp
        import numpy as np
        DIM = 128

        def _reference_tuple_inner(x, W_r, W_k, W_v, mu_r, mu_k):
            B, T, C = x.shape
            x_prev = jnp.concatenate([jnp.zeros((B, 1, C), x.dtype), x[:, :-1, :]], axis=1)
            xr = mu_r * x + (1.0 - mu_r) * x_prev
            xk = mu_k * x + (1.0 - mu_k) * x_prev
            r = jax.nn.sigmoid(jnp.einsum('btc,dc->btd', xr, W_r))
            k = jnp.einsum('btc,dc->btd', xk, W_k)
            k_act = jnp.square(jax.nn.relu(k))
            out = r * jnp.einsum('btc,dc->btd', k_act, W_v)
            new_state = x[:, -1, :]
            return (out, new_state)
        return _reference_tuple_inner(x, W_r, W_k, W_v, mu_r, mu_k)[0]
    x = L0_attn_a_x
    x = x + _L0_attn_a_ref(_layernorm(x, axis=-1), L0_attn_a_Wqkv, L0_attn_a_Wproj)
    x = x + _L0_ffn_ref(_layernorm(x, axis=-1), L0_ffn_W_r, L0_ffn_W_k, L0_ffn_W_v, L0_ffn_mu_r, L0_ffn_mu_k)
    x = x + _L0_attn_b_ref(_layernorm(x, axis=-1), L0_attn_b_norm_g, L0_attn_b_norm_b, L0_attn_b_Wq, L0_attn_b_Wkv, L0_attn_b_q_scale, L0_attn_b_k_scale, L0_attn_b_null_kv, L0_attn_b_Wout)
    x = x + _L0_ffn_ref(_layernorm(x, axis=-1), L0_ffn_W_r, L0_ffn_W_k, L0_ffn_W_v, L0_ffn_mu_r, L0_ffn_mu_k)
    return x

_drawn_inputs = setup_inputs


def setup_inputs(seed=0):
    import zlib

    import numpy as np

    out = dict(_drawn_inputs(seed))
    spreads = {'L0_attn_b_norm_g': (1.0, 0.6),
     'L0_attn_b_norm_b': (0.0, 2.0),
     'L0_attn_b_q_scale': (1.0, 0.6),
     'L0_attn_b_k_scale': (1.0, 0.6)}
    factors = {'L0_attn_a_Wqkv': 8.0, 'L0_attn_a_Wproj': 8.0, 'L0_ffn_mu_r': 3.142}
    for name, (base, spread) in spreads.items():
        noise = np.random.default_rng([zlib.crc32(name.encode()), seed]).standard_normal(out[name].shape)
        drawn = base * np.exp(spread * noise) if base else spread * noise
        out[name] = jnp.asarray(drawn.astype(out[name].dtype))
    for name, factor in factors.items():
        out[name] = (out[name] * factor).astype(out[name].dtype)
    return out
```

```python
from contextlib import ExitStack
import math

import concourse.bass as bass
from concourse import mybir

F32 = mybir.dt.float32
F16 = mybir.dt.float16
BF16 = mybir.dt.bfloat16
I32 = mybir.dt.int32
ALU = mybir.AluOpType
ACT = mybir.ActivationFunctionType
AX = mybir.AxisListType

P = 128
D = 128
H = 16
DA = D // H
DB = 64
NN = 2
STRIDE = 64
EPS = 1e-5
WS = 64.0
MASKED = 1e30
REPS = 4
GR = 4
UA = H // 2
OBW = DB + 1
OBH = 7
OBANKS = [(0, 7), (7, 14), (14, 16)]


def program(nc, x, a_wqkv, a_wproj, b_g, b_b, b_wq, b_wkv, b_qs, b_ks, b_nullkv, b_wout,
            f_wr, f_wk, f_wv, f_mur, f_muk, out):
    NS, S, _ = x.shape
    T = S // P
    NG = S // STRIDE // 2
    C_A = 1.0 / (WS * WS * math.sqrt(DA))
    start = 2.0 ** (-2.0 ** (-(math.log2(H) - 3)))
    slopes = [start * start ** h for h in range(H)]
    NUA, NUB = T * UA, T * H

    ctx = ExitStack()
    with ctx:
        def sb(name, shape, dt=F32):
            return ctx.enter_context(nc.sbuf_tensor(name, shape, dt))

        def sem(name):
            return ctx.enter_context(nc.semaphore(name))

        def bank(name, dt=F32):
            return ctx.enter_context(nc.psum_tensor(name, [P, 512], dt))
        SC = [bank("scores0"), bank("scores1")]
        TR = [bank("turned0"), bank("turned1")]
        OB = [bank("out0"), bank("out1"), bank("out2")]
        MB = bank("misc")
        PROJ = [SC[0], SC[1], TR[0], TR[1]]

        scratch = sb("scratch", [P, 8 * S])
        split_space = sb("split_space", [P, 4 * S])
        bias_space = sb("bias_space", [P, 2 * S])
        prob_space = sb("prob_space", [P, 2 * S])
        turned_space = sb("turned_space", [P, 3 * S])
        stack_space = sb("stack_space", [P, H * S], F16)

        def half(space, a, b, **dims):
            return space[:, a:b].bitcast(F16).rearrange("p (n s) -> p n s", s=S)

        wst = scratch[:, 0:2048]
        wa4 = scratch[:, 2048:3072].rearrange("p (k h r d) -> p k h r d", k=2, h=H, r=REPS)
        wa_sb = scratch[:, 3072:3072 + 3 * D]
        wfn = scratch[:, 3456:3456 + 3 * D].rearrange("p (k d) -> p k d", k=3)
        dist_i = bias_space[:, 0:S].bitcast(I32)
        dist = bias_space[:, S:2 * S]
        prev = scratch[:, 0:2 * S].rearrange("p (k s) -> p k s", k=2)
        mixed = scratch[:, 2 * S:4 * S].rearrange("p (k s) -> p k s", k=2)
        kr, ka, ez, ez1 = [scratch[:, j * S:(j + 1) * S] for j in range(4, 8)]
        gate, gv = kr, prev[:, 0, :]
        ka4 = stack_space[:, 0:GR * S].rearrange("p (g s) -> p g s", g=GR)
        qa4 = stack_space[:, GR * S:2 * GR * S].rearrange("p (g s) -> p g s", g=GR)
        ht = stack_space[:, 2 * GR * S:(2 * GR + 2) * S].rearrange("p (g s) -> p g s", g=2)
        raw = scratch[:].rearrange("p (n s) -> p n s", s=S)
        nh = half(split_space, 0, 2 * S).rearrange("p (a b) s -> p a b s", a=2)
        nl = half(split_space, 2 * S, 4 * S).rearrange("p (a b) s -> p a b s", a=2)
        sq = bias_space[:].rearrange("p (n s) -> p n s", s=S)
        xq = prob_space[:, 0:S]
        xqh, xql = [half(prob_space, S, 2 * S)[:, j, :] for j in range(2)]
        ssc, rn = turned_space[0:96, 0:S], turned_space[0:96, S:2 * S]
        rnh, rns = [half(turned_space, 2 * S, 3 * S)[0:96, j, :] for j in range(2)]
        qst = stack_space[:].rearrange("p (h s) -> p h s", h=H)
        prob = prob_space[:].rearrange("p (n s) -> p n s", s=S)
        pth = half(turned_space, 0, 3 * S // 2)
        ptl = half(turned_space, 3 * S // 2, 3 * S)
        sbias = bias_space[:].rearrange("p (n s) -> p n s", s=S)
        ob = split_space[:, 0:H * DB].rearrange("p (h d) -> p h d", h=H)
        obt = split_space[:, H * DB:2 * H * DB].rearrange("p (c q) -> p c q", q=P)

        ident = sb("ident", [P, P])
        identb = sb("identb", [P, P], BF16)
        mask_a = sb("mask_a", [P, 2, 2 * P], BF16)
        lo_rows = sb("lo_rows", [P, 3])
        rowi = sb("rowi", [P, 3], I32)
        alibi = sb("alibi", [P, H, S])
        null_i = sb("null_i", [P, T, NN], I32)
        null_f = sb("null_f", [P, T, NN])
        alibi_null = sb("alibi_null", [P, T, NN, H])
        blk = sb("blk", [P, H])
        head_sum = sb("head_sum", [P, 8, 96])
        head_fan = sb("head_fan", [96, 8, P], F16)
        fan_row = sb("fan_row", [P, 2, H])
        epsb = sb("epsb", [P, 4])
        wa4h = sb("wa4h", [P, 2, GR, P], F16)
        wa4l = sb("wa4l", [P, 2, GR, P], F16)
        wavh = sb("wavh", [P, D], F16)
        wavl = sb("wavl", [P, D], F16)
        wproj = sb("wproj", [P, D])
        wbh = sb("wbh", [P, 3, H * DB], F16)
        wbl = sb("wbl", [P, 3, H * DB], F16)
        wout = sb("wout", [P, 8, D])
        wft = sb("wft", [P, 3, D])
        cols = sb("cols", [P, 6])
        colx = sb("colx", [P, 3])
        nk_sb = sb("nk_sb", [NN * H, 2, DB])
        nkd = sb("nkd", [NN * H, 2 * DB])
        nks = sb("nks", [NN * H, 4])
        nkf = sb("nkf", [P, NN * H])
        nkh = sb("nkh", [P, NN * H], F16)
        nkl = sb("nkl", [P, NN * H], F16)
        nvh = sb("nvh", [NN * H, DB], F16)
        nvl = sb("nvl", [NN * H, DB], F16)
        nvbh = sb("nvbh", [NN * H, H, OBW], F16)
        nvbl = sb("nvbl", [NN * H, H, OBW], F16)

        x_in = sb("x_in", [P, T, D])
        x_a = sb("x_a", [P, T, D])
        x_f = sb("x_f", [P, T, D])
        xn = sb("xn", [P, T, D])
        xr2 = sb("xr2", [P, T, D])
        stats = sb("stats", [P, T, 6])
        mv = sb("mv", [P, T, 2])
        lnv = sb("lnv", [P, T])
        rstd = sb("rstd", [P, T])
        xh = sb("xh", [P, S], F16)
        xl = sb("xl", [P, S], F16)
        xg = sb("xg", [P, 2, NG * H], F16)
        km = sb("km", [P, H, S], F16)
        vah = sb("vah", [P, T, H, DA + 1], F16)
        val = sb("val", [P, T, H, DA + 1], F16)
        vgt = sb("vgt", [NG * H, H, DA])
        vgh = sb("vgh", [NG * H, H, DA + 1], F16)
        vgl = sb("vgl", [NG * H, H, DA + 1], F16)
        sgs = sb("sgs", [P, NG * H])
        gmin = sb("gmin", [P, H])
        amin = sb("amin", [P, H])
        abias = sb("abias", [P, 2, H])
        gt = sb("gt", [P, NG * H])
        pg = sb("pg", [P, NG * H])
        pgh = sb("pgh", [NG * H, P], F16)
        pgl = sb("pgl", [NG * H, P], F16)
        oa = sb("oa", [P, D])
        oat = sb("oat", [P, D])
        rden = sb("rden", [P, H])
        kh = sb("kh", [P, H, S], F16)
        kl = sb("kl", [P, H, S], F16)
        vbh = sb("vbh", [P, T, H, OBW], F16)
        vbl = sb("vbl", [P, T, H, OBW], F16)
        snb = sb("snb", [P, 2, NN, H])
        nmin = sb("nmin", [P, H])
        bmin = sb("bmin", [P, 2, H])
        nt = sb("nt", [P, NN * H])
        pn = sb("pn", [P, NN * H])
        pnh = sb("pnh", [NN * H, P], F16)
        pnl = sb("pnl", [NN * H, P], F16)
        xt = sb("xt", [P, 1 + S])

        x_b = x_out = x_a
        xn2 = xr2[:]

        w_loaded = sem("w_loaded")
        w_staged = sem("w_staged")
        pool_setup = sem("pool_setup")
        vec_setup = sem("vec_setup")
        act_setup = sem("act_setup")
        ident_ready = sem("ident_ready")
        iotas_ready = sem("iotas_ready")
        pool_ready = sem("pool_ready")
        alibi_ready = sem("alibi_ready")
        null_ss = sem("null_ss")
        wq_split = sem("wq_split")
        nulls_scaled = sem("nulls_scaled")
        vec_ready = sem("vec_ready")
        wav_hi = sem("wav_hi")
        wq_hi = sem("wq_hi")
        null_root = sem("null_root")
        nv_hi = sem("nv_hi")
        act_ready = sem("act_ready")
        mix_turned = sem("mix_turned")
        nulls_turned = sem("nulls_turned")
        x_first = sem("x_first")
        x_loaded = sem("x_loaded")
        x_stored = sem("x_stored")
        vec_order = sem("vec_order")
        act_order = sem("act_order")
        var_ready = sem("var_ready")
        rstd_ready = sem("rstd_ready")
        ln_ready = sem("ln_ready")
        turned_x = sem("turned_x")
        xh_ready = sem("xh_ready")
        xl_ready = sem("xl_ready")
        xg_ready = sem("xg_ready")
        a_proj = sem("a_proj")
        a_hi = sem("a_hi")
        a_stacked = sem("a_stacked")
        a_keys = sem("a_keys")
        va_proj = sem("va_proj")
        va_hi = sem("va_hi")
        va_ready = sem("va_ready")
        vg_proj = sem("vg_proj")
        vg_ready = sem("vg_ready")
        a_scores = sem("a_scores")
        a_globals = sem("a_globals")
        a_bias = sem("a_bias")
        a_exp = sem("a_exp")
        a_turned = sem("a_turned")
        a_pthi = sem("a_pthi")
        a_ptlo = sem("a_ptlo")
        a_pv = sem("a_pv")
        a_gsaved = sem("a_gsaved")
        a_gt = sem("a_gt")
        a_gexp = sem("a_gexp")
        a_gturned = sem("a_gturned")
        a_ghi = sem("a_ghi")
        a_glo = sem("a_glo")
        a_out = sem("a_out")
        a_normed = sem("a_normed")
        a_oturned = sem("a_oturned")
        a_oat = sem("a_oat")
        a_y = sem("a_y")
        a_added = sem("a_added")
        f_xt = sem("f_xt")
        f_mixed = sem("f_mixed")
        f_k = sem("f_k")
        f_r = sem("f_r")
        f_relu = sem("f_relu")
        f_e = sem("f_e")
        f_e1 = sem("f_e1")
        f_gate = sem("f_gate")
        f_ka = sem("f_ka")
        f_v = sem("f_v")
        f_done = sem("f_done")
        xq_ready = sem("xq_ready")
        b_proj = sem("b_proj")
        b_raw = sem("b_raw")
        b_sq = sem("b_sq")
        b_ss = sem("b_ss")
        b_clamped = sem("b_clamped")
        b_rn = sem("b_rn")
        b_rns = sem("b_rns")
        b_fan = sem("b_fan")
        b_norm = sem("b_norm")
        b_nhi = sem("b_nhi")
        b_nlo = sem("b_nlo")
        b_spread = [sem(f"b_spread{j}") for j in range(2)]
        vb_proj = sem("vb_proj")
        vb_hi = sem("vb_hi")
        vb_lo = sem("vb_lo")
        b_null = sem("b_null")
        b_nbias = sem("b_nbias")
        b_scores = sem("b_scores")
        b_biased = sem("b_biased")
        b_exp = sem("b_exp")
        b_turned = sem("b_turned")
        b_pthi = sem("b_pthi")
        b_ptlo = sem("b_ptlo")
        b_pv = sem("b_pv")
        b_nt = sem("b_nt")
        b_nexp = sem("b_nexp")
        b_nturned = sem("b_nturned")
        b_nhi2 = sem("b_nhi2")
        b_nlo2 = sem("b_nlo2")
        b_out = sem("b_out")
        b_normed = sem("b_normed")
        b_oturned = sem("b_oturned")
        b_obt = sem("b_obt")
        b_y = sem("b_y")
        b_added = sem("b_added")

        last_sem = b_added

        def spread(pair):
            m = pair // 2 + 1
            return b_spread[pair % 2], 16 * (8 * min(m, 2) + 4 * max(m - 2, 0))

        def waits(eng):
            def wait(s, n):
                if n > 0:
                    eng.wait_ge(s, n)
            return wait

        def copy(o, i, **kw):
            return nc.scalar.activation(o, i, ACT.Copy, **kw)

        def product(o, ah, al, bh, bl, first=True, last=True):
            nc.tensor.matmul(o, ah, bh, start=first, stop=False, skip_group_check=True)
            nc.tensor.matmul(o, al, bh, start=False, stop=False, skip_group_check=True)
            return nc.tensor.matmul(o, ah, bl, start=False, stop=last, skip_group_check=True)

        class Order:
            def __init__(self, eng, s):
                self.eng, self.s, self.n = eng, s, 0

            def done(self, ins):
                ins.then_inc(self.s, 1)
                self.n += 1
                self.eng.wait_ge(self.s, self.n)

        with nc.Block() as block:
            @block.sync
            def _(sp):
                def load(dst, src):
                    sp.dma_start(dst, src).then_inc(w_loaded, 16)
                sp.dma_start(x_in[:], x[0].rearrange("(t p) d -> p t d", p=P)).then_inc(x_first, 16)
                load(wa_sb[:], a_wqkv)
                load(wproj[:], a_wproj)
                load(wst[:, 0:1024], b_wq)
                load(wout[:], b_wout.rearrange("(c p) n -> p c n", p=P))
                load(wfn[:, 0, :], f_wr)
                load(wfn[:, 1, :], f_wk)
                load(wfn[:, 2, :], f_wv)
                for c, v in ((0, b_g), (1, b_b), (4, f_mur), (5, f_muk)):
                    load(cols[:, c:c + 1], v.rearrange("(p o) -> p o", o=1))
                for c, v in ((2, b_qs), (3, b_ks)):
                    for half in range(2):
                        load(cols[half * DB:half * DB + DB, c:c + 1], v.rearrange("(p o) -> p o", o=1))
                null = b_nullkv.rearrange("h (n c) d -> n h c d", c=2)
                for n in range(NN):
                    load(nk_sb[n * H:(n + 1) * H, :, :], null[n])
                sp.wait_ge(wq_split, 1)
                sp.dma_start(wst[:], b_wkv).then_inc(w_staged, 16)

            @block.gpsimd
            def _(pool):
                g = nc.gpsimd
                n = [0]

                def done(ins):
                    ins.then_inc(pool_setup, 1)
                    n[0] += 1
                    pool.wait_ge(pool_setup, n[0])

                done(g.memset(ident[:], 0.0))
                g.affine_select(out=ident[:], in_=ident[:], compare_op=ALU.not_equal, fill=1.0,
                                base=0, pattern=[[-1, P]], channel_multiplier=1).then_inc(ident_ready, 1)
                done(g.memset(mask_a[:], 0.0))
                for hh in range(2):
                    done(g.affine_select(out=mask_a[:, hh, 0:P], in_=mask_a[:, hh, 0:P], compare_op=ALU.is_gt,
                                         fill=MASKED, base=0, pattern=[[1, P]], channel_multiplier=-1))
                    done(g.affine_select(out=mask_a[:, hh, P:2 * P], in_=mask_a[:, hh, P:2 * P], compare_op=ALU.is_ge,
                                         fill=MASKED, base=0, pattern=[[-1, P]], channel_multiplier=1))
                    for k in range(0, P, STRIDE):
                        done(g.memset(mask_a[:, hh, k:k + 1], 0.0))
                done(g.iota(dist_i[:], pattern=[[-1, S]], base=S - P, channel_multiplier=1))
                done(g.iota(null_i[:], pattern=[[P, T], [-1, NN]], base=NN, channel_multiplier=1))
                g.iota(rowi[:], pattern=[[0, 3]], base=0, channel_multiplier=1).then_inc(iotas_ready, 1)
                done(g.memset(km[:], 0.0))
                done(g.memset(head_sum[:], 0.0))
                for b in range(8):
                    for j in range(2):
                        done(g.memset(head_sum[j * DB:j * DB + DB, b, 2 * b + j:96:H], 1.0))
                pool.wait_ge(alibi_ready, 1)
                g.affine_select(out=alibi[:, :, S - P:S], in_=alibi[:, :, S - P:S], compare_op=ALU.is_ge, fill=MASKED,
                                base=0, pattern=[[0, H], [-1, P]], channel_multiplier=1).then_inc(pool_ready, 1)

            @block.tensor
            def _(pe):
                pe.wait_ge(ident_ready, 1)
                pe.wait_ge(w_loaded, 16 * WLOADS)
                for k in range(3):
                    ins = pe.transpose(MB[:, k * D:(k + 1) * D], wfn[:, k, :], ident[:])
                ins.then_inc(mix_turned, 1)
                pe.wait_ge(nulls_scaled, 1)
                pe.transpose(OB[0][:, 0:NN * H], nkd[:], ident[0:NN * H, 0:NN * H]).then_inc(nulls_turned, 1)
                pe.wait_ge(vec_ready, 1)
                pe.wait_ge(act_ready, 1)
                pe.wait_ge(pool_ready, 1)

            @block.scalar
            def _(act):
                n = [0]

                def done(ins):
                    ins.then_inc(act_setup, 1)
                    n[0] += 1
                    act.wait_ge(act_setup, n[0])
                act.wait_ge(w_loaded, 16 * WLOADS)
                copy(wavh[:], wa_sb[:, 2 * D:3 * D], scale=WS).then_inc(wav_hi, 1)
                copy(wbh[:, 0, :], wst[:, 0:1024], scale=WS).then_inc(wq_hi, 1)
                act.wait_ge(null_ss, 1)
                done(act.activation(nks[:, 2:3], nks[:, 1:2], ACT.Ln, scale=2.0 ** 20))
                act.activation(nks[:, 3:4], nks[:, 2:3], ACT.Exp, scale=-0.5, bias=epsb[0:NN * H, 2:3]).then_inc(null_root, 1)
                copy(nvh[:], nk_sb[:, 1, :], scale=WS).then_inc(nv_hi, 1)
                act.wait_ge(w_staged, 16)
                copy(wbh[:, 1:3, :].rearrange("p k n -> p (k n)"), wst[:], scale=WS).then_inc(act_ready, 1)
                act.wait_ge(vec_ready, 1)

            @block.vector
            def _(v):
                n = [0]

                def done(ins):
                    ins.then_inc(vec_setup, 1)
                    n[0] += 1
                    v.wait_ge(vec_setup, n[0])

                v.wait_ge(iotas_ready, 1)
                done(v.tensor_copy(dist[:], dist_i[:]))
                for h in range(H):
                    ins = v.tensor_scalar(alibi[:, h, :], dist[:], slopes[h], None, ALU.mult)
                ins.then_inc(alibi_ready, 1)
                done(v.tensor_copy(null_f[:], null_i[:]))
                for h in range(H):
                    ins = v.tensor_scalar(alibi_null[:, :, :, h], null_f[:], slopes[h], None, ALU.mult)
                done(ins)
                for c, sh in ((0, 3), (1, 4), (2, 4)):
                    done(v.tensor_scalar(rowi[:, c:c + 1], rowi[:, c:c + 1], sh, None, ALU.logical_shift_right))
                done(v.tensor_scalar(rowi[:, 0:2], rowi[:, 0:2], 1, None, ALU.bitwise_and))
                done(v.tensor_copy(lo_rows[:], rowi[:]))
                done(v.tensor_scalar(lo_rows[:, 2:3], lo_rows[:, 2:3], 1.0, None, ALU.is_equal))
                done(v.tensor_scalar(lo_rows[:], lo_rows[:], -1.0, None, ALU.mult))
                v.memset(epsb[:, 0:1], EPS)
                v.memset(epsb[:, 1:2], math.log(1024.0) + 0.5 * math.log(256.0))
                done(v.memset(epsb[:, 2:4], 0.5 * math.log(2.0 ** 20)))
                v.wait_ge(ident_ready, 1)
                done(v.tensor_copy(identb[:], ident[:]))
                done(v.tensor_scalar(blk[:], ident[:, 0:H], WS, None, ALU.mult))
                for r in range(1, 8):
                    done(v.scalar_tensor_tensor(out=blk[:], in0=ident[:, r * H:(r + 1) * H], scalar=WS, in1=blk[:],
                                                op0=ALU.mult, op1=ALU.add))
                done(v.tensor_scalar(fan_row[:, 0, :], blk[:], 1.0 / WS / 1024.0, None, ALU.mult))
                done(v.memset(head_fan[:], 0.0))
                for b in range(8):
                    done(v.tensor_copy(head_fan[0:32, b, :].rearrange("p (j d) -> p j d", j=2),
                                       fan_row[0:32, 0, 2 * b:2 * b + 2].unsqueeze(2).broadcast_to([32, 2, DB])))
                v.memset(xt[:, 0:1], 0.0)
                for tile, c in ((vah, WS), (val, 0.0)):
                    v.memset(tile[:, :, :, DA:DA + 1], c)
                for tile, c in ((vbh, WS), (vbl, 0.0)):
                    v.memset(tile[:, :, :, DB:DB + 1], c)
                v.memset(vgl[:, :, DA:DA + 1], 0.0)
                v.tensor_copy(vgh[:, :, DA:DA + 1], blk[0:NG * H, :].unsqueeze(2))
                v.memset(nvbl[:, :, DB:DB + 1], 0.0)
                done(v.tensor_copy(nvbh[:, :, DB:DB + 1], blk[0:NN * H, :].unsqueeze(2)))
                v.wait_ge(w_loaded, 16 * WLOADS)
                done(v.tensor_tensor(nkd[:, 0:DB], nk_sb[:, 0, :], nk_sb[:, 0, :], ALU.mult))
                done(v.tensor_reduce(nks[:, 0:1], nkd[:, 0:DB], AX.X, ALU.add))
                v.tensor_scalar(nks[:, 1:2], nks[:, 0:1], 1e-24, None, ALU.max).then_inc(null_ss, 1)
                for kind, sc in ((0, -WS), (1, WS)):
                    w = wa_sb[:, kind * D:(kind + 1) * D].rearrange("p (h d) -> p h d", d=DA)
                    for r in range(REPS):
                        ins = v.tensor_scalar(wa4[:, kind, :, r, :], w, sc, None, ALU.mult)
                done(ins)
                wv = wa4[:].rearrange("p k h r d -> p (k h r d)")
                whv = wa4h[:].rearrange("p k g c -> p (k g c)")
                wlv = wa4l[:].rearrange("p k g c -> p (k g c)")
                done(v.tensor_copy(whv, wv))
                done(v.tensor_tensor(wlv, wv, whv, ALU.subtract))
                done(v.tensor_scalar(colx[:, 0:1], cols[:, 2:3], -8.0, None, ALU.mult))
                done(v.tensor_scalar(colx[:, 1:3], cols[:, 4:6], -1.0, 1.0, ALU.mult, ALU.add))
                v.wait_ge(wav_hi, 1)
                done(v.scalar_tensor_tensor(out=wavl[:], in0=wa_sb[:, 2 * D:3 * D], scalar=WS, in1=wavh[:],
                                            op0=ALU.mult, op1=ALU.subtract))
                v.wait_ge(wq_hi, 1)
                v.scalar_tensor_tensor(out=wbl[:, 0, :], in0=wst[:, 0:1024], scalar=WS, in1=wbh[:, 0, :],
                                       op0=ALU.mult, op1=ALU.subtract).then_inc(wq_split, 1)
                v.wait_ge(null_root, 1)
                for half in range(2):
                    ins = v.tensor_scalar(nkd[:, half * DB:(half + 1) * DB], nk_sb[:, 0, :], nks[:, 3:4], None, ALU.mult)
                ins.then_inc(nulls_scaled, 1)
                v.wait_ge(nv_hi, 1)
                done(v.scalar_tensor_tensor(out=nvl[:], in0=nk_sb[:, 1, :], scalar=WS, in1=nvh[:],
                                            op0=ALU.mult, op1=ALU.subtract))
                b1 = fan_row[0:NN * H, 1, :]
                done(v.tensor_scalar(b1, blk[0:NN * H, :], 1.0 / WS, None, ALU.mult))
                bb = b1.unsqueeze(2).broadcast_to([NN * H, H, DB])
                done(v.tensor_tensor(nvbh[:, :, 0:DB], nvh[:].unsqueeze(1).broadcast_to([NN * H, H, DB]), bb, ALU.mult))
                done(v.tensor_tensor(nvbl[:, :, 0:DB], nvl[:].unsqueeze(1).broadcast_to([NN * H, H, DB]), bb, ALU.mult))
                v.wait_ge(mix_turned, 1)
                done(v.tensor_copy(wft[:].rearrange("p k d -> p (k d)"), MB[:, 0:3 * D]))
                v.wait_ge(nulls_turned, 1)
                done(v.tensor_scalar(nkf[:], OB[0][:, 0:NN * H], cols[:, 3:4], None, ALU.mult))
                done(v.tensor_copy(nkh[:], nkf[:]))
                done(v.tensor_tensor(nkl[:], nkf[:], nkh[:], ALU.subtract))
                v.wait_ge(act_ready, 1)
                v.scalar_tensor_tensor(out=wbl[:, 1:3, :].rearrange("p k n -> p (k n)"), in0=wst[:], scalar=WS,
                                       in1=wbh[:, 1:3, :].rearrange("p k n -> p (k n)"),
                                       op0=ALU.mult, op1=ALU.subtract).then_inc(vec_ready, 1)
                v.wait_ge(pool_ready, 1)

        with nc.Fori(0, NS) as seq:
          with nc.Block() as block:
            @block.sync
            def _(sp):
                wait = waits(sp)
                wait(a_stacked, 4)
                kmv = km[:].rearrange("p (g r) s -> p g r s", r=GR)
                for r in range(GR):
                    sp.dma_start(kmv[32 * r:32 * r + 32, :, r, :],
                                 ka4[32 * r:32 * r + 32, :, :]).then_inc(a_keys, 16)
                wait(a_added, T)
                sp.dma_start(x_in[:], x[(seq + 1) % NS].rearrange("(t p) d -> p t d", p=P)).then_inc(x_loaded, 16)
                for kind in range(2):
                    for pair in range(4):
                        n = kind * 8 + 2 * pair + 2
                        wait(b_nhi, n)
                        wait(b_nlo, n)
                        for j in range(2):
                            for (src, tile, half) in (((nh, qst, 0), (nl, qst, 1)) if kind else
                                                      ((nh, kh, 0), (nh, kh, 1), (nl, kl, 0), (nl, kl, 1))):
                                sp.dma_start(
                                    tile[half * DB:half * DB + DB, 4 * pair + j:4 * pair + j + 3:2, :],
                                    src[j * DB:j * DB + DB, pair % 2, :, :]).then_inc(b_spread[pair % 2], 16)
                wait(f_done, 2)
                sp.dma_start(out[seq].rearrange("(t p) d -> p t d", p=P), x_out[:]).then_inc(x_stored, 16)
                wait(x_stored, 16)
                wait(x_loaded, 16)

            @block.gpsimd
            def _(pool):
                wait = waits(pool)
                for a in range(16):
                    wait(b_nhi, a + 1)
                    if a >= 4:
                        wait(*spread(a // 2 - 2))
                    nc.gpsimd.tensor_tensor(nl[:, (a // 2) % 2, a % 2, :], raw[:, a % 8, :], nh[:, (a // 2) % 2, a % 2, :],
                                    ALU.subtract).then_inc(b_nlo, 1)

            @block.tensor
            def _(pe):
                wait = waits(pe)

                def turn_x(n, src, dst):
                    wait(ln_ready, n + 1)
                    for t in range(T):
                        ins = pe.transpose(dst[:, t * P:(t + 1) * P], src[:, t, :], ident[:])
                    ins.then_inc(turned_x, 1)

                def mix(n):
                    turn_x(1 if n == 0 else 4, xn, MB)
                    wait(f_mixed, 2 * n + 1)
                    pe.matmul(SC[0][:], wft[:, 1, :], mixed[:, 1, :], start=True, stop=True).then_inc(f_k, 1)
                    wait(f_mixed, 2 * n + 2)
                    for t in range(T):
                        ins = pe.matmul(SC[1][:, t * P:(t + 1) * P], mixed[:, 0, t * P:(t + 1) * P], wft[:, 0, :],
                                        start=True, stop=True)
                    ins.then_inc(f_r, 1)
                    wait(f_ka, n + 1)
                    for t in range(T):
                        ins = pe.matmul(TR[0][:, t * P:(t + 1) * P], ka[:, t * P:(t + 1) * P], wft[:, 2, :],
                                        start=True, stop=True)
                    ins.then_inc(f_v, 1)

                turn_x(0, xn, MB)
                wait(xl_ready, 1)
                for a in range(8):
                    kind, grp = 1 - a // 4, a % 4
                    if a >= 4:
                        wait(a_stacked, a - 3)
                    product(PROJ[a % 4][:], wa4h[:, kind, grp, :], wa4l[:, kind, grp, :], xh[:], xl[:]).then_inc(a_proj, 1)
                for t in range(T):
                    s = slice(t * P, (t + 1) * P)
                    ins = product(MB[:, s], xh[:, s], xl[:, s], wavh[:], wavl[:])
                ins.then_inc(va_proj, 1)
                wait(xg_ready, 1)
                product(OB[0][0:NG * H, 0:D], xg[:, 0, :], xg[:, 1, :], wavh[:], wavl[:]).then_inc(vg_proj, 1)

                def a_sc(u):
                    i, hp = u // UA, u % UA
                    nk = min(i + 1, 2)
                    b = SC[u % 2]
                    if u >= 2:
                        wait(a_exp, u - 1)
                    pe.matmul(b[:, 0:2 * nk * P], identb[:], mask_a[:, :, (2 - nk) * P:2 * P],
                              start=True, stop=False, skip_group_check=True)
                    for hh in range(2):
                        h = 2 * hp + hh
                        ins = pe.matmul(b[:, hh * nk * P:(hh + 1) * nk * P], qa4[:, h // GR, i * P:(i + 1) * P],
                                        km[:, h, (i + 1 - nk) * P:(i + 1) * P], start=False, stop=True,
                                        skip_group_check=True)
                    ins.then_inc(a_scores, 1)

                def a_glob(i):
                    ng = 2 * (i - 1)
                    v = MB[:, 0:ng * H].rearrange("p (g h) -> p h g", h=H)
                    for grp in range(GR):
                        ins = pe.matmul(v[:, GR * grp:GR * (grp + 1), :], qa4[:, grp, i * P:(i + 1) * P],
                                        km[:, GR * grp:GR * (grp + 1), 0:ng * STRIDE:STRIDE], start=True, stop=True)
                    ins.then_inc(a_globals, 1)

                def a_turn(u):
                    nk = min(u // UA + 1, 2)
                    wait(a_exp, u + 1)
                    if u >= 2:
                        wait(a_ptlo, u - 1)
                    for c in range(2 * nk):
                        ins = pe.transpose(TR[u % 2][:, c * P:(c + 1) * P], prob[:, u % 2, c * P:(c + 1) * P], ident[:])
                    ins.then_inc(a_turned, 1)

                def a_pvs(u):
                    i, hp = u // UA, u % UA
                    nk = min(i + 1, 2)
                    wait(a_ptlo, u + 1)
                    if hp == 0 and i >= 2:
                        wait(a_normed, i - 1)
                    for hh in range(2):
                        h = 2 * hp + hh
                        o = OB[i % 2][:, h * (DA + 1):(h + 1) * (DA + 1)]
                        for c in range(nk):
                            kt = i + 1 - nk + c
                            s = slice((hh * nk + c) * P, (hh * nk + c + 1) * P)
                            ins = product(o, pth[:, u % 3, s], ptl[:, u % 3, s], vah[:, kt, h, :], val[:, kt, h, :],
                                          first=(hp == 0 and hh == 0 and c == 0))
                    ins.then_inc(a_pv, 1)

                def a_gturn(i):
                    ng = 2 * (i - 1)
                    wait(a_gexp, i - 1)
                    wait(a_gsaved, 2)
                    pe.transpose(MB[0:ng * H, 0:P], pg[:, 0:ng * H], ident[:]).then_inc(a_gturned, 1)

                def a_gpv(i):
                    ng = 2 * (i - 1)
                    wait(a_glo, i - 1)
                    v = slice(0, ng * H)
                    product(OB[i % 2][:, 0:H * (DA + 1)], pgh[v, :], pgl[v, :], vgh[v, :, :].rearrange("p h d -> p (h d)"),
                            vgl[v, :, :].rearrange("p h d -> p (h d)"), first=False).then_inc(a_out, 1)

                wait(a_stacked, 8)
                wait(a_keys, 64)
                wait(va_ready, 1)
                wait(vg_ready, 1)
                a_sc(0)
                a_sc(1)
                for s in range(NUA + 8):
                    i = s // UA
                    if s < NUA:
                        a_turn(s)
                    if s % UA == 0 and i >= 3 and i <= T:
                        a_gturn(i - 1)
                    if s + 2 < NUA:
                        if (s + 2) % UA == 0 and (s + 2) // UA >= 2:
                            if (s + 2) // UA == 3:
                                wait(a_gsaved, 1)
                            a_glob((s + 2) // UA)
                        a_sc(s + 2)
                    if 1 <= s <= NUA:
                        a_pvs(s - 1)
                    if s % UA == 1 and i >= 1:
                        if i >= 3:
                            a_gpv(i - 1)
                    if s % UA == 3 and i >= 1:
                        wait(a_normed, i)
                        if i >= 2:
                            wait(a_added, i - 1)
                        pe.transpose(OB[2][:, 0:P], oa[:], ident[:]).then_inc(a_oturned, 1)
                    if s % UA == 5 and i >= 1:
                        wait(a_oat, i)
                        pe.matmul(OB[2][:, 0:D], oat[:], wproj[:], start=True, stop=True).then_inc(a_y, 1)

                mix(0)

                turn_x(2, xn, MB)
                turn_x(3, xn2, OB[0])

                def b_ssq(a):
                    wait(b_sq, a + 1)
                    if a == 8:
                        wait(b_clamped, 1)
                    pe.matmul(OB[1][0:96, :], head_sum[:, a % 8, :], sq[:, a % 2, :], start=(a % 8 == 0),
                              stop=(a % 8 == 7)).then_inc(b_ss, 1)

                def b_fans(kind):
                    wait(b_rns, kind + 1)
                    for b in range(8):
                        a = kind * 8 + b
                        if a >= 2:
                            wait(b_norm, a - 1)
                        pe.matmul([OB[2], OB[0]][a % 2][:], head_fan[:, b, :], rns[:], start=True, stop=True).then_inc(b_fan, 1)

                wait(xl_ready, 2)
                for a in range(16):
                    kind, b = 1 - a // 8, a % 8
                    if a == 8:
                        wait(xl_ready, 3)
                    if a >= 4:
                        wait(b_raw, a - 3)
                    xs = (xh, xl) if kind else (xqh, xql)
                    product(PROJ[a % 4][:], wbh[:, kind, b * P:(b + 1) * P], wbl[:, kind, b * P:(b + 1) * P],
                            xs[0][:], xs[1][:]).then_inc(b_proj, 1)
                    if a % 8 >= 1:
                        b_ssq(a - 1)
                    if a == 7:
                        b_ssq(7)
                        b_fans(0)
                b_ssq(15)
                for a in range(2 * T):
                    t, half = a // 2, a % 2
                    if a >= 4:
                        wait(vb_lo, a - 3)
                    else:
                        wait(b_raw, 13 + a)
                    s = slice(half * 512, half * 512 + 512)
                    product(PROJ[a % 4][:], xh[:, t * P:(t + 1) * P], xl[:, t * P:(t + 1) * P], wbh[:, 2, s], wbl[:, 2, s]
                            ).then_inc(vb_proj, 1)
                b_fans(1)

                def b_nullsc(i):
                    for h in range(H):
                        o = MB[:, h:h + H + 1:H]
                        q = qst[:, h, i * P:(i + 1) * P]
                        pe.matmul(o, q, nkh[:, h:h + H + 1:H], start=True, stop=False, skip_group_check=True)
                        ins = pe.matmul(o, q, nkl[:, h:h + H + 1:H], start=False, stop=True, skip_group_check=True)
                    ins.then_inc(b_null, 1)

                def b_sc(u):
                    i, h = u // H, u % H
                    w = (i + 1) * P
                    if u >= 2:
                        wait(b_biased, u - 1)
                    q = qst[:, h, i * P:(i + 1) * P]
                    pe.matmul(SC[u % 2][:, 0:w], q, kh[:, h, 0:w], start=True, stop=False)
                    pe.matmul(SC[u % 2][:, 0:w], q, kl[:, h, 0:w], start=False, stop=True).then_inc(b_scores, 1)

                def b_turn(u):
                    wait(b_exp, u + 1)
                    if u >= 2:
                        wait(b_ptlo, u - 1)
                    for c in range(u // H + 1):
                        ins = pe.transpose(TR[u % 2][:, c * P:(c + 1) * P], prob[:, u % 2, c * P:(c + 1) * P], ident[:])
                    ins.then_inc(b_turned, 1)

                def b_pvs(u):
                    i, h = u // H, u % H
                    k = h // OBH
                    wait(b_ptlo, u + 1)
                    if h % OBH == 0 and i >= 1:
                        wait(b_normed, 3 * (i - 1) + k + 1)
                    o = OB[k][:, (h % OBH) * OBW:(h % OBH + 1) * OBW]
                    for c in range(i + 1):
                        s = slice(c * P, (c + 1) * P)
                        ins = product(o, pth[:, u % 3, s], ptl[:, u % 3, s], vbh[:, c, h, :], vbl[:, c, h, :],
                                      first=(h % OBH == 0 and c == 0))
                    ins.then_inc(b_pv, 1)

                def b_nullpv(i):
                    wait(b_nlo2, i + 1)
                    for k, (h0, h1) in enumerate(OBANKS):
                        product(OB[k][:, 0:(h1 - h0) * OBW], pnh[:], pnl[:],
                                nvbh[:, h0:h1, :].rearrange("p h d -> p (h d)"),
                                nvbl[:, h0:h1, :].rearrange("p h d -> p (h d)"), first=False).then_inc(b_out, 1)

                wait(vb_lo, 2 * T)
                wait(b_norm, 16)
                wait(*spread(6))
                wait(*spread(7))
                b_nullsc(0)
                b_sc(0)
                b_sc(1)
                for s in range(NUB + 12):
                    i = s // H
                    if s < NUB:
                        b_turn(s)
                    if s % H == 0 and i >= 1:
                        wait(b_nexp, i)
                        wait(b_nbias, min(i + 1, T))
                        pe.transpose(MB[0:NN * H, 0:P], pn[:], ident[:]).then_inc(b_nturned, 1)
                    if s + 2 < NUB:
                        if (s + 2) % H == 0:
                            wait(b_added, (s + 2) // H - 1)
                            b_nullsc((s + 2) // H)
                        b_sc(s + 2)
                    if s % H == 1 and i >= 1:
                        b_nullpv(i - 1)
                    if 1 <= s <= NUB:
                        b_pvs(s - 1)
                    for j in range(2):
                        if s % H == 4 + 2 * j and i >= 1:
                            if j == 0:
                                wait(b_normed, 3 * i)
                            wait(b_obt, 2 * (i - 1) + j)
                            for c in range(4):
                                ins = pe.transpose(MB[:, c * P:(c + 1) * P],
                                                   ob[:, 8 * j + 2 * c:8 * j + 2 * c + 2, :].rearrange("p h d -> p (h d)"), ident[:])
                            ins.then_inc(b_oturned, 1)
                    if s % H == 9 and i >= 1:
                        wait(b_obt, 2 * i)
                        for c in range(8):
                            ins = pe.matmul(MB[:, 0:D], obt[:, c, :], wout[:, c, :], start=(c == 0), stop=(c == 7))
                        ins.then_inc(b_y, 1)

                mix(1)

            @block.scalar
            def _(act):
                wait = waits(act)
                order = Order(act, act_order)

                def root(n):
                    wait(var_ready, n + 1)
                    order.done(act.activation(lnv[:], mv[:, :, 1], ACT.Ln, bias=epsb[:, 0:1]))
                    act.activation(rstd[:], lnv[:], ACT.Exp, scale=-0.5).then_inc(rstd_ready, 1)

                def mix(n):
                    root(1 if n == 0 else 4)
                    wait(turned_x, 2 if n == 0 else 5)
                    copy(xt[:, 1:1 + S], MB[:]).then_inc(f_xt, 1)
                    wait(f_k, n + 1)
                    act.activation(kr[:], SC[0][:], ACT.Relu).then_inc(f_relu, 1)
                    wait(f_r, n + 1)
                    act.activation(ez[:], SC[1][:], ACT.Exp, scale=-1.0).then_inc(f_e, 1)
                    wait(f_e1, n + 1)
                    order.done(act.activation(ez[:], ez1[:], ACT.Ln))
                    act.activation(gate[:], ez[:], ACT.Exp, scale=-1.0).then_inc(f_gate, 1)

                root(0)
                wait(turned_x, 1)
                copy(xh[:], MB[:]).then_inc(xh_ready, 1)
                for a in range(8):
                    wait(a_proj, a + 1)
                    if a >= 2:
                        wait(a_stacked, a - 1)
                    copy(ht[:, a % 2, :], PROJ[a % 4][:]).then_inc(a_hi, 1)
                wait(va_proj, 1)
                copy(vah[:, :, :, 0:DA].rearrange("p t h d -> p (t h) d"),
                     MB[:].rearrange("p (t d) -> p t d", d=DA)).then_inc(va_hi, 1)

                def a_ex(u):
                    i, hp = u // UA, u % UA
                    nk = min(i + 1, 2)
                    wait(a_bias, u + 1)
                    if u >= 2:
                        wait(a_turned, u - 1)
                    for hh in range(2):
                        h = 2 * hp + hh
                        s = slice(hh * nk * P, (hh + 1) * nk * P)
                        ins = act.activation(prob[:, u % 2, s], SC[u % 2][:, s], ACT.Exp, scale=-C_A,
                                             bias=abias[:, i % 2, h:h + 1])
                    ins.then_inc(a_exp, 1)

                def a_pth(u):
                    w = 2 * min(u // UA + 1, 2) * P
                    wait(a_turned, u + 1)
                    if u >= 3:
                        wait(a_pv, u - 2)
                    copy(pth[:, u % 3, 0:w], TR[u % 2][:, 0:w]).then_inc(a_pthi, 1)

                for s in range(NUA + 7):
                    i = s // UA
                    if s < NUA:
                        a_ex(s)
                        if s % UA == UA - 1 and i >= 2:
                            wait(a_gt, i - 1)
                            act.activation(pg[:, 0:2 * (i - 1) * H], gt[:, 0:2 * (i - 1) * H], ACT.Exp).then_inc(a_gexp, 1)
                    if 1 <= s <= NUA:
                        a_pth(s - 1)
                    if s % UA == 0 and i >= 3:
                        ng = 2 * (i - 2)
                        wait(a_gturned, i - 2)
                        copy(pgh[0:ng * H, :], MB[0:ng * H, 0:P]).then_inc(a_ghi, 1)
                    if s % UA == 4 and i >= 1:
                        wait(a_oturned, i)
                        copy(oat[:], OB[2][:, 0:P]).then_inc(a_oat, 1)

                mix(0)

                root(2)
                root(3)
                wait(turned_x, 3)
                copy(xh[:], MB[:]).then_inc(xh_ready, 1)
                wait(turned_x, 4)
                order.done(act.activation(xq[:], OB[0][:], ACT.Identity, scale=cols[:, 0:1], bias=cols[:, 1:2]))
                copy(xqh[:], xq[:]).then_inc(xh_ready, 1)

                def b_root(kind):
                    wait(b_clamped, kind + 1)
                    order.done(act.activation(ssc[:], ssc[:], ACT.Ln, scale=256.0))
                    act.activation(rn[:], ssc[:], ACT.Exp, scale=-0.5, bias=epsb[0:96, 1:2]).then_inc(b_rn, 1)

                def b_his(kind):
                    for b in range(8):
                        a = kind * 8 + b
                        wait(b_norm, a + 1)
                        if a >= 4:
                            wait(*spread(a // 2 - 2))
                        copy(nh[:, (a // 2) % 2, a % 2, :], raw[:, a % 8, :]).then_inc(b_nhi, 1)

                for a in range(16):
                    wait(b_proj, a + 1)
                    if a >= 2:
                        wait(b_ss, a - 1)
                    act.activation(sq[:, a % 2, :], PROJ[a % 4][:], ACT.Square).then_inc(b_sq, 1)
                    if a >= 8:
                        wait(b_nlo, a - 7)
                    copy(raw[:, a % 8, :], PROJ[a % 4][:]).then_inc(b_raw, 1)
                    if a == 7:
                        b_root(0)
                        b_his(0)
                b_root(1)
                for a in range(2 * T):
                    t, half = a // 2, a % 2
                    wait(vb_proj, a + 1)
                    copy(vbh[:, t, 8 * half:8 * half + 8, 0:DB],
                         PROJ[a % 4][:].rearrange("p (h d) -> p h d", d=DB)).then_inc(vb_hi, 1)
                b_his(1)

                def b_ex(u):
                    w = (u // H + 1) * P
                    wait(b_biased, u + 1)
                    if u >= 2:
                        wait(b_turned, u - 1)
                    act.activation(prob[:, u % 2, 0:w], sbias[:, u % 2, 0:w], ACT.Exp, scale=-1.0,
                                   bias=bmin[:, (u // H) % 2, u % H:u % H + 1]).then_inc(b_exp, 1)

                def b_pth(u):
                    w = (u // H + 1) * P
                    wait(b_turned, u + 1)
                    if u >= 3:
                        wait(b_pv, u - 2)
                    copy(pth[:, u % 3, 0:w], TR[u % 2][:, 0:w]).then_inc(b_pthi, 1)

                for s in range(NUB + 8):
                    i = s // H
                    if s < NUB:
                        b_ex(s)
                        if s % H == H - 1:
                            wait(b_nt, i + 1)
                            act.activation(pn[:], nt[:], ACT.Exp).then_inc(b_nexp, 1)
                    if 1 <= s <= NUB:
                        b_pth(s - 1)
                    if s % H == 0 and i >= 1:
                        wait(b_nturned, i)
                        copy(pnh[:], MB[0:NN * H, 0:P]).then_inc(b_nhi2, 1)
                    for j in range(2):
                        if s % H == 5 + 2 * j and i >= 1:
                            wait(b_oturned, 2 * (i - 1) + j + 1)
                            copy(obt[:, 4 * j:4 * j + 4, :].rearrange("p c q -> p (c q)"), MB[:]).then_inc(b_obt, 1)

                mix(1)

            @block.vector
            def _(v):
                wait = waits(v)
                order = Order(v, vec_order)
                done = order.done

                def layer_norm(n, src, dst):
                    for t in range(T):
                        ins = v.bn_stats(stats[:, t, :], src[:, t, :])
                    done(ins)
                    for t in range(T):
                        ins = v.bn_aggr(mv[:, t, :], stats[:, t, :])
                    ins.then_inc(var_ready, 1)
                    wait(var_ready, n + 1)
                    wait(rstd_ready, n + 1)
                    for t in range(T):
                        ins = v.tensor_scalar(dst[:, t, :], src[:, t, :], mv[:, t, 0:1], rstd[:, t:t + 1],
                                              ALU.subtract, ALU.mult)
                    ins.then_inc(ln_ready, 1)
                    wait(ln_ready, n + 1)

                def mix(n, src, dst):
                    layer_norm(1 if n == 0 else 4, src, xn)
                    wait(f_xt, n + 1)
                    for k in (1, 0):
                        done(v.tensor_scalar(prev[:, k, :], xt[:, 0:S], colx[:, 1 + k:2 + k], None, ALU.mult))
                        v.scalar_tensor_tensor(out=mixed[:, k, :], in0=xt[:, 1:1 + S], scalar=cols[:, 4 + k:5 + k],
                                               in1=prev[:, k, :], op0=ALU.mult, op1=ALU.add).then_inc(f_mixed, 1)
                    wait(f_relu, n + 1)
                    v.scalar_tensor_tensor(out=ka[:], in0=SC[0][:], scalar=0.0, in1=kr[:],
                                           op0=ALU.max, op1=ALU.mult).then_inc(f_ka, 1)
                    wait(f_e, n + 1)
                    v.tensor_scalar(ez1[:], ez[:], 1e18, 1.0, ALU.min, ALU.add).then_inc(f_e1, 1)
                    wait(f_gate, n + 1)
                    wait(f_v, n + 1)
                    done(v.tensor_tensor(gv[:], TR[0][:], gate[:], ALU.mult))
                    dv, sv = dst[:].rearrange("p t d -> p (t d)"), src[:].rearrange("p t d -> p (t d)")
                    v.tensor_tensor(dv, gv[:], sv, ALU.add).then_inc(f_done, 1)
                    wait(f_done, n + 1)

                wait(x_first, 16)
                layer_norm(0, x_in, xn)
                wait(xh_ready, 1)
                v.tensor_tensor(xl[:], MB[:], xh[:], ALU.subtract).then_inc(xl_ready, 1)
                wait(xl_ready, 1)
                for k, part in enumerate((xh, xl)):
                    ins = v.tensor_copy(xg[:, k, :].rearrange("p (g h) -> p g h", h=H),
                                        part[:, 0:NG * STRIDE:STRIDE].unsqueeze(2).broadcast_to([P, NG, H]))
                ins.then_inc(xg_ready, 1)
                for a in range(8):
                    kind, grp = 1 - a // 4, a % 4
                    wait(a_hi, a + 1)
                    dst = ka4 if kind else qa4
                    v.scalar_tensor_tensor(out=dst[:, grp, :], in0=ht[:, a % 2, :], scalar=lo_rows[:, kind:kind + 1],
                                           in1=PROJ[a % 4][:], op0=ALU.mult, op1=ALU.add).then_inc(a_stacked, 1)
                wait(va_hi, 1)
                v.tensor_tensor(val[:, :, :, 0:DA].rearrange("p t h d -> p (t h) d"),
                                MB[:].rearrange("p (t d) -> p t d", d=DA),
                                vah[:, :, :, 0:DA].rearrange("p t h d -> p (t h) d"), ALU.subtract).then_inc(va_ready, 1)
                wait(vg_proj, 1)
                one = blk[0:NG * H, :].unsqueeze(2).broadcast_to([NG * H, H, DA])
                done(v.scalar_tensor_tensor(out=vgt[:], in0=OB[0][0:NG * H, 0:D].rearrange("p (h d) -> p h d", d=DA),
                                            scalar=1.0 / WS, in1=one, op0=ALU.mult, op1=ALU.mult))
                done(v.tensor_copy(vgh[:, :, 0:DA], vgt[:]))
                v.tensor_tensor(vgl[:, :, 0:DA], vgt[:], vgh[:, :, 0:DA], ALU.subtract).then_inc(vg_ready, 1)

                def a_min(u):
                    i, hp = u // UA, u % UA
                    nk = min(i + 1, 2)
                    wait(a_scores, u + 1)
                    m, b = amin[:, 2 * hp:2 * hp + 2], abias[:, i % 2, 2 * hp:2 * hp + 2]
                    done(v.tensor_reduce(m, SC[u % 2][:, 0:2 * nk * P].rearrange("p (h k) -> p h k", h=2), AX.X, ALU.min))
                    if i >= 2:
                        ins = v.scalar_tensor_tensor(out=b, in0=m, scalar=C_A, in1=gmin[:, 2 * hp:2 * hp + 2],
                                                     op0=ALU.mult, op1=ALU.min)
                    else:
                        ins = v.tensor_scalar(b, m, C_A, None, ALU.mult)
                    ins.then_inc(a_bias, 1)

                def a_gmin(i):
                    ng = 2 * (i - 1)
                    wait(a_gt, i - 2)
                    wait(a_globals, i - 1)
                    v.tensor_scalar(sgs[:, 0:ng * H], MB[:, 0:ng * H], C_A, None, ALU.mult).then_inc(a_gsaved, 1)
                    wait(a_gsaved, i - 1)
                    done(v.tensor_reduce(gmin[:], sgs[:, 0:ng * H].rearrange("p (g h) -> p h g", h=H), AX.X, ALU.min))

                def a_gts(i):
                    ng = 2 * (i - 1)
                    wait(a_bias, UA * (i + 1))
                    v.tensor_tensor(gt[:, 0:ng * H].rearrange("p (g h) -> p g h", h=H),
                                    abias[:, i % 2, :].unsqueeze(1).broadcast_to([P, ng, H]),
                                    sgs[:, 0:ng * H].rearrange("p (g h) -> p g h", h=H), ALU.subtract).then_inc(a_gt, 1)

                def a_ptl(u):
                    w = 2 * min(u // UA + 1, 2) * P
                    wait(a_pthi, u + 1)
                    v.tensor_tensor(ptl[:, u % 3, 0:w], TR[u % 2][:, 0:w], pth[:, u % 3, 0:w], ALU.subtract).then_inc(a_ptlo, 1)

                def a_norm(i):
                    if i >= 2:
                        wait(a_out, i - 1)
                    else:
                        wait(a_pv, UA * (i + 1))
                    o = OB[i % 2][:, 0:H * (DA + 1)].rearrange("p (h d) -> p h d", d=DA + 1)
                    done(v.reciprocal(rden[:], o[:, :, DA]))
                    if i >= 1:
                        wait(a_oturned, i)
                    v.tensor_tensor(oa[:].rearrange("p (h d) -> p h d", d=DA), o[:, :, 0:DA],
                                    rden[:].unsqueeze(2).broadcast_to([P, H, DA]), ALU.mult).then_inc(a_normed, 1)

                a_min(0)
                for s in range(NUA + 8):
                    i = s // UA
                    if s + 1 < NUA:
                        if (s + 1) % UA == 0 and (s + 1) // UA >= 2:
                            a_gmin((s + 1) // UA)
                        a_min(s + 1)
                        if (s + 1) % UA == UA - 1 and i >= 2:
                            a_gts(i)
                    if 1 <= s <= NUA:
                        a_ptl(s - 1)
                    if s % UA == 0 and i >= 3:
                        ng = 2 * (i - 2)
                        wait(a_ghi, i - 2)
                        v.tensor_tensor(pgl[0:ng * H, :], MB[0:ng * H, 0:P], pgh[0:ng * H, :], ALU.subtract).then_inc(a_glo, 1)
                    if s % UA == 2 and i >= 1:
                        a_norm(i - 1)
                    if s % UA == 6 and i >= 1:
                        wait(a_y, i)
                        v.tensor_tensor(x_a[:, i - 1, :], OB[2][:, 0:D], x_in[:, i - 1, :], ALU.add).then_inc(a_added, 1)

                wait(a_added, T)
                mix(0, x_a, x_f)

                layer_norm(2, x_f, xn)
                layer_norm(3, xn, xn2)
                wait(xh_ready, 2)
                v.tensor_tensor(xl[:], MB[:], xh[:], ALU.subtract).then_inc(xl_ready, 1)
                wait(xh_ready, 3)
                v.tensor_tensor(xql[:], xq[:], xqh[:], ALU.subtract).then_inc(xl_ready, 1)

                def b_clamp(kind):
                    wait(b_ss, 8 * kind + 8)
                    if kind:
                        wait(b_rn, 1)
                    v.tensor_scalar(ssc[:], OB[1][0:96, :], 4.096e-21, None, ALU.max).then_inc(b_clamped, 1)

                def b_rsplit(kind):
                    wait(b_rn, kind + 1)
                    if kind:
                        wait(b_fan, 8)
                    done(v.tensor_copy(rnh[:], rn[:]))
                    v.scalar_tensor_tensor(out=rns[:], in0=rnh[:], scalar=lo_rows[0:96, 2:3], in1=rn[:],
                                           op0=ALU.mult, op1=ALU.add).then_inc(b_rns, 1)

                def b_norms(kind):
                    for b in range(8):
                        a = kind * 8 + b
                        wait(b_fan, a + 1)
                        wait(b_raw, a + 1)
                        scale = cols[:, 3:4] if kind == 0 else colx[:, 0:1]
                        v.scalar_tensor_tensor(out=raw[:, b, :], in0=[OB[2], OB[0]][a % 2][:], scalar=scale, in1=raw[:, b, :],
                                               op0=ALU.mult, op1=ALU.mult).then_inc(b_norm, 1)

                b_clamp(0)
                b_rsplit(0)
                b_norms(0)
                b_clamp(1)
                b_rsplit(1)
                for a in range(2 * T):
                    t, half = a // 2, a % 2
                    wait(vb_hi, a + 1)
                    hs = slice(8 * half, 8 * half + 8)
                    v.tensor_tensor(vbl[:, t, hs, 0:DB], PROJ[a % 4][:].rearrange("p (h d) -> p h d", d=DB),
                                    vbh[:, t, hs, 0:DB], ALU.subtract).then_inc(vb_lo, 1)
                b_norms(1)

                def b_nullbias(i):
                    wait(b_null, i + 1)
                    done(v.tensor_tensor(snb[:, i % 2].rearrange("p n h -> p (n h)"), MB[:, 0:NN * H],
                                         alibi_null[:, i].rearrange("p n h -> p (n h)"), ALU.add))
                    ins = v.tensor_tensor(nmin[:], snb[:, i % 2, 0, :], snb[:, i % 2, 1, :], ALU.min)
                    ins.then_inc(b_nbias, 1)
                    wait(b_nbias, i + 1)

                def b_bias(u):
                    i, h = u // H, u % H
                    w = (i + 1) * P
                    wait(b_scores, u + 1)
                    if u >= 2:
                        wait(b_exp, u - 1)
                    v.tensor_tensor_reduce(sbias[:, u % 2, 0:w], SC[u % 2][:, 0:w], alibi[:, h, S - w:S],
                                           1.0, nmin[:, h:h + 1], ALU.add, ALU.min,
                                           bmin[:, i % 2, h:h + 1]).then_inc(b_biased, 1)

                def b_nulls(i):
                    wait(b_biased, H * (i + 1))
                    v.tensor_tensor(nt[:].rearrange("p (n h) -> p n h", h=H),
                                    bmin[:, i % 2, :].unsqueeze(1).broadcast_to([P, NN, H]),
                                    snb[:, i % 2], ALU.subtract).then_inc(b_nt, 1)

                def b_ptl(u):
                    w = (u // H + 1) * P
                    wait(b_pthi, u + 1)
                    v.tensor_tensor(ptl[:, u % 3, 0:w], TR[u % 2][:, 0:w], pth[:, u % 3, 0:w], ALU.subtract).then_inc(b_ptlo, 1)

                def b_normal(i):
                    for k, (h0, h1) in enumerate(OBANKS):
                        wait(b_out, 3 * i + k + 1)
                        if i >= 1 and k == 0:
                            wait(b_oturned, 2 * i)
                        o = OB[k][:, 0:(h1 - h0) * OBW].rearrange("p (h d) -> p h d", d=OBW)
                        done(v.reciprocal(rden[:, h0:h1], o[:, :, DB]))
                        v.tensor_tensor(ob[:, h0:h1, :], o[:, :, 0:DB],
                                        rden[:, h0:h1].unsqueeze(2).broadcast_to([P, h1 - h0, DB]), ALU.mult).then_inc(b_normed, 1)

                b_nullbias(0)
                b_bias(0)
                for s in range(NUB + 12):
                    i = s // H
                    if s + 1 < NUB:
                        if (s + 1) % H == 0:
                            b_nullbias((s + 1) // H)
                        b_bias(s + 1)
                        if (s + 1) % H == H - 1:
                            b_nulls(i)
                    if 1 <= s <= NUB:
                        b_ptl(s - 1)
                    if s % H == 0 and i >= 1:
                        wait(b_nhi2, i)
                        v.tensor_tensor(pnl[:], MB[0:NN * H, 0:P], pnh[:], ALU.subtract).then_inc(b_nlo2, 1)
                    if s % H == 1 and i >= 1:
                        b_normal(i - 1)
                    if s % H == 11 and i >= 1:
                        wait(b_y, i)
                        v.tensor_tensor(x_b[:, i - 1, :], MB[:, 0:D], x_f[:, i - 1, :], ALU.add).then_inc(b_added, 1)
                wait(b_added, T)
                mix(1, x_b, x_out)

          nc.all_engine_barrier(sems_to_clear=range(x_loaded.num, last_sem.num + 1))


WLOADS = 17

_INS = ["L0_attn_a_x", "L0_attn_a_Wqkv", "L0_attn_a_Wproj", "L0_attn_b_norm_g", "L0_attn_b_norm_b",
        "L0_attn_b_Wq", "L0_attn_b_Wkv", "L0_attn_b_q_scale", "L0_attn_b_k_scale", "L0_attn_b_null_kv",
        "L0_attn_b_Wout", "L0_ffn_W_r", "L0_ffn_W_k", "L0_ffn_W_v", "L0_ffn_mu_r", "L0_ffn_mu_k"]


def kernel(**inputs):
    import numpy as _np
    import concourse.bacc as _bacc
    from concourse import mybir as _mybir
    from concourse.bass_utils import run_bass_kernel_spmd as _run

    nc = _bacc.Bacc("TRN2", target_bir_lowering=False, num_devices=1)
    arrays, args = {}, []
    for name in _INS:
        a = _np.ascontiguousarray(inputs[name])
        arrays[f"in_{name}"] = a
        args.append(nc.dram_tensor(f"in_{name}", a.shape, _mybir.dt.from_np(a.dtype), kind="ExternalInput").ap())
    shape = inputs["L0_attn_a_x"].shape
    args.append(nc.dram_tensor("out_0", shape, _mybir.dt.float32, kind="ExternalOutput").ap())
    program(nc, *args)
    r = _run(nc, [arrays], core_ids=[0])
    return r.results[0]["out_0"]
```

```python
from contextlib import ExitStack
import math

import concourse.bass as bass
from concourse import mybir

F32 = mybir.dt.float32
F16 = mybir.dt.float16
BF16 = mybir.dt.bfloat16
I32 = mybir.dt.int32
ALU = mybir.AluOpType
ACT = mybir.ActivationFunctionType
AX = mybir.AxisListType

P = 128
D = 128
H = 16
DA = D // H
DB = 64
NN = 2
STRIDE = 64
EPS = 1e-5
WS = 64.0
MASKED = 1e30
REPS = 4
GR = 4
UA = H // 2
OBH = 8


def program(nc, x, a_wqkv, a_wproj, b_g, b_b, b_wq, b_wkv, b_qs, b_ks, b_nullkv, b_wout,
            f_wr, f_wk, f_wv, f_mur, f_muk, out):
    NS, S, _ = x.shape
    T = S // P
    NG = S // STRIDE // 2
    C_A = 1.0 / (WS * WS * math.sqrt(DA))
    start = 2.0 ** (-2.0 ** (-(math.log2(H) - 3)))
    slopes = [start * start ** h for h in range(H)]
    NUA, NUB = T * UA, T * H

    ctx = ExitStack()
    with ctx:
        def sb(name, shape, dt=F32):
            return ctx.enter_context(nc.sbuf_tensor(name, shape, dt))

        def sem(name):
            return ctx.enter_context(nc.semaphore(name))

        def bank(name, dt=F32):
            return ctx.enter_context(nc.psum_tensor(name, [P, 512], dt))
        SA, TA, OA = bank("scores_a"), bank("turned_a"), bank("out_a")
        SC, TR, OB = bank("scores_b"), [bank("turned_b0"), bank("turned_b1")], [bank("out_b0"), bank("out_b1")]
        PROJ_A = [TA, OA]
        PROJ_B = [SC, TR[0], TR[1]]

        scratch = sb("scratch", [P, 8 * S])
        split_space = sb("split_space", [P, 4 * S])
        bias_space = sb("bias_space", [P, 2 * S])
        norm_space = sb("norm_space", [P, 2 * S])
        stack_space = sb("stack_space", [P, H * S], F16)
        front_space = sb("front_space", [P, 7 * S + 8])

        def half(space, a, b, **dims):
            return space[:, a:b].bitcast(F16).rearrange("p (n s) -> p n s", s=S)

        wst = scratch[:, 0:2048]
        wa4 = scratch[:, 2048:3072].rearrange("p (k h r d) -> p k h r d", k=2, h=H, r=REPS)
        wa_sb = scratch[:, 3072:3072 + 3 * D]
        wfn = scratch[:, 3456:3456 + 3 * D].rearrange("p (k d) -> p k d", k=3)
        dist_i = bias_space[:, 0:S].bitcast(I32)
        dist = bias_space[:, S:2 * S]
        ka4 = half(front_space, 0, 2 * S)
        qa4 = half(front_space, 2 * S, 4 * S)
        ht = half(front_space, 4 * S, 5 * S)
        prob_a = front_space[:, 4 * S:5 * S]
        pth_a = half(front_space, 5 * S, 6 * S)
        ptl_a = half(front_space, 6 * S, 7 * S)
        raw = scratch[:].rearrange("p (n s) -> p n s", s=S)
        nh = half(split_space, 0, 2 * S).rearrange("p (a b) s -> p a b s", a=2)
        nl = half(split_space, 2 * S, 4 * S).rearrange("p (a b) s -> p a b s", a=2)
        sq = bias_space[:].rearrange("p (n s) -> p n s", s=S)
        xq = norm_space[:, 0:S]
        rn = norm_space[0:96, 0:S]
        rnh, rns = [half(norm_space, S, 2 * S)[0:96, j, :] for j in range(2)]
        qst = stack_space[:].rearrange("p (h s) -> p h s", h=H)
        sbias = scratch[:, 0:2 * S].rearrange("p (n s) -> p n s", s=S)
        prob = scratch[:, 2 * S:4 * S].rearrange("p (n s) -> p n s", s=S)
        pth = half(scratch, 4 * S, 11 * S // 2)
        ptl = half(scratch, 11 * S // 2, 7 * S)
        ob = split_space[:, 0:H * DB].rearrange("p (h d) -> p h d", h=H)
        obt = split_space[:, H * DB:2 * H * DB].rearrange("p (c q) -> p c q", q=P)

        ident = sb("ident", [P, P])
        identb = sb("identb", [P, P], BF16)
        mask_a = sb("mask_a", [P, 2, 2 * P], BF16)
        lo_rows = sb("lo_rows", [P, 3])
        rowi = sb("rowi", [P, 4], I32)
        head_rows = sb("head_rows", [P, GR])
        alibi = sb("alibi", [P, H, S])
        null_i = sb("null_i", [P, T, NN], I32)
        null_f = sb("null_f", [P, T, NN])
        alibi_null = sb("alibi_null", [P, T, NN, H])
        blk = sb("blk", [P, H])
        head_sum = sb("head_sum", [P, 96 + H - 2])
        head_fan = sb("head_fan", [96, 8, P], F16)
        fan_row = sb("fan_row", [P, 2, H])
        epsb = sb("epsb", [P, 4])
        wa4h = sb("wa4h", [P, 2, GR, P], F16)
        wa4l = sb("wa4l", [P, 2, GR, P], F16)
        wavh = sb("wavh", [P, D], F16)
        wavl = sb("wavl", [P, D], F16)
        wproj = sb("wproj", [P, D])
        wbh = sb("wbh", [P, 3, H * DB], F16)
        wbl = sb("wbl", [P, 3, H * DB], F16)
        wout = sb("wout", [P, 8, D])
        wft = sb("wft", [P, 3, D])
        cols = sb("cols", [P, 6])
        colx = sb("colx", [P, 3])
        nk_sb = sb("nk_sb", [NN * H, 2, DB])
        nkd = sb("nkd", [NN * H, 2 * DB])
        nks = sb("nks", [NN * H, 4])
        nkf = sb("nkf", [P, NN * H])
        nkh = sb("nkh", [P, NN * H], F16)
        nkl = sb("nkl", [P, NN * H], F16)
        nvh = sb("nvh", [NN * H, DB], F16)
        nvl = sb("nvl", [NN * H, DB], F16)
        nvbh = sb("nvbh", [NN * H, H, DB], F16)
        nvbl = sb("nvbl", [NN * H, H, DB], F16)

        x_in = sb("x_in", [P, T, D])
        x_a = sb("x_a", [P, T, D])
        x_f = sb("x_f", [P, T, D])
        x_b = sb("x_b", [P, T, D])
        xh_b, xl_b = sb("xh_b", [P, S], F16), sb("xl_b", [P, S], F16)
        xg = sb("xg", [P, 2, NG * H], F16)
        qm = sb("qm", [P, 2, H, P], F16)
        vah = sb("vah", [P, T, H, DA + 1], F16)
        val = sb("val", [P, T, H, DA + 1], F16)
        vgt = sb("vgt", [NG * H, H, DA])
        vgh = sb("vgh", [NG * H, H, DA + 1], F16)
        vgl = sb("vgl", [NG * H, H, DA + 1], F16)
        sgs = sb("sgs", [P, NG * H])
        gmin = sb("gmin", [P, H])
        amin = sb("amin", [P, H])
        abias = sb("abias", [P, 2, H])
        gt = sb("gt", [P, NG * H])
        pg = sb("pg", [P, NG * H])
        pgh = sb("pgh", [NG * H, P], F16)
        pgl = sb("pgl", [NG * H, P], F16)
        oa = sb("oa", [P, D])
        oat = sb("oat", [P, D])
        rden_a = sb("rden_a", [P, H])
        kh = sb("kh", [P, H, S], F16)
        kl = sb("kl", [P, H, S], F16)
        vbh = sb("vbh", [P, T, H, DB], F16)
        vbl = sb("vbl", [P, T, H, DB], F16)
        snb = sb("snb", [P, 2, NN, H])
        nmin = sb("nmin", [P, H])
        bmin = sb("bmin", [P, 2, H])
        bden = sb("bden", [P, 2, H])
        den = sb("den", [P, H])
        rden_b = sb("rden_b", [P, H])
        nt = sb("nt", [P, NN * H])
        pn = sb("pn", [P, NN * H])
        pnh = sb("pnh", [NN * H, P], F16)
        pnl = sb("pnl", [NN * H, P], F16)
        xn2 = x_b

        w_loaded = sem("w_loaded")
        w_staged = sem("w_staged")
        pool_setup = sem("pool_setup")
        vec_setup = sem("vec_setup")
        act_setup = sem("act_setup")
        ident_ready = sem("ident_ready")
        iotas_ready = sem("iotas_ready")
        pool_ready = sem("pool_ready")
        alibi_ready = sem("alibi_ready")
        null_ss = sem("null_ss")
        wq_split = sem("wq_split")
        nulls_scaled = sem("nulls_scaled")
        vec_ready = sem("vec_ready")
        wav_hi = sem("wav_hi")
        wq_hi = sem("wq_hi")
        null_root = sem("null_root")
        nv_hi = sem("nv_hi")
        act_ready = sem("act_ready")
        mix_turned = sem("mix_turned")
        nulls_turned = sem("nulls_turned")
        x_first = sem("x_first")
        x_loaded = sem("x_loaded")
        x_stored = sem("x_stored")
        vec_order = sem("vec_order")
        act_order = sem("act_order")
        xh_ready = sem("xh_ready")
        xl_ready = sem("xl_ready")
        xg_ready = sem("xg_ready")
        a_proj = sem("a_proj")
        a_hi = sem("a_hi")
        a_stacked = sem("a_stacked")
        a_masked = sem("a_masked")
        va_proj = sem("va_proj")
        va_hi = sem("va_hi")
        va_ready = sem("va_ready")
        vg_proj = sem("vg_proj")
        vg_ready = sem("vg_ready")
        a_filled = sem("a_filled")
        a_read = sem("a_read")
        a_bias = sem("a_bias")
        a_exp = sem("a_exp")
        a_turned = sem("a_turned")
        a_pthi = sem("a_pthi")
        a_ptlo = sem("a_ptlo")
        a_pv = sem("a_pv")
        a_gt = sem("a_gt")
        a_gexp = sem("a_gexp")
        a_ghi = sem("a_ghi")
        a_out = sem("a_out")
        a_normed = sem("a_normed")
        a_added = sem("a_added")
        b_xh = sem("b_xh")
        b_xl = sem("b_xl")
        xq_hi = sem("xq_hi")
        xq_lo = sem("xq_lo")
        b_proj = sem("b_proj")
        b_raw = sem("b_raw")
        b_sq = sem("b_sq")
        b_ss = sem("b_ss")
        b_clamped = sem("b_clamped")
        b_rn = sem("b_rn")
        b_rns = sem("b_rns")
        b_fan = sem("b_fan")
        b_norm = sem("b_norm")
        b_nhi = sem("b_nhi")
        b_nlo = sem("b_nlo")
        vb_proj = sem("vb_proj")
        vb_hi = sem("vb_hi")
        vb_lo = sem("vb_lo")
        b_filled = sem("b_filled")
        b_read = sem("b_read")
        b_biased = sem("b_biased")
        b_exp = sem("b_exp")
        b_turned = sem("b_turned")
        b_pthi = sem("b_pthi")
        b_ptlo = sem("b_ptlo")
        b_pv = sem("b_pv")
        b_nt = sem("b_nt")
        b_nexp = sem("b_nexp")
        b_nhi2 = sem("b_nhi2")
        b_out = sem("b_out")
        b_normed = sem("b_normed")
        b_added = sem("b_added")
        b_spread = [sem(f"b_spread{j}") for j in range(2)]

        class Stream:
            def __init__(self, name, space, banks):
                def own(part):
                    return sem(f"{name}_{part}")
                self.stats = sb(f"{name}_stats", [P, T, 6])
                self.mv = sb(f"{name}_mv", [P, T, 2])
                self.lnv = sb(f"{name}_lnv", [P, T])
                self.rstd = sb(f"{name}_rstd", [P, T])
                self.xn = sb(f"{name}_xn", [P, T, D])
                self.mixed = space[:, 0:2 * S].rearrange("p (k s) -> p k s", k=2)
                self.prev, self.kr, self.ka, self.ez = [space[:, j * S:(j + 1) * S] for j in range(2, 6)]
                self.xt = space[:, 6 * S:7 * S + 1]
                self.gate, self.gv = self.kr, self.prev
                self.banks = banks
                self.var_ready = own("var_ready")
                self.rstd_ready = own("rstd_ready")
                self.ln_ready = own("ln_ready")
                self.turned = own("turned")
                self.f_xt = own("f_xt")
                self.f_mixed = own("f_mixed")
                self.f_k = own("f_k")
                self.f_r = own("f_r")
                self.f_relu = own("f_relu")
                self.f_e = own("f_e")
                self.f_e1 = own("f_e1")
                self.f_gate = own("f_gate")
                self.f_ka = own("f_ka")
                self.f_v = own("f_v")
                self.f_done = own("f_done")

        FR = Stream("front", front_space, [SA, TA, OA])
        BK = Stream("back", scratch, [SC, TR[0], TR[1]])
        last_sem = BK.f_done
        xh_a, xl_a = [FR.xn[:].rearrange("p t d -> p (t d)").bitcast(F16)[:, j * S:(j + 1) * S] for j in range(2)]
        xqh, xql = [BK.xn[:].rearrange("p t d -> p (t d)").bitcast(F16)[:, j * S:(j + 1) * S] for j in range(2)]

        def slots_a():
            slots = []
            for i in range(T):
                units = [("unit", UA * i + k) for k in range(UA)]
                if i >= 2:
                    slots.append(("glob", i))
                if i >= 3:
                    slots.insert(len(slots) - 1, ("turn_glob", i - 1))
                if i >= 1:
                    units = units[0:3] + [("turn_out", i - 1)] + units[3:4] + [("y", i - 1)] + units[4:]
                slots += units
            return slots + [("turn_glob", T - 1), None, None, ("turn_out", T - 1), ("y", T - 1)]

        def slots_b():
            slots = []
            for i in range(T):
                u = [("unit", H * i + k) for k in range(H)]
                slots.append(("null", i))
                if i >= 1:
                    u = (u[0:1] + [("turn_null", i - 1)] + u[1:4] + [("turn_out", (i - 1, 0))] + u[4:5] +
                         [("turn_out", (i - 1, 1))] + u[5:6] + [("y", i - 1)] + u[6:])
                slots += u
            return slots + [None, None, ("turn_null", T - 1), None, None, None,
                            ("turn_out", (T - 1, 0)), ("turn_out", (T - 1, 1)), ("y", T - 1)]

        SLOTS_A, SLOTS_B = slots_a(), slots_b()

        def filled(slots, what):
            return sum(s is not None for s in slots[:slots.index(what) + 1])

        def misc(slots, what):
            return sum(s is not None and s[0] not in ("unit", "y") for s in slots[:slots.index(what) + 1])

        def read_before(slots, n, unit_read, y_read, misc_read):
            for kind, arg in reversed([s for s in slots[:n] if s is not None]):
                if kind == "unit":
                    return unit_read, arg + 1
                if kind == "y":
                    return y_read, arg + 1
                return misc_read, misc(slots, (kind, arg))
            return misc_read, 0

        def at(slots, n):
            return slots[n] if 0 <= n < len(slots) and slots[n] is not None else (None, 0)

        def unit(slots, n):
            kind, u = at(slots, n)
            return u if kind == "unit" else None

        A0 = 17
        AM = A0 + 3 * len(SLOTS_A)
        NF = AM + 11
        K0, V0, FK0, Q0 = 6, 14, 18, 24
        GAP = 6
        FQ0 = Q0 + 11
        B0 = FQ0 + 5 + GAP
        BM = B0 + len(SLOTS_B)
        NB = BM + 11

        def weight_front(n):
            if n < 6:
                return 1.0
            if n < A0:
                return 1.2
            if n >= AM:
                return 1.4
            kind, arg = at(SLOTS_A, (n - A0) // 3)
            if kind == "unit":
                return 0.7 if arg < UA else 1.0
            return 0.3

        def weight_back(n):
            if n < K0:
                return 1.1
            if n < V0:
                return 1.5
            if n < Q0:
                return 1.5
            if n < Q0 + 8:
                return 1.9
            if n < FQ0:
                return 1.2
            if n < B0:
                return 2.0
            if n >= BM:
                return 1.5
            kind, arg = at(SLOTS_B, n - B0)
            if kind == "unit":
                return (0.85, 0.95, 1.2, 1.45)[arg // H]
            return {"null": 1.5, "turn_null": 0.8, "turn_out": 1.2, "y": 2.5}.get(kind, 1.2)

        def placed(count, weight):
            total, so_far, places = sum(weight(n) for n in range(count)), 0, []
            for n in range(count):
                places.append((so_far + weight(n) / 2) / total)
                so_far += weight(n)
            return places

        MERGED = sorted([(p, 1, n) for n, p in enumerate(placed(NF, weight_front))] +
                        [(p, 0, n) for n, p in enumerate(placed(NB, weight_back))])
        FRONT_ONLY = [(1, n) for n in range(NF)]
        BACK_ONLY = [(0, n) for n in range(NB)]
        BOTH = [(f, n) for _, f, n in MERGED]

        def spread(pair):
            m = pair // 2 + 1
            return b_spread[pair % 2], 16 * (8 * min(m, 2) + 4 * max(m - 2, 0))

        def copy(o, i, **kw):
            return nc.scalar.activation(o, i, ACT.Copy, **kw)

        def product(o, ah, al, bh, bl, first=True, last=True):
            nc.tensor.matmul(o, ah, bh, start=first, stop=False, skip_group_check=True)
            nc.tensor.matmul(o, al, bh, start=False, stop=False, skip_group_check=True)
            return nc.tensor.matmul(o, ah, bl, start=False, stop=last, skip_group_check=True)

        class Order:
            def __init__(self, eng, s):
                self.eng, self.s, self.n = eng, s, 0

            def done(self, ins):
                ins.then_inc(self.s, 1)
                self.n += 1
                self.eng.wait_ge(self.s, self.n)

        with nc.Block() as block:
            @block.sync
            def _(sp):
                def load(dst, src):
                    sp.dma_start(dst, src).then_inc(w_loaded, 16)
                sp.dma_start(x_in[:], x[0].rearrange("(t p) d -> p t d", p=P)).then_inc(x_first, 16)
                load(wa_sb[:], a_wqkv)
                load(wproj[:], a_wproj)
                load(wst[:, 0:1024], b_wq)
                load(wout[:], b_wout.rearrange("(c p) n -> p c n", p=P))
                load(wfn[:, 0, :], f_wr)
                load(wfn[:, 1, :], f_wk)
                load(wfn[:, 2, :], f_wv)
                for c, v in ((0, b_g), (1, b_b), (4, f_mur), (5, f_muk)):
                    load(cols[:, c:c + 1], v.rearrange("(p o) -> p o", o=1))
                for c, v in ((2, b_qs), (3, b_ks)):
                    for half in range(2):
                        load(cols[half * DB:half * DB + DB, c:c + 1], v.rearrange("(p o) -> p o", o=1))
                null = b_nullkv.rearrange("h (n c) d -> n h c d", c=2)
                for n in range(NN):
                    load(nk_sb[n * H:(n + 1) * H, :, :], null[n])
                sp.wait_ge(wq_split, 1)
                sp.dma_start(wst[:], b_wkv).then_inc(w_staged, 16)

            @block.gpsimd
            def _(pool):
                g = nc.gpsimd
                n = [0]

                def done(ins):
                    ins.then_inc(pool_setup, 1)
                    n[0] += 1
                    pool.wait_ge(pool_setup, n[0])

                done(g.memset(ident[:], 0.0))
                g.affine_select(out=ident[:], in_=ident[:], compare_op=ALU.not_equal, fill=1.0,
                                base=0, pattern=[[-1, P]], channel_multiplier=1).then_inc(ident_ready, 1)
                done(g.memset(mask_a[:], 0.0))
                for hh in range(2):
                    done(g.affine_select(out=mask_a[:, hh, 0:P], in_=mask_a[:, hh, 0:P], compare_op=ALU.is_gt,
                                         fill=MASKED, base=0, pattern=[[1, P]], channel_multiplier=-1))
                    done(g.affine_select(out=mask_a[:, hh, P:2 * P], in_=mask_a[:, hh, P:2 * P], compare_op=ALU.is_ge,
                                         fill=MASKED, base=0, pattern=[[-1, P]], channel_multiplier=1))
                    for k in range(0, P, STRIDE):
                        done(g.memset(mask_a[:, hh, k:k + 1], 0.0))
                done(g.iota(dist_i[:], pattern=[[-1, S]], base=S - P, channel_multiplier=1))
                done(g.iota(null_i[:], pattern=[[P, T], [-1, NN]], base=NN, channel_multiplier=1))
                g.iota(rowi[:], pattern=[[0, 4]], base=0, channel_multiplier=1).then_inc(iotas_ready, 1)
                done(g.memset(head_sum[:], 0.0))
                for j in range(2):
                    done(g.memset(head_sum[j * DB:j * DB + DB, H - 2 + j:96 + H - 2:H], 1.0))
                pool.wait_ge(alibi_ready, 1)
                g.affine_select(out=alibi[:, :, S - P:S], in_=alibi[:, :, S - P:S], compare_op=ALU.is_ge, fill=MASKED,
                                base=0, pattern=[[0, H], [-1, P]], channel_multiplier=1).then_inc(pool_ready, 1)

            @block.tensor
            def _(pe):
                pe.wait_ge(ident_ready, 1)
                pe.wait_ge(w_loaded, 16 * WLOADS)
                for k in range(3):
                    ins = pe.transpose(SA[:, k * D:(k + 1) * D], wfn[:, k, :], ident[:])
                ins.then_inc(mix_turned, 1)
                pe.wait_ge(nulls_scaled, 1)
                pe.transpose(TA[:, 0:NN * H], nkd[:], ident[0:NN * H, 0:NN * H]).then_inc(nulls_turned, 1)
                pe.wait_ge(vec_ready, 1)
                pe.wait_ge(act_ready, 1)
                pe.wait_ge(pool_ready, 1)

            @block.scalar
            def _(act):
                n = [0]

                def done(ins):
                    ins.then_inc(act_setup, 1)
                    n[0] += 1
                    act.wait_ge(act_setup, n[0])
                act.preload_act_table_set("natural_log_exp_and_others")
                act.wait_ge(w_loaded, 16 * WLOADS)
                copy(wavh[:], wa_sb[:, 2 * D:3 * D], scale=WS).then_inc(wav_hi, 1)
                copy(wbh[:, 0, :], wst[:, 0:1024], scale=WS).then_inc(wq_hi, 1)
                act.wait_ge(null_ss, 1)
                done(act.activation(nks[:, 2:3], nks[:, 1:2], ACT.Ln, scale=2.0 ** 20))
                act.activation(nks[:, 3:4], nks[:, 2:3], ACT.Exp, scale=-0.5, bias=epsb[0:NN * H, 2:3]).then_inc(null_root, 1)
                copy(nvh[:], nk_sb[:, 1, :], scale=WS).then_inc(nv_hi, 1)
                act.wait_ge(w_staged, 16)
                copy(wbh[:, 1:3, :].rearrange("p k n -> p (k n)"), wst[:], scale=WS).then_inc(act_ready, 1)
                act.wait_ge(vec_ready, 1)

            @block.vector
            def _(v):
                n = [0]

                def done(ins):
                    ins.then_inc(vec_setup, 1)
                    n[0] += 1
                    v.wait_ge(vec_setup, n[0])

                v.wait_ge(iotas_ready, 1)
                done(v.tensor_copy(dist[:], dist_i[:]))
                for h in range(H):
                    ins = v.tensor_scalar(alibi[:, h, :], dist[:], slopes[h], None, ALU.mult)
                ins.then_inc(alibi_ready, 1)
                done(v.tensor_copy(null_f[:], null_i[:]))
                for h in range(H):
                    ins = v.tensor_scalar(alibi_null[:, :, :, h], null_f[:], slopes[h], None, ALU.mult)
                done(ins)
                for c, sh in ((0, 3), (1, 4), (2, 4), (3, 5)):
                    done(v.tensor_scalar(rowi[:, c:c + 1], rowi[:, c:c + 1], sh, None, ALU.logical_shift_right))
                done(v.tensor_scalar(rowi[:, 0:2], rowi[:, 0:2], 1, None, ALU.bitwise_and))
                done(v.tensor_copy(lo_rows[:], rowi[:, 0:3]))
                done(v.tensor_copy(head_rows[:, GR - 1:GR], rowi[:, 3:4]))
                for r in range(GR):
                    done(v.tensor_scalar(head_rows[:, r:r + 1], head_rows[:, GR - 1:GR], float(r), None, ALU.is_equal))
                done(v.tensor_scalar(lo_rows[:, 2:3], lo_rows[:, 2:3], 1.0, None, ALU.is_equal))
                done(v.tensor_scalar(lo_rows[:], lo_rows[:], -1.0, None, ALU.mult))
                v.memset(epsb[:, 0:1], EPS)
                v.memset(epsb[:, 1:2], math.log(1024.0) + 0.5 * math.log(256.0))
                done(v.memset(epsb[:, 2:4], 0.5 * math.log(2.0 ** 20)))
                v.wait_ge(ident_ready, 1)
                done(v.tensor_copy(identb[:], ident[:]))
                done(v.tensor_scalar(blk[:], ident[:, 0:H], WS, None, ALU.mult))
                for r in range(1, 8):
                    done(v.scalar_tensor_tensor(out=blk[:], in0=ident[:, r * H:(r + 1) * H], scalar=WS, in1=blk[:],
                                                op0=ALU.mult, op1=ALU.add))
                done(v.tensor_scalar(fan_row[:, 0, :], blk[:], 1.0 / WS / 1024.0, None, ALU.mult))
                done(v.memset(head_fan[:], 0.0))
                for b in range(8):
                    done(v.tensor_copy(head_fan[0:32, b, :].rearrange("p (j d) -> p j d", j=2),
                                       fan_row[0:32, 0, 2 * b:2 * b + 2].unsqueeze(2).broadcast_to([32, 2, DB])))
                for tile, c in ((vah, WS), (val, 0.0)):
                    v.memset(tile[:, :, :, DA:DA + 1], c)
                v.memset(vgl[:, :, DA:DA + 1], 0.0)
                done(v.tensor_copy(vgh[:, :, DA:DA + 1], blk[0:NG * H, :].unsqueeze(2)))
                v.wait_ge(w_loaded, 16 * WLOADS)
                done(v.tensor_tensor(nkd[:, 0:DB], nk_sb[:, 0, :], nk_sb[:, 0, :], ALU.mult))
                done(v.tensor_reduce(nks[:, 0:1], nkd[:, 0:DB], AX.X, ALU.add))
                v.tensor_scalar(nks[:, 1:2], nks[:, 0:1], 1e-24, None, ALU.max).then_inc(null_ss, 1)
                for kind, sc in ((0, -WS), (1, WS)):
                    w = wa_sb[:, kind * D:(kind + 1) * D].rearrange("p (h d) -> p h d", d=DA)
                    for r in range(REPS):
                        ins = v.tensor_scalar(wa4[:, kind, :, r, :], w, sc, None, ALU.mult)
                done(ins)
                wv = wa4[:].rearrange("p k h r d -> p (k h r d)")
                whv = wa4h[:].rearrange("p k g c -> p (k g c)")
                wlv = wa4l[:].rearrange("p k g c -> p (k g c)")
                done(v.tensor_copy(whv, wv))
                done(v.tensor_tensor(wlv, wv, whv, ALU.subtract))
                done(v.tensor_scalar(wout[:], wout[:], 1.0 / WS, None, ALU.mult))
                done(v.tensor_scalar(colx[:, 0:1], cols[:, 2:3], -8.0, None, ALU.mult))
                done(v.tensor_scalar(colx[:, 1:3], cols[:, 4:6], -1.0, 1.0, ALU.mult, ALU.add))
                v.wait_ge(wav_hi, 1)
                done(v.scalar_tensor_tensor(out=wavl[:], in0=wa_sb[:, 2 * D:3 * D], scalar=WS, in1=wavh[:],
                                            op0=ALU.mult, op1=ALU.subtract))
                v.wait_ge(wq_hi, 1)
                v.scalar_tensor_tensor(out=wbl[:, 0, :], in0=wst[:, 0:1024], scalar=WS, in1=wbh[:, 0, :],
                                       op0=ALU.mult, op1=ALU.subtract).then_inc(wq_split, 1)
                v.wait_ge(null_root, 1)
                for half in range(2):
                    ins = v.tensor_scalar(nkd[:, half * DB:(half + 1) * DB], nk_sb[:, 0, :], nks[:, 3:4], None, ALU.mult)
                ins.then_inc(nulls_scaled, 1)
                v.wait_ge(nv_hi, 1)
                done(v.scalar_tensor_tensor(out=nvl[:], in0=nk_sb[:, 1, :], scalar=WS, in1=nvh[:],
                                            op0=ALU.mult, op1=ALU.subtract))
                b1 = fan_row[0:NN * H, 1, :]
                done(v.tensor_scalar(b1, blk[0:NN * H, :], 1.0 / WS, None, ALU.mult))
                bb = b1.unsqueeze(2).broadcast_to([NN * H, H, DB])
                done(v.tensor_tensor(nvbh[:, :, 0:DB], nvh[:].unsqueeze(1).broadcast_to([NN * H, H, DB]), bb, ALU.mult))
                done(v.tensor_tensor(nvbl[:, :, 0:DB], nvl[:].unsqueeze(1).broadcast_to([NN * H, H, DB]), bb, ALU.mult))
                v.wait_ge(mix_turned, 1)
                done(v.tensor_copy(wft[:].rearrange("p k d -> p (k d)"), SA[:, 0:3 * D]))
                v.wait_ge(nulls_turned, 1)
                done(v.tensor_scalar(nkf[:], TA[:, 0:NN * H], cols[:, 3:4], None, ALU.mult))
                done(v.tensor_copy(nkh[:], nkf[:]))
                done(v.tensor_tensor(nkl[:], nkf[:], nkh[:], ALU.subtract))
                v.wait_ge(act_ready, 1)
                v.scalar_tensor_tensor(out=wbl[:, 1:3, :].rearrange("p k n -> p (k n)"), in0=wst[:], scalar=WS,
                                       in1=wbh[:, 1:3, :].rearrange("p k n -> p (k n)"),
                                       op0=ALU.mult, op1=ALU.subtract).then_inc(vec_ready, 1)
                v.wait_ge(pool_ready, 1)

        def streams(order, seq, first=False):
            has_front = any(f for f, _ in order)
            has_back = any(not f for f, _ in order)

            def run(front, back):
                for f, n in order:
                    if f:
                        front(n)
                    else:
                        back(n)

            with nc.Block() as block:
                @block.sync
                def _(sp):

                    def front(n):
                        if n == AM:
                            sp.wait_ge(a_added, T)
                            nxt = x[1] if first else x[(seq + 2) % NS]
                            sp.dma_start(x_in[:], nxt.rearrange("(t p) d -> p t d", p=P)).then_inc(x_loaded, 16)

                    def back(n):
                        for kind in range(2):
                            for pair in range(4):
                                if n != (FK0 + 4 + 2 * pair, FQ0 + 2 + pair)[kind]:
                                    continue
                                m = kind * 8 + 2 * pair + 2
                                sp.wait_ge(b_nhi, m)
                                sp.wait_ge(b_nlo, m)
                                for j in range(2):
                                    for (src, tile, half) in (((nh, qst, 0), (nl, qst, 1)) if kind else
                                                              ((nh, kh, 0), (nh, kh, 1), (nl, kl, 0), (nl, kl, 1))):
                                        sp.dma_start(
                                            tile[half * DB:half * DB + DB, 4 * pair + j:4 * pair + j + 3:2, :],
                                            src[j * DB:j * DB + DB, pair % 2, :, :]).then_inc(b_spread[pair % 2], 16)
                        if n == NB - 1:
                            sp.wait_ge(BK.f_done, 1)
                            sp.dma_start(out[seq].rearrange("(t p) d -> p t d", p=P), x_b[:]).then_inc(x_stored, 16)

                    run(front, back)
                    if has_back:
                        sp.wait_ge(x_stored, 16)
                    if has_front:
                        sp.wait_ge(x_loaded, 16)

                @block.gpsimd
                def _(pool):

                    def front(n):
                        for i in range(T):
                            for r in range(GR):
                                if n != (15 if i == 0 else A0 + 3 * SLOTS_A.index(("unit", UA * (i - 1) + 1 + r)) + 1):
                                    continue
                                pool.wait_ge(a_stacked, 8)
                                if i >= 2:
                                    pool.wait_ge(a_filled, filled(SLOTS_A, ("unit", UA * (i - 1) - 1)))
                                nc.gpsimd.tensor_scalar(qm[:, i % 2, r:H:GR, :], qa4[:, :, i * P:(i + 1) * P],
                                                        head_rows[:, r:r + 1], None, ALU.mult).then_inc(a_masked, 1)

                    def back(n):
                        for a in range(16):
                            if n == (FK0 + 2 + a if a < 8 else FQ0 + 1 + (a - 8) // 2):
                                pool.wait_ge(b_nhi, a + 1)
                                if a >= 4:
                                    pool.wait_ge(*spread(a // 2 - 2))
                                nc.gpsimd.tensor_tensor(nl[:, (a // 2) % 2, a % 2, :], raw[:, a % 8, :],
                                                        nh[:, (a // 2) % 2, a % 2, :], ALU.subtract).then_inc(b_nlo, 1)

                    run(front, back)

                @block.tensor
                def _(pe):

                    def turn_x(st, k, src, dst):
                        pe.wait_ge(st.ln_ready, k)
                        for t in range(T):
                            ins = pe.transpose(dst[:, t * P:(t + 1) * P], src[:, t, :], ident[:])
                        ins.then_inc(st.turned, 1)

                    def mix(st, k, n):
                        b0, b1, b2 = st.banks
                        if n == 3:
                            turn_x(st, k, st.xn, b0)
                        if n == 6:
                            pe.wait_ge(st.f_mixed, 1)
                            pe.matmul(b1[:], wft[:, 1, :], st.mixed[:, 1, :], start=True, stop=True).then_inc(st.f_k, 1)
                            pe.wait_ge(st.f_mixed, 2)
                            for t in range(T):
                                ins = pe.matmul(b2[:, t * P:(t + 1) * P], st.mixed[:, 0, t * P:(t + 1) * P], wft[:, 0, :],
                                                start=True, stop=True)
                            ins.then_inc(st.f_r, 1)
                        if n == 9:
                            pe.wait_ge(st.f_ka, 1)
                            for t in range(T):
                                ins = pe.matmul(b0[:, t * P:(t + 1) * P], st.ka[:, t * P:(t + 1) * P], wft[:, 2, :],
                                                start=True, stop=True)
                            ins.then_inc(st.f_v, 1)

                    def a_sc(u):
                        i, hp = u // UA, u % UA
                        nk = min(i + 1, 2)
                        if hp == 0:
                            pe.wait_ge(a_masked, GR * (i + 1))
                        pe.matmul(SA[:, 0:2 * nk * P], identb[:], mask_a[:, :, (2 - nk) * P:2 * P],
                                  start=True, stop=False, skip_group_check=True)
                        for hh in range(2):
                            h = 2 * hp + hh
                            ins = pe.matmul(SA[:, hh * nk * P:(hh + 1) * nk * P], qm[:, i % 2, h, :],
                                            ka4[:, h // GR, (i + 1 - nk) * P:(i + 1) * P], start=False, stop=True,
                                            skip_group_check=True)
                        return ins

                    def a_glob(i):
                        ng = 2 * (i - 1)
                        v = SA[:, 0:ng * H].rearrange("p (g h) -> p g h", h=H)
                        pe.wait_ge(a_masked, GR * (i + 1))
                        for h in range(H):
                            ins = pe.matmul(v[:, :, h], qm[:, i % 2, h, :], ka4[:, h // GR, 0:ng * STRIDE:STRIDE],
                                            start=True, stop=True)
                        return ins

                    def a_turn(u):
                        nk = min(u // UA + 1, 2)
                        pe.wait_ge(a_exp, u + 1)
                        if u > 0:
                            pe.wait_ge(a_ptlo, u)
                        for c in range(2 * nk):
                            ins = pe.transpose(TA[:, c * P:(c + 1) * P], prob_a[:, c * P:(c + 1) * P], ident[:])
                        ins.then_inc(a_turned, 1)

                    def a_pvs(u):
                        i, hp = u // UA, u % UA
                        nk = min(i + 1, 2)
                        pe.wait_ge(a_ptlo, u + 1)
                        if hp == 0:
                            if i > 0:
                                pe.wait_ge(a_normed, i)
                        for hh in range(2):
                            h = 2 * hp + hh
                            o = OA[:, h * (DA + 1):(h + 1) * (DA + 1)]
                            for c in range(nk):
                                kt = i + 1 - nk + c
                                s = slice((hh * nk + c) * P, (hh * nk + c + 1) * P)
                                ins = product(o, pth_a[:, u % 2, s], ptl_a[:, u % 2, s], vah[:, kt, h, :], val[:, kt, h, :],
                                              first=(hp == 0 and hh == 0 and c == 0))
                        ins.then_inc(a_pv, 1)
                        if hp == UA - 1 and i >= 2:
                            pe.wait_ge(a_read, misc(SLOTS_A, ("turn_glob", i)))
                            v = slice(0, 2 * (i - 1) * H)
                            product(OA[:, 0:H * (DA + 1)], pgh[v, :], pgl[v, :], vgh[v, :, :].rearrange("p h d -> p (h d)"),
                                    vgl[v, :, :].rearrange("p h d -> p (h d)"), first=False).then_inc(a_out, 1)

                    def front(n):
                        if n == 3:
                            turn_x(FR, 1, FR.xn, SA)
                        if 6 <= n < 14:
                            a = n - 6
                            kind, grp = 1 - a // 4, a % 4
                            pe.wait_ge(xl_ready, 1)
                            if a > 1:
                                pe.wait_ge(a_stacked, a - 1)
                            product(PROJ_A[a % 2][:], wa4h[:, kind, grp, :], wa4l[:, kind, grp, :], xh_a[:], xl_a[:]
                                    ).then_inc(a_proj, 1)
                        if n == 14:
                            for t in range(T):
                                s = slice(t * P, (t + 1) * P)
                                ins = product(SA[:, s], xh_a[:, s], xl_a[:, s], wavh[:], wavl[:])
                            ins.then_inc(va_proj, 1)
                        if n == 15:
                            pe.wait_ge(xg_ready, 1)
                            pe.wait_ge(a_stacked, 8)
                            product(OA[0:NG * H, 0:D], xg[:, 0, :], xg[:, 1, :], wavh[:], wavl[:]).then_inc(vg_proj, 1)
                        if n == A0:
                            pe.wait_ge(va_ready, 1)
                            pe.wait_ge(vg_ready, 1)
                        if A0 <= n < AM:
                            slot, sub = (n - A0) // 3, (n - A0) % 3
                            kind, arg = at(SLOTS_A, slot) if sub == 0 else (None, 0)
                            if kind is not None:
                                if slot > 0:
                                    pe.wait_ge(*read_before(SLOTS_A, slot, a_exp, a_added, a_read))
                            if kind == "unit":
                                ins = a_sc(arg)
                            if kind == "glob":
                                ins = a_glob(arg)
                            if kind == "turn_glob":
                                ng = 2 * (arg - 1)
                                pe.wait_ge(a_gexp, arg - 1)
                                ins = pe.transpose(SA[0:ng * H, 0:P], pg[:, 0:ng * H], ident[:])
                            if kind == "turn_out":
                                pe.wait_ge(a_normed, arg + 1)
                                ins = pe.transpose(SA[:, 0:P], oa[:], ident[:])
                            if kind == "y":
                                pe.wait_ge(a_read, misc(SLOTS_A, ("turn_out", arg)))
                                ins = pe.matmul(SA[:, 0:D], oat[:], wproj[:], start=True, stop=True)
                            if kind is not None:
                                ins.then_inc(a_filled, 1)
                            u = unit(SLOTS_A, slot - 1)
                            if sub == 1 and u is not None:
                                a_turn(u)
                            u = unit(SLOTS_A, slot - 2)
                            if sub == 2 and u is not None:
                                a_pvs(u)
                        if n >= AM:
                            mix(FR, 2, n - AM)

                    def b_proj_free(j):
                        j -= 3
                        if j >= 16:
                            pe.wait_ge(b_raw, j - 8 + 1)
                        elif j >= 8:
                            pe.wait_ge(vb_lo, j - 8 + 1)
                        elif j >= 0:
                            pe.wait_ge(b_raw, j + 1)

                    def b_ssq(a):
                        pe.wait_ge(b_sq, a + 1)
                        if a == 8:
                            pe.wait_ge(b_norm, 7)
                        pe.matmul(OB[0][0:96, :], head_sum[:, H - 2 - 2 * (a % 8):H - 2 - 2 * (a % 8) + 96], sq[:, a % 2, :], start=(a % 8 == 0),
                                  stop=(a % 8 == 7)).then_inc(b_ss, 1)

                    def b_qk(a):
                        kind, b = 1 - a // 8, a % 8
                        j = a if kind else a + 8
                        b_proj_free(j)
                        xs = (xh_b, xl_b) if kind else (xqh, xql)
                        product(PROJ_B[j % 3][:], wbh[:, kind, b * P:(b + 1) * P], wbl[:, kind, b * P:(b + 1) * P],
                                xs[0][:], xs[1][:]).then_inc(b_proj, 1)

                    def b_v(a):
                        b_proj_free(a + 8)
                        t, s = a // 2, slice(a % 2 * 512, a % 2 * 512 + 512)
                        product(PROJ_B[(a + 8) % 3][:], xh_b[:, t * P:(t + 1) * P], xl_b[:, t * P:(t + 1) * P],
                                wbh[:, 2, s], wbl[:, 2, s]).then_inc(vb_proj, 1)

                    def b_fans(a):
                        pe.wait_ge(b_rns, a // 8 + 1)
                        if a > 1:
                            pe.wait_ge(b_norm, a - 1)
                        if a % 8 == 0:
                            pe.wait_ge(b_clamped, a // 8 + 1)
                        pe.matmul(OB[a % 2][:], head_fan[:, a % 8, :], rns[:], start=True, stop=True
                                  ).then_inc(b_fan, 1)

                    def b_nullsc(i):
                        for h in range(H):
                            o = SC[:, h:h + H + 1:H]
                            q = qst[:, h, i * P:(i + 1) * P]
                            pe.matmul(o, q, nkh[:, h:h + H + 1:H], start=True, stop=False, skip_group_check=True)
                            ins = pe.matmul(o, q, nkl[:, h:h + H + 1:H], start=False, stop=True, skip_group_check=True)
                        return ins

                    def b_sc(u):
                        i, h = u // H, u % H
                        w = (i + 1) * P
                        q = qst[:, h, i * P:(i + 1) * P]
                        pe.matmul(SC[:, 0:w], q, kh[:, h, 0:w], start=True, stop=False)
                        return pe.matmul(SC[:, 0:w], q, kl[:, h, 0:w], start=False, stop=True)

                    def b_turn(u):
                        pe.wait_ge(b_exp, u + 1)
                        if u > 1:
                            pe.wait_ge(b_ptlo, u - 1)
                        for c in range(u // H + 1):
                            ins = pe.transpose(TR[u % 2][:, c * P:(c + 1) * P], prob[:, u % 2, c * P:(c + 1) * P], ident[:])
                        ins.then_inc(b_turned, 1)

                    def b_pvs(u):
                        i, h = u // H, u % H
                        k = h // OBH
                        pe.wait_ge(b_ptlo, u + 1)
                        if h % OBH == 0:
                            if i >= 1:
                                pe.wait_ge(b_normed, 2 * (i - 1) + k + 1)
                            else:
                                pe.wait_ge(b_norm, 16)
                        o = OB[k][:, (h % OBH) * DB:(h % OBH + 1) * DB]
                        for c in range(i + 1):
                            s = slice(c * P, (c + 1) * P)
                            ins = product(o, pth[:, u % 3, s], ptl[:, u % 3, s], vbh[:, c, h, :], vbl[:, c, h, :],
                                          first=(h % OBH == 0 and c == 0))
                        ins.then_inc(b_pv, 1)
                        if h == H - 1:
                            pe.wait_ge(b_read, misc(SLOTS_B, ("turn_null", i)))
                            for k in range(2):
                                hs = slice(k * OBH, (k + 1) * OBH)
                                product(OB[k][:], pnh[:], pnl[:], nvbh[:, hs, :].rearrange("p h d -> p (h d)"),
                                        nvbl[:, hs, :].rearrange("p h d -> p (h d)"), first=False).then_inc(b_out, 1)

                    def back(n):
                        if n == 3:
                            turn_x(BK, 1, BK.xn, TR[0])
                        if K0 <= n < K0 + 8:
                            if n == K0:
                                pe.wait_ge(b_xl, 1)
                            if n == K0 + 2:
                                pe.wait_ge(xq_hi, 1)
                            b_qk(n - K0)
                        if n == 6:
                            turn_x(BK, 2, xn2, TR[1])
                        if K0 < n <= K0 + 8:
                            b_ssq(n - K0 - 1)
                        if V0 <= n < V0 + 8:
                            b_v(n - V0)
                        if FK0 <= n < FK0 + 8:
                            b_fans(n - FK0)
                        if Q0 <= n < Q0 + 8:
                            if n == Q0:
                                pe.wait_ge(xq_lo, 1)
                            b_qk(8 + n - Q0)
                        if Q0 < n <= Q0 + 8:
                            b_ssq(8 + n - Q0 - 1)
                        if FQ0 <= n < FQ0 + 4:
                            b_fans(8 + 2 * (n - FQ0))
                            b_fans(8 + 2 * (n - FQ0) + 1)
                        if n == B0:
                            pe.wait_ge(b_raw, 16)
                            pe.wait_ge(vb_lo, 2 * T)
                            pe.wait_ge(*spread(6))
                            pe.wait_ge(*spread(7))
                        if B0 <= n < BM:
                            slot = n - B0
                            kind, arg = at(SLOTS_B, slot)
                            if kind is not None:
                                if slot > 0:
                                    pe.wait_ge(*read_before(SLOTS_B, slot, b_biased, b_added, b_read))
                            if kind == "unit":
                                ins = b_sc(arg)
                            if kind == "null":
                                ins = b_nullsc(arg)
                            if kind == "turn_null":
                                pe.wait_ge(b_nexp, arg + 1)
                                ins = pe.transpose(SC[0:NN * H, 0:P], pn[:], ident[:])
                            if kind == "turn_out":
                                i, j = arg
                                pe.wait_ge(b_normed, 2 * i + j + 1)
                                for c in range(4):
                                    ins = pe.transpose(SC[:, c * P:(c + 1) * P],
                                                       ob[:, 8 * j + 2 * c:8 * j + 2 * c + 2, :].rearrange("p h d -> p (h d)"),
                                                       ident[:])
                            if kind == "y":
                                pe.wait_ge(b_read, misc(SLOTS_B, ("turn_out", (arg, 1))))
                                for c in range(8):
                                    ins = pe.matmul(SC[:, 0:D], obt[:, c, :], wout[:, c, :], start=(c == 0), stop=(c == 7))
                            if kind is not None:
                                ins.then_inc(b_filled, 1)
                            u = unit(SLOTS_B, slot - 2)
                            if u is not None:
                                b_turn(u)
                            u = unit(SLOTS_B, slot - 4)
                            if u is not None:
                                b_pvs(u)
                        if n >= BM:
                            mix(BK, 3, n - BM)

                    run(front, back)

                @block.scalar
                def _(act):
                    order = Order(act, act_order)

                    def root(st, k):
                        act.wait_ge(st.var_ready, k)
                        order.done(act.activation(st.lnv[:], st.mv[:, :, 1], ACT.Ln, bias=epsb[:, 0:1]))
                        act.activation(st.rstd[:], st.lnv[:], ACT.Exp, scale=-0.5).then_inc(st.rstd_ready, 1)

                    def mix(st, k, n):
                        b0, b1, b2 = st.banks
                        if n == 1:
                            root(st, k)
                        if n == 4:
                            act.wait_ge(st.turned, k)
                            copy(st.xt[:, 1:1 + S], b0[:]).then_inc(st.f_xt, 1)
                        if n == 6:
                            act.wait_ge(st.f_k, 1)
                            act.activation(st.kr[:], b1[:], ACT.Relu).then_inc(st.f_relu, 1)
                            act.wait_ge(st.f_r, 1)
                            act.activation(st.ez[:], b2[:], ACT.Exp, scale=-1.0).then_inc(st.f_e, 1)
                        if n == 8:
                            act.wait_ge(st.f_e1, 1)
                            act.wait_ge(st.f_ka, 1)
                            order.done(act.activation(st.ez[:], st.ez[:], ACT.Ln))
                            act.activation(st.gate[:], st.ez[:], ACT.Exp, scale=-1.0).then_inc(st.f_gate, 1)

                    def front(n):
                        if n == 1:
                            root(FR, 1)
                        if n == 4:
                            act.wait_ge(FR.turned, 1)
                            copy(xh_a[:], SA[:]).then_inc(xh_ready, 1)
                        if 6 <= n < 14:
                            a = n - 6
                            act.wait_ge(a_proj, a + 1)
                            if a > 1:
                                act.wait_ge(a_stacked, a - 1)
                            copy(ht[:, a % 2, :], PROJ_A[a % 2][:]).then_inc(a_hi, 1)
                        if n == 15:
                            act.wait_ge(va_proj, 1)
                            copy(vah[:, :, :, 0:DA].rearrange("p t h d -> p (t h) d"),
                                 SA[:].rearrange("p (t d) -> p t d", d=DA)).then_inc(va_hi, 1)
                        if A0 <= n < AM:
                            slot, sub = (n - A0) // 3, (n - A0) % 3
                            kind, arg = at(SLOTS_A, slot)
                            if sub == 0:
                                u = unit(SLOTS_A, slot - 2)
                                if u is not None:
                                    w = 2 * min(u // UA + 1, 2) * P
                                    act.wait_ge(a_turned, u + 1)
                                    if u > 1:
                                        act.wait_ge(a_pv, u - 1)
                                    copy(pth_a[:, u % 2, 0:w], TA[:, 0:w]).then_inc(a_pthi, 1)
                            if sub == 1:
                                if kind == "turn_glob":
                                    ng = 2 * (arg - 1)
                                    act.wait_ge(a_filled, filled(SLOTS_A, (kind, arg)))
                                    if arg > 2:
                                        act.wait_ge(a_out, arg - 2)
                                    copy(pgh[0:ng * H, :], SA[0:ng * H, 0:P]).then_inc(a_ghi, 1)
                                if kind == "turn_out":
                                    act.wait_ge(a_filled, filled(SLOTS_A, (kind, arg)))
                                    copy(oat[:], SA[:, 0:P]).then_inc(a_read, 1)
                            if sub == 2 and kind == "unit":
                                i = arg // UA
                                hp = arg % UA
                                nk = min(i + 1, 2)
                                act.wait_ge(a_bias, arg + 1)
                                if arg > 0:
                                    act.wait_ge(a_turned, arg)
                                for hh in range(2):
                                    h = 2 * hp + hh
                                    s = slice(hh * nk * P, (hh + 1) * nk * P)
                                    ins = act.activation(prob_a[:, s], SA[:, s], ACT.Exp, scale=-C_A,
                                                         bias=abias[:, i % 2, h:h + 1])
                                ins.then_inc(a_exp, 1)
                                if hp == UA - 1 and i >= 2:
                                    ng = 2 * (i - 1)
                                    act.wait_ge(a_gt, i - 1)
                                    act.activation(pg[:, 0:ng * H], gt[:, 0:ng * H], ACT.Exp).then_inc(a_gexp, 1)
                        if n >= AM:
                            mix(FR, 2, n - AM)

                    def b_root(kind):
                        act.wait_ge(b_clamped, kind + 1)
                        order.done(act.activation(rn[:], rn[:], ACT.Ln, scale=256.0))
                        act.activation(rn[:], rn[:], ACT.Exp, scale=-0.5, bias=epsb[0:96, 1:2]).then_inc(b_rn, 1)

                    def b_his(a):
                        act.wait_ge(b_norm, a + 1)
                        if a >= 4:
                            act.wait_ge(*spread(a // 2 - 2))
                        copy(nh[:, (a // 2) % 2, a % 2, :], raw[:, a % 8, :]).then_inc(b_nhi, 1)

                    def b_evac(a):
                        j = a if a < 8 else a + 8
                        act.wait_ge(b_proj, a + 1)
                        if a > 1:
                            act.wait_ge(b_ss, a - 1)
                        act.activation(sq[:, a % 2, :], PROJ_B[j % 3][:], ACT.Square).then_inc(b_sq, 1)
                        if a > 7:
                            act.wait_ge(b_nlo, a - 7)
                        copy(raw[:, a % 8, :], PROJ_B[j % 3][:]).then_inc(b_raw, 1)

                    def b_vhi(a):
                        t, hf = a // 2, a % 2
                        act.wait_ge(vb_proj, a + 1)
                        copy(vbh[:, t, 8 * hf:8 * hf + 8, :].rearrange("p h d -> p (h d)"),
                             PROJ_B[(a + 8) % 3][:]).then_inc(vb_hi, 1)

                    def back(n):
                        if n == 1:
                            root(BK, 1)
                        if n == 4:
                            root(BK, 2)
                            act.wait_ge(BK.turned, 1)
                            copy(xh_b[:], TR[0][:]).then_inc(b_xh, 1)
                        if n == 7:
                            act.wait_ge(BK.turned, 2)
                            order.done(act.activation(xq[:], TR[1][:], ACT.Identity, scale=cols[:, 0:1], bias=cols[:, 1:2]))
                            copy(xqh[:], xq[:]).then_inc(xq_hi, 1)
                        if K0 <= n < K0 + 8:
                            b_evac(n - K0)
                        if n == V0 + 2:
                            b_root(0)
                        if V0 <= n < V0 + 8:
                            b_vhi(n - V0)
                        if FK0 + 1 < n <= FK0 + 9:
                            b_his(n - FK0 - 2)
                        if Q0 <= n < Q0 + 8:
                            b_evac(8 + n - Q0)
                        if n == Q0 + 9:
                            b_root(1)
                        if FQ0 < n <= FQ0 + 4:
                            b_his(8 + 2 * (n - FQ0 - 1))
                            b_his(8 + 2 * (n - FQ0 - 1) + 1)
                        if B0 <= n < BM:
                            slot = n - B0
                            kind, arg = at(SLOTS_B, slot)
                            u = unit(SLOTS_B, slot - 3)
                            if u is not None:
                                w = (u // H + 1) * P
                                act.wait_ge(b_turned, u + 1)
                                if u > 2:
                                    act.wait_ge(b_pv, u - 2)
                                copy(pth[:, u % 3, 0:w], TR[u % 2][:, 0:w]).then_inc(b_pthi, 1)
                            if kind == "turn_null":
                                act.wait_ge(b_filled, filled(SLOTS_B, (kind, arg)))
                                if arg > 0:
                                    act.wait_ge(b_out, 2 * arg)
                                copy(pnh[:], SC[0:NN * H, 0:P]).then_inc(b_nhi2, 1)
                            if kind == "turn_out":
                                i, j = arg
                                act.wait_ge(b_filled, filled(SLOTS_B, (kind, arg)))
                                copy(obt[:, 4 * j:4 * j + 4, :].rearrange("p c q -> p (c q)"), SC[:]).then_inc(b_read, 1)
                            u = unit(SLOTS_B, slot - 1)
                            if u is not None:
                                i, h = u // H, u % H
                                w = (i + 1) * P
                                act.wait_ge(b_biased, u + 1)
                                if u > 1:
                                    act.wait_ge(b_turned, u - 1)
                                act.activation(prob[:, u % 2, 0:w], sbias[:, u % 2, 0:w], ACT.Exp, scale=-1.0,
                                               bias=bmin[:, i % 2, h:h + 1],
                                               accum_out=bden[:, i % 2, h:h + 1]).then_inc(b_exp, 1)
                                if h == H - 1:
                                    act.wait_ge(b_nt, i + 1)
                                    if i > 0:
                                        act.wait_ge(b_normed, 2 * i)
                                    act.activation(pn[:], nt[:], ACT.Exp).then_inc(b_nexp, 1)
                        if n >= BM:
                            mix(BK, 3, n - BM)

                    run(front, back)

                @block.vector
                def _(v):
                    order = Order(v, vec_order)
                    done = order.done

                    def ln_stats(st, src):
                        for t in range(T):
                            ins = v.bn_stats(st.stats[:, t, :], src[:, t, :])
                        done(ins)
                        for t in range(T):
                            ins = v.bn_aggr(st.mv[:, t, :], st.stats[:, t, :])
                        ins.then_inc(st.var_ready, 1)

                    def ln_apply(st, k, src, dst):
                        v.wait_ge(st.var_ready, k)
                        v.wait_ge(st.rstd_ready, k)
                        for t in range(T):
                            ins = v.tensor_scalar(dst[:, t, :], src[:, t, :], st.mv[:, t, 0:1], st.rstd[:, t:t + 1],
                                                  ALU.subtract, ALU.mult)
                        ins.then_inc(st.ln_ready, 1)

                    def mix(st, k, n, src, dst, free):
                        b0, b1, b2 = st.banks
                        if n == 0:
                            ln_stats(st, src)
                        if n == 2:
                            ln_apply(st, k, src, st.xn)
                            v.memset(st.xt[:, 0:1], 0.0).then_inc(st.ln_ready, 1)
                        if n == 5:
                            v.wait_ge(st.f_xt, 1)
                            v.wait_ge(st.ln_ready, k + 1)
                            for j in (1, 0):
                                done(v.tensor_scalar(st.prev[:], st.xt[:, 0:S], colx[:, 1 + j:2 + j], None, ALU.mult))
                                v.scalar_tensor_tensor(out=st.mixed[:, j, :], in0=st.xt[:, 1:1 + S], scalar=cols[:, 4 + j:5 + j],
                                                       in1=st.prev[:], op0=ALU.mult, op1=ALU.add).then_inc(st.f_mixed, 1)
                                v.wait_ge(st.f_mixed, 2 - j)
                        if n == 7:
                            v.wait_ge(st.f_e, 1)
                            v.tensor_scalar(st.ez[:], st.ez[:], 1e18, 1.0, ALU.min, ALU.add).then_inc(st.f_e1, 1)
                            v.wait_ge(st.f_relu, 1)
                            v.scalar_tensor_tensor(out=st.ka[:], in0=b1[:], scalar=0.0, in1=st.kr[:],
                                                   op0=ALU.max, op1=ALU.mult).then_inc(st.f_ka, 1)
                        if n == 10:
                            v.wait_ge(st.f_gate, 1)
                            v.wait_ge(st.f_v, 1)
                            done(v.tensor_tensor(st.gv[:], b0[:], st.gate[:], ALU.mult))
                            free()
                            dv, sv = dst[:].rearrange("p t d -> p (t d)"), src[:].rearrange("p t d -> p (t d)")
                            v.tensor_tensor(dv, st.gv[:], sv, ALU.add).then_inc(st.f_done, 1)

                    def a_min(u):
                        i, hp = u // UA, u % UA
                        nk = min(i + 1, 2)
                        v.wait_ge(a_filled, filled(SLOTS_A, ("unit", u)))
                        m, b = amin[:, 2 * hp:2 * hp + 2], abias[:, i % 2, 2 * hp:2 * hp + 2]
                        done(v.tensor_reduce(m, SA[:, 0:2 * nk * P].rearrange("p (h k) -> p h k", h=2), AX.X, ALU.min))
                        if i >= 2:
                            ins = v.scalar_tensor_tensor(out=b, in0=m, scalar=C_A, in1=gmin[:, 2 * hp:2 * hp + 2],
                                                         op0=ALU.mult, op1=ALU.min)
                        else:
                            ins = v.tensor_scalar(b, m, C_A, None, ALU.mult)
                        ins.then_inc(a_bias, 1)
                        if hp == UA - 1 and i >= 2:
                            ng = 2 * (i - 1)
                            v.wait_ge(a_bias, UA * (i + 1))
                            v.tensor_tensor(gt[:, 0:ng * H].rearrange("p (g h) -> p g h", h=H),
                                            abias[:, i % 2, :].unsqueeze(1).broadcast_to([P, ng, H]),
                                            sgs[:, 0:ng * H].rearrange("p (g h) -> p g h", h=H), ALU.subtract).then_inc(a_gt, 1)

                    def a_gmin(i):
                        ng = 2 * (i - 1)
                        if i > 2:
                            v.wait_ge(a_gt, i - 2)
                        v.wait_ge(a_filled, filled(SLOTS_A, ("glob", i)))
                        v.tensor_scalar(sgs[:, 0:ng * H], SA[:, 0:ng * H], C_A, None, ALU.mult).then_inc(a_read, 1)
                        v.wait_ge(a_read, misc(SLOTS_A, ("glob", i)))
                        done(v.tensor_reduce(gmin[:], sgs[:, 0:ng * H].rearrange("p (g h) -> p h g", h=H), AX.X, ALU.min))

                    def a_norm(i):
                        if i >= 2:
                            v.wait_ge(a_out, i - 1)
                        else:
                            v.wait_ge(a_pv, UA * (i + 1))
                        if i >= 1:
                            v.wait_ge(a_filled, filled(SLOTS_A, ("turn_out", i - 1)))
                        o = OA[:, 0:H * (DA + 1)].rearrange("p (h d) -> p h d", d=DA + 1)
                        done(v.reciprocal(rden_a[:], o[:, :, DA]))
                        v.tensor_tensor(oa[:].rearrange("p (h d) -> p h d", d=DA), o[:, :, 0:DA],
                                        rden_a[:].unsqueeze(2).broadcast_to([P, H, DA]), ALU.mult).then_inc(a_normed, 1)

                    def front(n):
                        if n == 0:
                            if first:
                                v.wait_ge(x_first, 16)
                            ln_stats(FR, x_in)
                        if n == 2:
                            ln_apply(FR, 1, x_in, FR.xn)
                        if n == 5:
                            v.wait_ge(xh_ready, 1)
                            v.tensor_tensor(xl_a[:], SA[:], xh_a[:], ALU.subtract).then_inc(xl_ready, 1)
                            v.wait_ge(xl_ready, 1)
                            for k, part in enumerate((xh_a, xl_a)):
                                ins = v.tensor_copy(xg[:, k, :].rearrange("p (g h) -> p g h", h=H),
                                                    part[:, 0:NG * STRIDE:STRIDE].unsqueeze(2).broadcast_to([P, NG, H]))
                            ins.then_inc(xg_ready, 1)
                        if 7 <= n < 15:
                            a = n - 7
                            kind, grp = 1 - a // 4, a % 4
                            v.wait_ge(a_hi, a + 1)
                            dst = ka4 if kind else qa4
                            v.scalar_tensor_tensor(out=dst[:, grp, :], in0=ht[:, a % 2, :], scalar=lo_rows[:, kind:kind + 1],
                                                   in1=PROJ_A[a % 2][:], op0=ALU.mult, op1=ALU.add).then_inc(a_stacked, 1)
                        if n == 16:
                            v.wait_ge(va_hi, 1)
                            v.tensor_tensor(val[:, :, :, 0:DA].rearrange("p t h d -> p (t h) d"),
                                            SA[:].rearrange("p (t d) -> p t d", d=DA),
                                            vah[:, :, :, 0:DA].rearrange("p t h d -> p (t h) d"), ALU.subtract).then_inc(va_ready, 1)
                            v.wait_ge(vg_proj, 1)
                            one = blk[0:NG * H, :].unsqueeze(2).broadcast_to([NG * H, H, DA])
                            done(v.scalar_tensor_tensor(out=vgt[:], in0=OA[0:NG * H, 0:D].rearrange("p (h d) -> p h d", d=DA),
                                                        scalar=1.0 / WS, in1=one, op0=ALU.mult, op1=ALU.mult))
                            done(v.tensor_copy(vgh[:, :, 0:DA], vgt[:]))
                            v.tensor_tensor(vgl[:, :, 0:DA], vgt[:], vgh[:, :, 0:DA], ALU.subtract).then_inc(vg_ready, 1)
                        if A0 <= n < AM:
                            slot, sub = (n - A0) // 3, (n - A0) % 3
                            kind, arg = at(SLOTS_A, slot)
                            if sub == 0:
                                u = unit(SLOTS_A, slot - 3)
                                if u is not None and u % UA == UA - 1:
                                    a_norm(u // UA)
                                u = unit(SLOTS_A, slot - 2)
                                if u is not None:
                                    w = 2 * min(u // UA + 1, 2) * P
                                    v.wait_ge(a_pthi, u + 1)
                                    v.tensor_tensor(ptl_a[:, u % 2, 0:w], TA[:, 0:w], pth_a[:, u % 2, 0:w], ALU.subtract
                                                    ).then_inc(a_ptlo, 1)
                            if sub == 1:
                                if kind == "unit":
                                    a_min(arg)
                                if kind == "glob":
                                    a_gmin(arg)
                                if kind == "y":
                                    v.wait_ge(a_filled, filled(SLOTS_A, (kind, arg)))
                                    v.tensor_tensor(x_a[:, arg, :], SA[:, 0:D], x_in[:, arg, :], ALU.add).then_inc(a_added, 1)
                            if sub == 2:
                                if kind == "turn_glob":
                                    ng = 2 * (arg - 1)
                                    v.wait_ge(a_ghi, arg - 1)
                                    v.tensor_tensor(pgl[0:ng * H, :], SA[0:ng * H, 0:P], pgh[0:ng * H, :], ALU.subtract
                                                    ).then_inc(a_read, 1)
                        if n == AM:
                            v.wait_ge(a_added, T)
                        if n >= AM:
                            mix(FR, 2, n - AM, x_a, x_f, (lambda: v.wait_ge(b_added, T)) if has_back else (lambda: None))

                    def b_rsplit(kind):
                        v.wait_ge(b_rn, kind + 1)
                        if kind:
                            v.wait_ge(b_fan, 8)
                        done(v.tensor_copy(rnh[:], rn[:]))
                        v.scalar_tensor_tensor(out=rns[:], in0=rnh[:], scalar=lo_rows[0:96, 2:3], in1=rn[:],
                                               op0=ALU.mult, op1=ALU.add).then_inc(b_rns, 1)

                    def b_norms(a):
                        v.wait_ge(b_fan, a + 1)
                        v.wait_ge(b_raw, a + 1)
                        scale = cols[:, 3:4] if a < 8 else colx[:, 0:1]
                        v.scalar_tensor_tensor(out=raw[:, a % 8, :], in0=OB[a % 2][:], scalar=scale,
                                               in1=raw[:, a % 8, :], op0=ALU.mult, op1=ALU.mult).then_inc(b_norm, 1)

                    def b_vlo(a):
                        t, hf = a // 2, a % 2
                        v.wait_ge(vb_hi, a + 1)
                        v.tensor_tensor(vbl[:, t, 8 * hf:8 * hf + 8, :].rearrange("p h d -> p (h d)"), PROJ_B[(a + 8) % 3][:],
                                        vbh[:, t, 8 * hf:8 * hf + 8, :].rearrange("p h d -> p (h d)"),
                                        ALU.subtract).then_inc(vb_lo, 1)

                    def b_nullbias(i):
                        v.wait_ge(b_filled, filled(SLOTS_B, ("null", i)))
                        v.tensor_tensor(snb[:, i % 2].rearrange("p n h -> p (n h)"), SC[:, 0:NN * H],
                                        alibi_null[:, i].rearrange("p n h -> p (n h)"), ALU.add).then_inc(b_read, 1)
                        v.wait_ge(b_read, misc(SLOTS_B, ("null", i)))
                        done(v.tensor_tensor(nmin[:], snb[:, i % 2, 0, :], snb[:, i % 2, 1, :], ALU.min))

                    def b_bias(u):
                        i, h = u // H, u % H
                        w = (i + 1) * P
                        n = filled(SLOTS_B, ("unit", u))
                        v.wait_ge(b_filled, n)
                        if u > 1:
                            v.wait_ge(b_exp, u - 1)
                        v.tensor_tensor_reduce(sbias[:, u % 2, 0:w], SC[:, 0:w], alibi[:, h, S - w:S],
                                               1.0, nmin[:, h:h + 1], ALU.add, ALU.min,
                                               bmin[:, i % 2, h:h + 1]).then_inc(b_biased, 1)

                    def b_normal(i):
                        v.wait_ge(b_exp, H * (i + 1))
                        v.wait_ge(b_nexp, i + 1)
                        if i >= 1:
                            v.wait_ge(b_filled, filled(SLOTS_B, ("turn_out", (i - 1, 1))))
                        done(v.tensor_tensor(den[:], bden[:, i % 2, :], pn[:, 0:H], ALU.add))
                        done(v.tensor_tensor(den[:], den[:], pn[:, H:2 * H], ALU.add))
                        done(v.reciprocal(rden_b[:], den[:]))
                        for k in range(2):
                            v.wait_ge(b_out, 2 * i + k + 1)
                            hs = slice(k * OBH, (k + 1) * OBH)
                            v.tensor_tensor(ob[:, hs, :], OB[k][:].rearrange("p (h d) -> p h d", d=DB),
                                            rden_b[:, hs].unsqueeze(2).broadcast_to([P, OBH, DB]), ALU.mult).then_inc(b_normed, 1)

                    def back(n):
                        if n == 0:
                            ln_stats(BK, x_f)
                        if n == 2:
                            ln_apply(BK, 1, x_f, BK.xn)
                        if n == 3:
                            v.wait_ge(BK.ln_ready, 1)
                            ln_stats(BK, BK.xn)
                        if n == 5:
                            ln_apply(BK, 2, BK.xn, xn2)
                            v.wait_ge(b_xh, 1)
                            v.tensor_tensor(xl_b[:], TR[0][:], xh_b[:], ALU.subtract).then_inc(b_xl, 1)
                        if n == 8:
                            v.wait_ge(xq_hi, 1)
                            v.tensor_tensor(xql[:], xq[:], xqh[:], ALU.subtract).then_inc(xq_lo, 1)
                        for kind, at_step in ((0, V0 + 1), (1, Q0 + 8)):
                            if n == at_step:
                                v.wait_ge(b_ss, 8 * kind + 8)
                                v.wait_ge(xq_lo, 1)
                                if kind > 0:
                                    v.wait_ge(b_rns, kind)
                                v.tensor_scalar(rn[:], OB[0][0:96, :], 4.096e-21, None, ALU.max).then_inc(b_clamped, 1)
                            if n == at_step + 2:
                                b_rsplit(kind)
                        if V0 < n <= V0 + 8:
                            b_vlo(n - V0 - 1)
                        if FK0 < n <= FK0 + 8:
                            b_norms(n - FK0 - 1)
                        if FQ0 <= n < FQ0 + 4:
                            b_norms(8 + 2 * (n - FQ0))
                            b_norms(8 + 2 * (n - FQ0) + 1)
                        if B0 <= n < BM:
                            slot = n - B0
                            kind, arg = at(SLOTS_B, slot)
                            u = unit(SLOTS_B, slot - 5)
                            if u is not None and u % H == H - 1:
                                b_normal(u // H)
                            if kind == "unit":
                                b_bias(arg)
                                i, h = arg // H, arg % H
                                if h == H - 1:
                                    v.wait_ge(b_biased, H * (i + 1))
                                    if i > 0:
                                        v.wait_ge(b_nexp, i)
                                    v.tensor_tensor(nt[:].rearrange("p (n h) -> p n h", h=H),
                                                    bmin[:, i % 2, :].unsqueeze(1).broadcast_to([P, NN, H]),
                                                    snb[:, i % 2], ALU.subtract).then_inc(b_nt, 1)
                            if kind == "null":
                                b_nullbias(arg)
                            if kind == "y":
                                v.wait_ge(b_filled, filled(SLOTS_B, (kind, arg)))
                                v.tensor_tensor(x_b[:, arg, :], SC[:, 0:D], x_f[:, arg, :], ALU.add).then_inc(b_added, 1)
                            u = unit(SLOTS_B, slot - 3)
                            if u is not None:
                                w = (u // H + 1) * P
                                v.wait_ge(b_pthi, u + 1)
                                v.tensor_tensor(ptl[:, u % 3, 0:w], TR[u % 2][:, 0:w], pth[:, u % 3, 0:w], ALU.subtract
                                                ).then_inc(b_ptlo, 1)
                            if kind == "turn_null":
                                v.wait_ge(b_nhi2, arg + 1)
                                v.tensor_tensor(pnl[:], SC[0:NN * H, 0:P], pnh[:], ALU.subtract).then_inc(b_read, 1)
                        if n == BM:
                            v.wait_ge(b_added, T)
                        if n >= BM:
                            mix(BK, 3, n - BM, x_b, x_b, lambda: None)

                    run(front, back)

            nc.all_engine_barrier(sems_to_clear=range(x_loaded.num, last_sem.num + 1))

        streams(FRONT_ONLY, None, first=True)
        with nc.Fori(0, NS - 1) as seq:
            streams(BOTH, seq)
        streams(BACK_ONLY, NS - 1)


WLOADS = 17

_INS = ["L0_attn_a_x", "L0_attn_a_Wqkv", "L0_attn_a_Wproj", "L0_attn_b_norm_g", "L0_attn_b_norm_b",
        "L0_attn_b_Wq", "L0_attn_b_Wkv", "L0_attn_b_q_scale", "L0_attn_b_k_scale", "L0_attn_b_null_kv",
        "L0_attn_b_Wout", "L0_ffn_W_r", "L0_ffn_W_k", "L0_ffn_W_v", "L0_ffn_mu_r", "L0_ffn_mu_k"]


def kernel(**inputs):
    import numpy as _np
    import concourse.bacc as _bacc
    from concourse import mybir as _mybir
    from concourse.bass_utils import run_bass_kernel_spmd as _run

    nc = _bacc.Bacc("TRN2", target_bir_lowering=False, num_devices=1)
    arrays, args = {}, []
    for name in _INS:
        a = _np.ascontiguousarray(inputs[name])
        arrays[f"in_{name}"] = a
        args.append(nc.dram_tensor(f"in_{name}", a.shape, _mybir.dt.from_np(a.dtype), kind="ExternalInput").ap())
    shape = inputs["L0_attn_a_x"].shape
    args.append(nc.dram_tensor("out_0", shape, _mybir.dt.float32, kind="ExternalOutput").ap())
    program(nc, *args)
    r = _run(nc, [arrays], core_ids=[0])
    return r.results[0]["out_0"]
```

```python
from contextlib import ExitStack
import math

import concourse.bass as bass
from concourse import mybir

F32 = mybir.dt.float32
F16 = mybir.dt.float16
BF16 = mybir.dt.bfloat16
I32 = mybir.dt.int32
ALU = mybir.AluOpType
ACT = mybir.ActivationFunctionType
AX = mybir.AxisListType

P = 128
D = 128
H = 16
DA = D // H
DB = 64
NN = 2
STRIDE = 64
EPS = 1e-5
WS = 64.0
MASKED = 1e30
REPS = 4
GR = 4
OBH = 8


def program(nc, x, a_wqkv, a_wproj, b_g, b_b, b_wq, b_wkv, b_qs, b_ks, b_nullkv, b_wout,
            f_wr, f_wk, f_wv, f_mur, f_muk, out):
    NS, S, _ = x.shape
    T = S // P
    NG = S // STRIDE // 2
    C_A = 1.0 / (WS * WS * math.sqrt(DA))
    start = 2.0 ** (-2.0 ** (-(math.log2(H) - 3)))
    slopes = [start * start ** h for h in range(H)]
    UNITS_A = [(i, h, n) for i in range(T) for n in (512 // (min(i + 1, 2) * P),) for h in range(0, H, n)]
    UNITS_B = [(i, h, n) for i in range(T) for n in (max(512 // ((i + 1) * P), 1),) for h in range(0, H, n)]

    def upto(units, i):
        return sum(t <= i for t, _, _ in units)


    ctx = ExitStack()
    with ctx:
        def sb(name, shape, dt=F32):
            return ctx.enter_context(nc.sbuf_tensor(name, shape, dt))

        def sem(name):
            return ctx.enter_context(nc.semaphore(name))

        def bank(name, dt=F32):
            return ctx.enter_context(nc.psum_tensor(name, [P, 512], dt))
        SA, TA, OA = bank("scores_a"), bank("turned_a"), bank("out_a")
        SC, TR, OB = bank("scores_b"), [bank("turned_b0"), bank("turned_b1")], [bank("out_b0"), bank("out_b1")]
        PROJ_A = [TA, OA]
        PROJ_B = [SC, TR[0], TR[1]]

        scratch = sb("scratch", [P, 8 * S])
        split_space = sb("split_space", [P, 4 * S])
        bias_space = sb("bias_space", [P, 2 * S])
        norm_space = sb("norm_space", [P, 2 * S])
        stack_space = sb("stack_space", [P, H * S], F16)
        front_space = sb("front_space", [P, 7 * S + 8])

        def half(space, a, b, **dims):
            return space[:, a:b].bitcast(F16).rearrange("p (n s) -> p n s", s=S)

        wst = scratch[:, 0:2048]
        wst_kv = stack_space[:, 0:4 * H * DB].bitcast(F32)
        wa4 = scratch[:, 2048:3072].rearrange("p (k h r d) -> p k h r d", k=2, h=H, r=REPS)
        wa_sb = scratch[:, 3072:3072 + 3 * D]
        wfn = scratch[:, 3456:3456 + 3 * D].rearrange("p (k d) -> p k d", k=3)
        dist_i = bias_space[:, 0:S].bitcast(I32)
        dist = bias_space[:, S:2 * S]
        ka4 = half(front_space, 0, 2 * S)
        qa4 = half(front_space, 2 * S, 4 * S)
        ht = half(front_space, 4 * S, 5 * S)
        prob_a = front_space[:, 4 * S:5 * S]
        pth_a = half(front_space, 5 * S, 6 * S)
        ptl_a = half(front_space, 6 * S, 7 * S)
        raw = scratch[:].rearrange("p (n s) -> p n s", s=S)
        nh = half(split_space, 0, 2 * S).rearrange("p (a b) s -> p a b s", a=2)
        nl = half(split_space, 2 * S, 4 * S).rearrange("p (a b) s -> p a b s", a=2)
        sq = bias_space[:].rearrange("p (n s) -> p n s", s=S)
        xq = norm_space[:, 0:S]
        rn = norm_space[0:96, 0:S]
        rnh, rns = [half(norm_space, S, 2 * S)[0:96, j, :] for j in range(2)]
        qst = stack_space[:].rearrange("p (h s) -> p h s", h=H)
        sbias = scratch[:, 0:2 * S].rearrange("p (n s) -> p n s", s=S)
        prob = scratch[:, 2 * S:4 * S].rearrange("p (n s) -> p n s", s=S)
        pth = half(scratch, 4 * S, 11 * S // 2)
        ptl = half(scratch, 11 * S // 2, 7 * S)
        ob = split_space[:, 0:H * DB].rearrange("p (h d) -> p h d", h=H)
        obt = split_space[:, H * DB:2 * H * DB].rearrange("p (c q) -> p c q", q=P)

        ident = sb("ident", [P, P])
        identb = sb("identb", [P, P], BF16)
        mask_a = sb("mask_a", [P, 2 * P], BF16)
        lo_rows = sb("lo_rows", [P, 3])
        rowi = sb("rowi", [P, 4], I32)
        head_rows = sb("head_rows", [P, GR])
        alibi = sb("alibi", [P, H, S])
        null_i = sb("null_i", [P, T, NN], I32)
        null_f = sb("null_f", [P, T, NN])
        alibi_null = sb("alibi_null", [P, T, NN, H])
        blk = sb("blk", [P, H])
        head_sum = sb("head_sum", [P, 96 + H - 2])
        head_fan = sb("head_fan", [96, 8, P], F16)
        fan_row = sb("fan_row", [P, 2, H])
        epsb = sb("epsb", [P, 4])
        wa4h = sb("wa4h", [P, 2, GR, P], F16)
        wa4l = sb("wa4l", [P, 2, GR, P], F16)
        wavh = sb("wavh", [P, D], F16)
        wavl = sb("wavl", [P, D], F16)
        wproj = sb("wproj", [P, D])
        wbh = sb("wbh", [P, 3, H * DB], F16)
        wbl = sb("wbl", [P, 3, H * DB], F16)
        wout = sb("wout", [P, 8, D])
        wft = sb("wft", [P, 3, D])
        cols = sb("cols", [P, 6])
        colx = sb("colx", [P, 3])
        nk_sb = sb("nk_sb", [NN * H, 2, DB])
        nkd = sb("nkd", [NN * H, 2 * DB])
        nks = sb("nks", [NN * H, 4])
        nkf = sb("nkf", [P, NN * H])
        nkh = sb("nkh", [P, NN * H], F16)
        nkl = sb("nkl", [P, NN * H], F16)
        nvh = sb("nvh", [NN * H, DB], F16)
        nvl = sb("nvl", [NN * H, DB], F16)
        nvbh = sb("nvbh", [NN * H, H, DB], F16)
        nvbl = sb("nvbl", [NN * H, H, DB], F16)

        x_in = sb("x_in", [P, T, D])
        x_a = sb("x_a", [P, T, D])
        x_next = sb("x_next", [P, T, D])
        x_f = sb("x_f", [P, T, D])
        x_b = sb("x_b", [P, T, D])
        xh_b, xl_b = sb("xh_b", [P, S], F16), sb("xl_b", [P, S], F16)
        xg = sb("xg", [P, 2, NG * H], F16)
        qm = sb("qm", [P, 2, H, P], F16)
        vah = sb("vah", [P, T, H, DA + 1], F16)
        val = sb("val", [P, T, H, DA + 1], F16)
        vgt = sb("vgt", [NG * H, H, DA])
        vgh = sb("vgh", [NG * H, H, DA + 1], F16)
        vgl = sb("vgl", [NG * H, H, DA + 1], F16)
        sgs = sb("sgs", [P, NG * H])
        gmin = sb("gmin", [P, H])
        amin = sb("amin", [P, H])
        abias = sb("abias", [P, 2, H])
        gt = sb("gt", [P, NG * H])
        pg = sb("pg", [P, NG * H])
        pgh = sb("pgh", [NG * H, P], F16)
        pgl = sb("pgl", [NG * H, P], F16)
        oa = sb("oa", [P, D])
        oat = sb("oat", [P, D])
        rden_a = sb("rden_a", [P, H])
        kh = sb("kh", [P, H, S], F16)
        kl = sb("kl", [P, H, S], F16)
        vbh = sb("vbh", [P, T, H, DB], F16)
        vbl = sb("vbl", [P, T, H, DB], F16)
        snb = sb("snb", [P, 2, NN, H])
        nmin = sb("nmin", [P, H])
        bmin = sb("bmin", [P, 2, H])
        bden = sb("bden", [P, 2, H])
        den = sb("den", [P, H])
        rden_b = sb("rden_b", [P, H])
        nt = sb("nt", [P, NN * H])
        pn = sb("pn", [P, NN * H])
        pnh = sb("pnh", [NN * H, P], F16)
        pnl = sb("pnl", [NN * H, P], F16)
        xn2 = x_b

        w_loaded = sem("w_loaded")
        w_staged = sem("w_staged")
        pool_setup = sem("pool_setup")
        vec_setup = sem("vec_setup")
        act_setup = sem("act_setup")
        ident_ready = sem("ident_ready")
        iotas_ready = sem("iotas_ready")
        pool_ready = sem("pool_ready")
        alibi_ready = sem("alibi_ready")
        null_ss = sem("null_ss")
        nulls_scaled = sem("nulls_scaled")
        vec_ready = sem("vec_ready")
        wav_hi = sem("wav_hi")
        wq_hi = sem("wq_hi")
        null_root = sem("null_root")
        nv_hi = sem("nv_hi")
        act_ready = sem("act_ready")
        mix_turned = sem("mix_turned")
        nulls_turned = sem("nulls_turned")
        x_first = sem("x_first")
        x_loaded = sem("x_loaded")
        x_stored = sem("x_stored")
        vec_order = sem("vec_order")
        act_order = sem("act_order")
        xh_ready = sem("xh_ready")
        xl_ready = sem("xl_ready")
        xg_ready = sem("xg_ready")
        a_proj = sem("a_proj")
        a_hi = sem("a_hi")
        a_stacked = sem("a_stacked")
        a_masked = sem("a_masked")
        va_proj = sem("va_proj")
        va_hi = sem("va_hi")
        va_ready = sem("va_ready")
        vg_proj = sem("vg_proj")
        vg_ready = sem("vg_ready")
        a_filled = sem("a_filled")
        a_read = sem("a_read")
        a_bias = sem("a_bias")
        a_exp = sem("a_exp")
        a_turned = sem("a_turned")
        a_pthi = sem("a_pthi")
        a_ptlo = sem("a_ptlo")
        a_pv = sem("a_pv")
        a_gt = sem("a_gt")
        a_gexp = sem("a_gexp")
        a_ghi = sem("a_ghi")
        a_out = sem("a_out")
        a_normed = sem("a_normed")
        a_added = sem("a_added")
        b_xh = sem("b_xh")
        b_xl = sem("b_xl")
        xq_hi = sem("xq_hi")
        xq_lo = sem("xq_lo")
        b_proj = sem("b_proj")
        b_raw = sem("b_raw")
        b_sq = sem("b_sq")
        b_ss = sem("b_ss")
        b_clamped = sem("b_clamped")
        b_rn = sem("b_rn")
        b_rns = sem("b_rns")
        b_fan = sem("b_fan")
        b_norm = sem("b_norm")
        b_nhi = sem("b_nhi")
        b_nlo = sem("b_nlo")
        vb_proj = sem("vb_proj")
        vb_hi = sem("vb_hi")
        vb_lo = sem("vb_lo")
        b_filled = sem("b_filled")
        b_read = sem("b_read")
        b_biased = sem("b_biased")
        b_exp = sem("b_exp")
        b_turned = sem("b_turned")
        b_pthi = sem("b_pthi")
        b_ptlo = sem("b_ptlo")
        b_pv = sem("b_pv")
        b_nt = sem("b_nt")
        b_nexp = sem("b_nexp")
        b_nhi2 = sem("b_nhi2")
        b_out = sem("b_out")
        b_normed = sem("b_normed")
        b_added = sem("b_added")
        b_spread = [sem(f"b_spread{j}") for j in range(2)]

        class Stream:
            def __init__(self, name, space, banks):
                def own(part):
                    return sem(f"{name}_{part}")
                self.stats = sb(f"{name}_stats", [P, T, 6])
                self.mv = sb(f"{name}_mv", [P, T, 2])
                self.lnv = sb(f"{name}_lnv", [P, T])
                self.rstd = sb(f"{name}_rstd", [P, T])
                self.xn = sb(f"{name}_xn", [P, T, D])
                self.mixed = space[:, 0:2 * S].rearrange("p (k s) -> p k s", k=2)
                self.prev, self.kr, self.ka, self.ez = [space[:, j * S:(j + 1) * S] for j in range(2, 6)]
                self.xt = space[:, 6 * S:7 * S + 1]
                self.gate, self.gv = self.kr, self.prev
                self.banks = banks
                self.var_ready = own("var_ready")
                self.rstd_ready = own("rstd_ready")
                self.ln_ready = own("ln_ready")
                self.turned = own("turned")
                self.f_xt = own("f_xt")
                self.f_mixed = own("f_mixed")
                self.f_k = own("f_k")
                self.f_r = own("f_r")
                self.f_relu = own("f_relu")
                self.f_e = own("f_e")
                self.f_e1 = own("f_e1")
                self.f_gate = own("f_gate")
                self.f_ka = own("f_ka")
                self.f_v = own("f_v")
                self.f_done = own("f_done")

        FR = Stream("front", front_space, [SA, TA, OA])
        BK = Stream("back", scratch, [SC, TR[0], TR[1]])
        last_sem = BK.f_done
        xh_a, xl_a = [FR.xn[:].rearrange("p t d -> p (t d)").bitcast(F16)[:, j * S:(j + 1) * S] for j in range(2)]
        xqh, xql = [BK.xn[:].rearrange("p t d -> p (t d)").bitcast(F16)[:, j * S:(j + 1) * S] for j in range(2)]

        def slots_a():
            slots = []
            for i in range(T):
                units = [("unit", k) for k in range(upto(UNITS_A, i - 1), upto(UNITS_A, i))]
                if i >= 2:
                    slots.append(("glob", i))
                if i >= 3:
                    slots.insert(len(slots) - 1, ("turn_glob", i - 1))
                if i >= 1:
                    units = units[0:3] + [("turn_out", i - 1)] + units[3:4] + [("y", i - 1)] + units[4:]
                slots += units
            return slots + [("turn_glob", T - 1), None, None, ("turn_out", T - 1), ("y", T - 1)]

        def slots_b():
            slots = []
            for i in range(T):
                u = [("unit", k) for k in range(upto(UNITS_B, i - 1), upto(UNITS_B, i))]
                slots.append(("null", i))
                if i >= 1:
                    u = (u[0:1] + [("turn_null", i - 1)] + u[1:4] + [("turn_out", (i - 1, 0))] + u[4:5] +
                         [("turn_out", (i - 1, 1))] + u[5:6] + [("y", i - 1)] + u[6:])
                slots += u
            return slots + [None, None, ("turn_null", T - 1), None, None, None,
                            ("turn_out", (T - 1, 0)), ("turn_out", (T - 1, 1)), ("y", T - 1)]

        SLOTS_A, SLOTS_B = slots_a(), slots_b()

        def filled(slots, what):
            return sum(s is not None for s in slots[:slots.index(what) + 1])

        def misc(slots, what):
            return sum(s is not None and s[0] not in ("unit", "y") for s in slots[:slots.index(what) + 1])

        def read_before(slots, n, unit_read, y_read, misc_read):
            for kind, arg in reversed([s for s in slots[:n] if s is not None]):
                if kind == "unit":
                    return unit_read, arg + 1
                if kind == "y":
                    return y_read, arg + 1
                return misc_read, misc(slots, (kind, arg))
            return misc_read, 0

        def at(slots, n):
            return slots[n] if 0 <= n < len(slots) and slots[n] is not None else (None, 0)

        def unit(slots, n):
            kind, u = at(slots, n)
            return u if kind == "unit" else None

        A0 = 17
        AM = A0 + 3 * len(SLOTS_A)
        NF = AM + 11
        K0, V0, FK0, Q0 = 6, 14, 18, 25
        GAP = 6
        FQ0 = Q0 + 11
        B0 = FQ0 + 5 + GAP
        BM = B0 + len(SLOTS_B)
        NB = BM + 11

        def weight_front(n):
            if n < 6:
                return 0.88
            if n < A0:
                return 1.20
            if n >= AM:
                return 1.40
            kind, arg = at(SLOTS_A, (n - A0) // 3)
            if kind == "unit":
                return 0.90
            return 0.60

        def weight_back(n):
            if n < K0:
                return 1.10
            if n < V0:
                return 1.50
            if n < Q0:
                return 0.75
            if n < Q0 + 8:
                return 1.90
            if n < FQ0:
                return 1.20
            if n < B0:
                return 2.00
            if n >= BM:
                return 1.50
            kind, arg = at(SLOTS_B, n - B0)
            if kind == "unit":
                return (1.90, 1.60, 0.84, 1.45)[UNITS_B[arg][0]]
            return {"null": 1.50, "turn_null": 0.72, "turn_out": 1.20, "y": 2.50}.get(kind, 1.20)

        def placed(steps, weight):
            total, so_far, places = sum(weight(n) for n in steps), 0, []
            for n in steps:
                places.append((n, (so_far + weight(n) / 2) / total))
                so_far += weight(n)
            return places

        FRONT = list(range(A0, NF)) + list(range(A0))
        BACK_ENDS = 0.980
        MERGED = sorted([(p, 1, n) for n, p in placed(FRONT, weight_front)] +
                        [(BACK_ENDS * p, 0, n) for n, p in placed(range(NB), weight_back)])
        PROJECT_ONLY = [(1, n) for n in range(A0)]
        FRONT_ONLY = [(1, n) for n in FRONT]
        BACK_ONLY = [(0, n) for n in range(NB)]
        BOTH = [(f, n) for _, f, n in MERGED]

        def spread(pair):
            m = pair // 2 + 1
            return b_spread[pair % 2], 16 * (8 * min(m, 2) + 4 * max(m - 2, 0))

        def copy(o, i, **kw):
            return nc.scalar.activation(o, i, ACT.Copy, **kw)

        def product(o, ah, al, bh, bl, first=True, last=True):
            nc.tensor.matmul(o, ah, bh, start=first, stop=False, skip_group_check=True)
            nc.tensor.matmul(o, al, bh, start=False, stop=False, skip_group_check=True)
            return nc.tensor.matmul(o, ah, bl, start=False, stop=last, skip_group_check=True)

        class Order:
            def __init__(self, eng, s):
                self.eng, self.s, self.n = eng, s, 0

            def done(self, ins):
                ins.then_inc(self.s, 1)
                self.n += 1
                self.eng.wait_ge(self.s, self.n)

        with nc.Block() as block:
            @block.sync
            def _(sp):
                def load(dst, src):
                    sp.dma_start(dst, src).then_inc(w_loaded, 16)
                sp.dma_start(x_in[:], x[0].rearrange("(t p) d -> p t d", p=P)).then_inc(x_first, 16)
                load(wa_sb[:], a_wqkv)
                load(wproj[:], a_wproj)
                load(wst[:, 0:1024], b_wq)
                load(wout[:], b_wout.rearrange("(c p) n -> p c n", p=P))
                load(wfn[:, 0, :], f_wr)
                load(wfn[:, 1, :], f_wk)
                load(wfn[:, 2, :], f_wv)
                for c, v in ((0, b_g), (1, b_b), (4, f_mur), (5, f_muk)):
                    load(cols[:, c:c + 1], v.rearrange("(p o) -> p o", o=1))
                for c, v in ((2, b_qs), (3, b_ks)):
                    for half in range(2):
                        load(cols[half * DB:half * DB + DB, c:c + 1], v.rearrange("(p o) -> p o", o=1))
                null = b_nullkv.rearrange("h (n c) d -> n h c d", c=2)
                for n in range(NN):
                    load(nk_sb[n * H:(n + 1) * H, :, :], null[n])
                sp.dma_start(wst_kv[:], b_wkv).then_inc(w_staged, 16)

            @block.gpsimd
            def _(pool):
                g = nc.gpsimd
                n = [0]

                def done(ins):
                    ins.then_inc(pool_setup, 1)
                    n[0] += 1
                    pool.wait_ge(pool_setup, n[0])

                done(g.memset(ident[:], 0.0))
                g.affine_select(out=ident[:], in_=ident[:], compare_op=ALU.not_equal, fill=1.0,
                                base=0, pattern=[[-1, P]], channel_multiplier=1).then_inc(ident_ready, 1)
                done(g.memset(mask_a[:], 0.0))
                done(g.affine_select(out=mask_a[:, 0:P], in_=mask_a[:, 0:P], compare_op=ALU.is_gt,
                                     fill=MASKED, base=0, pattern=[[1, P]], channel_multiplier=-1))
                done(g.affine_select(out=mask_a[:, P:2 * P], in_=mask_a[:, P:2 * P], compare_op=ALU.is_ge,
                                     fill=MASKED, base=0, pattern=[[-1, P]], channel_multiplier=1))
                for k in range(0, P, STRIDE):
                    done(g.memset(mask_a[:, k:k + 1], 0.0))
                done(g.iota(dist_i[:], pattern=[[-1, S]], base=S - P, channel_multiplier=1))
                done(g.iota(null_i[:], pattern=[[P, T], [-1, NN]], base=NN, channel_multiplier=1))
                g.iota(rowi[:], pattern=[[0, 4]], base=0, channel_multiplier=1).then_inc(iotas_ready, 1)
                done(g.memset(head_sum[:], 0.0))
                for j in range(2):
                    done(g.memset(head_sum[j * DB:j * DB + DB, H - 2 + j:96 + H - 2:H], 1.0))
                pool.wait_ge(alibi_ready, 1)
                g.affine_select(out=alibi[:, :, S - P:S], in_=alibi[:, :, S - P:S], compare_op=ALU.is_ge, fill=MASKED,
                                base=0, pattern=[[0, H], [-1, P]], channel_multiplier=1).then_inc(pool_ready, 1)

            @block.tensor
            def _(pe):
                pe.wait_ge(ident_ready, 1)
                pe.wait_ge(w_loaded, 16 * WLOADS)
                for k in range(3):
                    ins = pe.transpose(SA[:, k * D:(k + 1) * D], wfn[:, k, :], ident[:])
                ins.then_inc(mix_turned, 1)
                pe.wait_ge(nulls_scaled, 1)
                pe.transpose(TA[:, 0:NN * H], nkd[:], ident[0:NN * H, 0:NN * H]).then_inc(nulls_turned, 1)
                pe.wait_ge(vec_ready, 1)
                pe.wait_ge(act_ready, 1)
                pe.wait_ge(pool_ready, 1)

            @block.scalar
            def _(act):
                n = [0]

                def done(ins):
                    ins.then_inc(act_setup, 1)
                    n[0] += 1
                    act.wait_ge(act_setup, n[0])
                act.preload_act_table_set("natural_log_exp_and_others")
                act.wait_ge(w_loaded, 16 * WLOADS)
                copy(wavh[:], wa_sb[:, 2 * D:3 * D], scale=WS).then_inc(wav_hi, 1)
                copy(wbh[:, 0, :], wst[:, 0:1024], scale=WS).then_inc(wq_hi, 1)
                act.wait_ge(null_ss, 1)
                done(act.activation(nks[:, 2:3], nks[:, 1:2], ACT.Ln, scale=2.0 ** 20))
                act.activation(nks[:, 3:4], nks[:, 2:3], ACT.Exp, scale=-0.5, bias=epsb[0:NN * H, 2:3]).then_inc(null_root, 1)
                copy(nvh[:], nk_sb[:, 1, :], scale=WS).then_inc(nv_hi, 1)
                act.wait_ge(w_staged, 16)
                copy(wbh[:, 1:3, :].rearrange("p k n -> p (k n)"), wst_kv[:], scale=WS).then_inc(act_ready, 1)
                act.wait_ge(vec_ready, 1)

            @block.vector
            def _(v):
                n = [0]

                def done(ins):
                    ins.then_inc(vec_setup, 1)
                    n[0] += 1
                    v.wait_ge(vec_setup, n[0])

                v.wait_ge(iotas_ready, 1)
                done(v.tensor_copy(dist[:], dist_i[:]))
                for h in range(H):
                    ins = v.tensor_scalar(alibi[:, h, :], dist[:], slopes[h], None, ALU.mult)
                ins.then_inc(alibi_ready, 1)
                done(v.tensor_copy(null_f[:], null_i[:]))
                for h in range(H):
                    ins = v.tensor_scalar(alibi_null[:, :, :, h], null_f[:], slopes[h], None, ALU.mult)
                done(ins)
                for c, sh in ((0, 3), (1, 4), (2, 4), (3, 5)):
                    done(v.tensor_scalar(rowi[:, c:c + 1], rowi[:, c:c + 1], sh, None, ALU.logical_shift_right))
                done(v.tensor_scalar(rowi[:, 0:2], rowi[:, 0:2], 1, None, ALU.bitwise_and))
                done(v.tensor_copy(lo_rows[:], rowi[:, 0:3]))
                done(v.tensor_copy(head_rows[:, GR - 1:GR], rowi[:, 3:4]))
                for r in range(GR):
                    done(v.tensor_scalar(head_rows[:, r:r + 1], head_rows[:, GR - 1:GR], float(r), None, ALU.is_equal))
                done(v.tensor_scalar(lo_rows[:, 2:3], lo_rows[:, 2:3], 1.0, None, ALU.is_equal))
                done(v.tensor_scalar(lo_rows[:], lo_rows[:], -1.0, None, ALU.mult))
                v.memset(epsb[:, 0:1], EPS)
                v.memset(epsb[:, 1:2], math.log(1024.0) + 0.5 * math.log(256.0))
                done(v.memset(epsb[:, 2:4], 0.5 * math.log(2.0 ** 20)))
                v.wait_ge(ident_ready, 1)
                done(v.tensor_copy(identb[:], ident[:]))
                done(v.tensor_scalar(blk[:], ident[:, 0:H], WS, None, ALU.mult))
                for r in range(1, 8):
                    done(v.scalar_tensor_tensor(out=blk[:], in0=ident[:, r * H:(r + 1) * H], scalar=WS, in1=blk[:],
                                                op0=ALU.mult, op1=ALU.add))
                done(v.tensor_scalar(fan_row[:, 0, :], blk[:], 1.0 / WS / 1024.0, None, ALU.mult))
                done(v.memset(head_fan[:], 0.0))
                for b in range(8):
                    done(v.tensor_copy(head_fan[0:32, b, :].rearrange("p (j d) -> p j d", j=2),
                                       fan_row[0:32, 0, 2 * b:2 * b + 2].unsqueeze(2).broadcast_to([32, 2, DB])))
                for tile, c in ((vah, WS), (val, 0.0)):
                    v.memset(tile[:, :, :, DA:DA + 1], c)
                v.memset(vgl[:, :, DA:DA + 1], 0.0)
                done(v.tensor_copy(vgh[:, :, DA:DA + 1], blk[0:NG * H, :].unsqueeze(2)))
                v.wait_ge(w_loaded, 16 * WLOADS)
                done(v.tensor_tensor(nkd[:, 0:DB], nk_sb[:, 0, :], nk_sb[:, 0, :], ALU.mult))
                done(v.tensor_reduce(nks[:, 0:1], nkd[:, 0:DB], AX.X, ALU.add))
                v.tensor_scalar(nks[:, 1:2], nks[:, 0:1], 1e-24, None, ALU.max).then_inc(null_ss, 1)
                for kind, sc in ((0, -WS), (1, WS)):
                    w = wa_sb[:, kind * D:(kind + 1) * D].rearrange("p (h d) -> p h d", d=DA)
                    for r in range(REPS):
                        ins = v.tensor_scalar(wa4[:, kind, :, r, :], w, sc, None, ALU.mult)
                done(ins)
                wv = wa4[:].rearrange("p k h r d -> p (k h r d)")
                whv = wa4h[:].rearrange("p k g c -> p (k g c)")
                wlv = wa4l[:].rearrange("p k g c -> p (k g c)")
                done(v.tensor_copy(whv, wv))
                done(v.tensor_tensor(wlv, wv, whv, ALU.subtract))
                done(v.tensor_scalar(wout[:], wout[:], 1.0 / WS, None, ALU.mult))
                done(v.tensor_scalar(colx[:, 0:1], cols[:, 2:3], -8.0, None, ALU.mult))
                done(v.tensor_scalar(colx[:, 1:3], cols[:, 4:6], -1.0, 1.0, ALU.mult, ALU.add))
                v.wait_ge(wav_hi, 1)
                done(v.scalar_tensor_tensor(out=wavl[:], in0=wa_sb[:, 2 * D:3 * D], scalar=WS, in1=wavh[:],
                                            op0=ALU.mult, op1=ALU.subtract))
                v.wait_ge(wq_hi, 1)
                v.scalar_tensor_tensor(out=wbl[:, 0, :], in0=wst[:, 0:1024], scalar=WS, in1=wbh[:, 0, :],
                                       op0=ALU.mult, op1=ALU.subtract)
                v.wait_ge(null_root, 1)
                for half in range(2):
                    ins = v.tensor_scalar(nkd[:, half * DB:(half + 1) * DB], nk_sb[:, 0, :], nks[:, 3:4], None, ALU.mult)
                ins.then_inc(nulls_scaled, 1)
                v.wait_ge(nv_hi, 1)
                done(v.scalar_tensor_tensor(out=nvl[:], in0=nk_sb[:, 1, :], scalar=WS, in1=nvh[:],
                                            op0=ALU.mult, op1=ALU.subtract))
                b1 = fan_row[0:NN * H, 1, :]
                done(v.tensor_scalar(b1, blk[0:NN * H, :], 1.0 / WS, None, ALU.mult))
                bb = b1.unsqueeze(2).broadcast_to([NN * H, H, DB])
                done(v.tensor_tensor(nvbh[:, :, 0:DB], nvh[:].unsqueeze(1).broadcast_to([NN * H, H, DB]), bb, ALU.mult))
                done(v.tensor_tensor(nvbl[:, :, 0:DB], nvl[:].unsqueeze(1).broadcast_to([NN * H, H, DB]), bb, ALU.mult))
                v.wait_ge(mix_turned, 1)
                done(v.tensor_copy(wft[:].rearrange("p k d -> p (k d)"), SA[:, 0:3 * D]))
                v.wait_ge(nulls_turned, 1)
                done(v.tensor_scalar(nkf[:], TA[:, 0:NN * H], cols[:, 3:4], None, ALU.mult))
                done(v.tensor_copy(nkh[:], nkf[:]))
                done(v.tensor_tensor(nkl[:], nkf[:], nkh[:], ALU.subtract))
                v.wait_ge(act_ready, 1)
                v.scalar_tensor_tensor(out=wbl[:, 1:3, :].rearrange("p k n -> p (k n)"), in0=wst_kv[:], scalar=WS,
                                       in1=wbh[:, 1:3, :].rearrange("p k n -> p (k n)"),
                                       op0=ALU.mult, op1=ALU.subtract).then_inc(vec_ready, 1)
                v.wait_ge(pool_ready, 1)

        def streams(order, seq, load=None):
            has_back = any(not f for f, _ in order)
            has_attention = (1, A0) in order
            before = 1 if has_attention else 0

            def run(front, back):
                for f, n in order:
                    if f:
                        front(n)
                    else:
                        back(n)

            with nc.Block() as block:
                @block.sync
                def _(sp):

                    def front(n):
                        if n == AM:
                            sp.wait_ge(a_added, T)
                            sp.dma_start(x_in[:], load.rearrange("(t p) d -> p t d", p=P)).then_inc(x_loaded, 16)

                    def back(n):
                        for kind in range(2):
                            for pair in range(4):
                                if n != (FK0 + 3 + 2 * pair + 2 * (pair >= 2), FQ0 + 2 + pair)[kind]:
                                    continue
                                m = kind * 8 + 2 * pair + 2
                                sp.wait_ge(b_nhi, m)
                                sp.wait_ge(b_nlo, m)
                                for j in range(2):
                                    for (src, tile, half) in (((nh, qst, 0), (nl, qst, 1)) if kind else
                                                              ((nh, kh, 0), (nh, kh, 1), (nl, kl, 0), (nl, kl, 1))):
                                        sp.dma_start(
                                            tile[half * DB:half * DB + DB, 4 * pair + j:4 * pair + j + 3:2, :],
                                            src[j * DB:j * DB + DB, pair % 2, :, :]).then_inc(b_spread[pair % 2], 16)
                        if n == NB - 1:
                            sp.wait_ge(BK.f_done, 1)
                            sp.dma_start(out[seq].rearrange("(t p) d -> p t d", p=P), x_b[:]).then_inc(x_stored, 16)

                    run(front, back)
                    if has_back:
                        sp.wait_ge(x_stored, 16)

                @block.gpsimd
                def _(pool):

                    def front(n):
                        for i in range(1, T):
                            for r in range(GR):
                                if n != (A0 + 3 * SLOTS_A.index(("unit", upto(UNITS_A, i - 2))) + 2 * r):
                                    continue
                                if i >= 2:
                                    pool.wait_ge(a_filled, filled(SLOTS_A, ("unit", upto(UNITS_A, i - 2) - 1)))
                                nc.gpsimd.tensor_tensor(qm[:, i % 2, r:H:GR, :], qa4[:, :, i * P:(i + 1) * P],
                                                        head_rows[:, r:r + 1].unsqueeze(2).broadcast_to([P, GR, P]),
                                                        ALU.mult).then_inc(a_masked, 1)

                    def back(n):
                        for a in range(16):
                            if n == (FK0 + 2 + a + 2 * (a >= 4) if a < 8 else FQ0 + 1 + (a - 8) // 2):
                                pool.wait_ge(b_nhi, a + 1)
                                if a >= 4:
                                    pool.wait_ge(*spread(a // 2 - 2))
                                nc.gpsimd.tensor_tensor(nl[:, (a // 2) % 2, a % 2, :], raw[:, a % 8, :],
                                                        nh[:, (a // 2) % 2, a % 2, :], ALU.subtract).then_inc(b_nlo, 1)

                    run(front, back)

                @block.tensor
                def _(pe):

                    def turn_x(st, k, src, dst):
                        pe.wait_ge(st.ln_ready, k)
                        for t in range(T):
                            ins = pe.transpose(dst[:, t * P:(t + 1) * P], src[:, t, :], ident[:])
                        ins.then_inc(st.turned, 1)

                    def mix(st, k, n):
                        b0, b1, b2 = st.banks
                        if n == 3:
                            turn_x(st, k, st.xn, b0)
                        if n == 6:
                            pe.wait_ge(st.f_mixed, 1)
                            pe.matmul(b1[:], wft[:, 1, :], st.mixed[:, 1, :], start=True, stop=True).then_inc(st.f_k, 1)
                            pe.wait_ge(st.f_mixed, 2)
                            for t in range(T):
                                ins = pe.matmul(b2[:, t * P:(t + 1) * P], st.mixed[:, 0, t * P:(t + 1) * P], wft[:, 0, :],
                                                start=True, stop=True)
                            ins.then_inc(st.f_r, 1)
                        if n == 9:
                            pe.wait_ge(st.f_ka, 1)
                            for t in range(T):
                                ins = pe.matmul(b0[:, t * P:(t + 1) * P], st.ka[:, t * P:(t + 1) * P], wft[:, 2, :],
                                                start=True, stop=True)
                            ins.then_inc(st.f_v, 1)

                    def a_sc(u):
                        i, h0, nh = UNITS_A[u]
                        w = min(i + 1, 2) * P
                        if h0 == 0 and i >= 1:
                            pe.wait_ge(a_masked, GR * i)
                        pe.matmul(SA[:, 0:nh * w], identb[:], mask_a[:, 2 * P - w:2 * P].unsqueeze(1).broadcast_to([P, nh, w]),
                                  start=True, stop=False, skip_group_check=True)
                        for j in range(nh):
                            ins = pe.matmul(SA[:, j * w:(j + 1) * w], qm[:, i % 2, h0 + j, :],
                                            ka4[:, (h0 + j) // GR, (i + 1) * P - w:(i + 1) * P], start=False, stop=True,
                                            skip_group_check=True)
                        return ins

                    def a_glob(i):
                        ng = 2 * (i - 1)
                        v = SA[:, 0:ng * H].rearrange("p (g h) -> p g h", h=H)
                        pe.wait_ge(a_masked, GR * i)
                        for h in range(H):
                            ins = pe.matmul(v[:, :, h], qm[:, i % 2, h, :], ka4[:, h // GR, 0:ng * STRIDE:STRIDE],
                                            start=True, stop=True)
                        return ins

                    def a_turn(u):
                        pe.wait_ge(a_exp, u + 1)
                        if u > 0:
                            pe.wait_ge(a_ptlo, u)
                        for c in range(UNITS_A[u][2] * min(UNITS_A[u][0] + 1, 2)):
                            ins = pe.transpose(TA[:, c * P:(c + 1) * P], prob_a[:, c * P:(c + 1) * P], ident[:])
                        ins.then_inc(a_turned, 1)

                    def a_pvs(u):
                        i, h0, nh = UNITS_A[u]
                        nk = min(i + 1, 2)
                        pe.wait_ge(a_ptlo, u + 1)
                        if h0 == 0:
                            if i > 0:
                                pe.wait_ge(a_normed, i)
                        for j in range(nh):
                            h = h0 + j
                            o = OA[:, h * (DA + 1):(h + 1) * (DA + 1)]
                            for c in range(nk):
                                kt = i + 1 - nk + c
                                s = slice((j * nk + c) * P, (j * nk + c + 1) * P)
                                ins = product(o, pth_a[:, u % 2, s], ptl_a[:, u % 2, s], vah[:, kt, h, :], val[:, kt, h, :],
                                              first=(h == 0 and c == 0))
                        ins.then_inc(a_pv, 1)
                        if h0 + nh == H and i >= 2:
                            pe.wait_ge(a_read, misc(SLOTS_A, ("turn_glob", i)))
                            v = slice(0, 2 * (i - 1) * H)
                            product(OA[:, 0:H * (DA + 1)], pgh[v, :], pgl[v, :], vgh[v, :, :].rearrange("p h d -> p (h d)"),
                                    vgl[v, :, :].rearrange("p h d -> p (h d)"), first=False).then_inc(a_out, 1)

                    def front(n):
                        if n == 3:
                            turn_x(FR, 1 + 2 * before, FR.xn, SA)
                        if 6 <= n < 14:
                            a = n - 6
                            kind, grp = 1 - a // 4, a % 4
                            pe.wait_ge(xl_ready, 1)
                            if a > 1:
                                pe.wait_ge(a_stacked, a - 1)
                            product(PROJ_A[a % 2][:], wa4h[:, kind, grp, :], wa4l[:, kind, grp, :], xh_a[:], xl_a[:]
                                    ).then_inc(a_proj, 1)
                        if n == 14:
                            for t in range(T):
                                s = slice(t * P, (t + 1) * P)
                                ins = product(SA[:, s], xh_a[:, s], xl_a[:, s], wavh[:], wavl[:])
                            ins.then_inc(va_proj, 1)
                        if n == 15:
                            pe.wait_ge(xg_ready, 1)
                            pe.wait_ge(a_stacked, 8)
                            product(OA[0:NG * H, 0:D], xg[:, 0, :], xg[:, 1, :], wavh[:], wavl[:]).then_inc(vg_proj, 1)
                        if A0 <= n < AM:
                            slot, sub = (n - A0) // 3, (n - A0) % 3
                            kind, arg = at(SLOTS_A, slot) if sub == 0 else (None, 0)
                            if kind is not None:
                                if slot > 0:
                                    pe.wait_ge(*read_before(SLOTS_A, slot, a_exp, a_added, a_read))
                            if kind == "unit":
                                ins = a_sc(arg)
                            if kind == "glob":
                                ins = a_glob(arg)
                            if kind == "turn_glob":
                                ng = 2 * (arg - 1)
                                pe.wait_ge(a_gexp, arg - 1)
                                ins = pe.transpose(SA[0:ng * H, 0:P], pg[:, 0:ng * H], ident[:])
                            if kind == "turn_out":
                                pe.wait_ge(a_normed, arg + 1)
                                ins = pe.transpose(SA[:, 0:P], oa[:], ident[:])
                            if kind == "y":
                                pe.wait_ge(a_read, misc(SLOTS_A, ("turn_out", arg)))
                                ins = pe.matmul(SA[:, 0:D], oat[:], wproj[:], start=True, stop=True)
                            if kind is not None:
                                ins.then_inc(a_filled, 1)
                            u = unit(SLOTS_A, slot - 2)
                            if sub == 1 and u is not None:
                                a_pvs(u)
                            u = unit(SLOTS_A, slot)
                            if sub == 2 and u is not None:
                                a_turn(u)
                        if n >= AM:
                            mix(FR, 1, n - AM)

                    def b_proj_free(j):
                        j -= 3
                        if j >= 16:
                            pe.wait_ge(b_raw, j - 8 + 1)
                        elif j >= 8:
                            pe.wait_ge(vb_lo, j - 8 + 1)
                        elif j >= 0:
                            pe.wait_ge(b_raw, j + 1)

                    def b_ssq(a):
                        pe.wait_ge(b_sq, a + 1)
                        if a == 8:
                            pe.wait_ge(b_norm, 7)
                        pe.matmul(OB[0][0:96, :], head_sum[:, H - 2 - 2 * (a % 8):H - 2 - 2 * (a % 8) + 96], sq[:, a % 2, :], start=(a % 8 == 0),
                                  stop=(a % 8 == 7)).then_inc(b_ss, 1)

                    def b_qk(a):
                        kind, b = 1 - a // 8, a % 8
                        j = a if kind else a + 8
                        b_proj_free(j)
                        xs = (xh_b, xl_b) if kind else (xqh, xql)
                        product(PROJ_B[j % 3][:], wbh[:, kind, b * P:(b + 1) * P], wbl[:, kind, b * P:(b + 1) * P],
                                xs[0][:], xs[1][:]).then_inc(b_proj, 1)

                    def b_v(a):
                        b_proj_free(a + 8)
                        t, s = a // 2, slice(a % 2 * 512, a % 2 * 512 + 512)
                        product(PROJ_B[(a + 8) % 3][:], xh_b[:, t * P:(t + 1) * P], xl_b[:, t * P:(t + 1) * P],
                                wbh[:, 2, s], wbl[:, 2, s]).then_inc(vb_proj, 1)

                    def b_fans(a):
                        pe.wait_ge(b_rns, a // 8 + 1)
                        if a > 1:
                            pe.wait_ge(b_norm, a - 1)
                        if a % 8 == 0:
                            pe.wait_ge(b_clamped, a // 8 + 1)
                        pe.matmul(OB[a % 2][:], head_fan[:, a % 8, :], rns[:], start=True, stop=True
                                  ).then_inc(b_fan, 1)

                    def b_nullsc(i):
                        for h in range(H):
                            o = SC[:, h:h + H + 1:H]
                            q = qst[:, h, i * P:(i + 1) * P]
                            pe.matmul(o, q, nkh[:, h:h + H + 1:H], start=True, stop=False, skip_group_check=True)
                            ins = pe.matmul(o, q, nkl[:, h:h + H + 1:H], start=False, stop=True, skip_group_check=True)
                        return ins

                    def b_sc(u):
                        i, h0, nh = UNITS_B[u]
                        w = (i + 1) * P
                        for j in range(nh):
                            q = qst[:, h0 + j, i * P:(i + 1) * P]
                            o = SC[:, j * w:(j + 1) * w]
                            pe.matmul(o, q, kh[:, h0 + j, 0:w], start=True, stop=False, skip_group_check=True)
                            ins = pe.matmul(o, q, kl[:, h0 + j, 0:w], start=False, stop=True, skip_group_check=True)
                        return ins

                    def b_turn(u):
                        i, h0, nh = UNITS_B[u]
                        pe.wait_ge(b_exp, u + 1)
                        if u > 1:
                            pe.wait_ge(b_ptlo, u - 1)
                        for c in range(nh * (i + 1)):
                            ins = pe.transpose(TR[u % 2][:, c * P:(c + 1) * P], prob[:, u % 2, c * P:(c + 1) * P], ident[:])
                        ins.then_inc(b_turned, 1)

                    def b_pvs(u):
                        i, h0, nh = UNITS_B[u]
                        k = h0 // OBH
                        pe.wait_ge(b_ptlo, u + 1)
                        if h0 % OBH == 0:
                            if i >= 1:
                                pe.wait_ge(b_normed, 2 * (i - 1) + k + 1)
                            else:
                                pe.wait_ge(b_norm, 16)
                        for j in range(nh):
                            h = h0 + j
                            o = OB[k][:, (h % OBH) * DB:(h % OBH + 1) * DB]
                            for c in range(i + 1):
                                s = slice((j * (i + 1) + c) * P, (j * (i + 1) + c + 1) * P)
                                ins = product(o, pth[:, u % 3, s], ptl[:, u % 3, s], vbh[:, c, h, :], vbl[:, c, h, :],
                                              first=(h % OBH == 0 and c == 0))
                        ins.then_inc(b_pv, 1)
                        if h0 + nh == H:
                            pe.wait_ge(b_read, misc(SLOTS_B, ("turn_null", i)))
                            for k in range(2):
                                hs = slice(k * OBH, (k + 1) * OBH)
                                product(OB[k][:], pnh[:], pnl[:], nvbh[:, hs, :].rearrange("p h d -> p (h d)"),
                                        nvbl[:, hs, :].rearrange("p h d -> p (h d)"), first=False).then_inc(b_out, 1)

                    def back(n):
                        if n == 3:
                            turn_x(BK, 1, BK.xn, TR[0])
                        if K0 <= n < K0 + 8:
                            if n == K0:
                                pe.wait_ge(b_xl, 1)
                            if n == K0 + 2:
                                pe.wait_ge(xq_hi, 1)
                            b_qk(n - K0)
                        if n == 6:
                            turn_x(BK, 2, xn2, TR[1])
                        if K0 < n <= K0 + 8:
                            b_ssq(n - K0 - 1)
                        if V0 <= n < V0 + 8:
                            b_v(n - V0)
                        if FK0 <= n < FK0 + 8:
                            b_fans(n - FK0)
                        if Q0 <= n < Q0 + 8:
                            if n == Q0:
                                pe.wait_ge(xq_lo, 1)
                            b_qk(8 + n - Q0)
                        if Q0 < n <= Q0 + 8:
                            b_ssq(8 + n - Q0 - 1)
                        if FQ0 <= n < FQ0 + 4:
                            b_fans(8 + 2 * (n - FQ0))
                            b_fans(8 + 2 * (n - FQ0) + 1)
                        if n == B0:
                            pe.wait_ge(b_raw, 16)
                            pe.wait_ge(vb_lo, 2 * T)
                            pe.wait_ge(*spread(6))
                            pe.wait_ge(*spread(7))
                        if B0 <= n < BM:
                            slot = n - B0
                            kind, arg = at(SLOTS_B, slot)
                            if kind is not None:
                                if slot > 0:
                                    pe.wait_ge(*read_before(SLOTS_B, slot, b_biased, b_added, b_read))
                            if kind == "unit":
                                ins = b_sc(arg)
                            if kind == "null":
                                ins = b_nullsc(arg)
                            if kind == "turn_null":
                                pe.wait_ge(b_nexp, arg + 1)
                                ins = pe.transpose(SC[0:NN * H, 0:P], pn[:], ident[:])
                            if kind == "turn_out":
                                i, j = arg
                                pe.wait_ge(b_normed, 2 * i + j + 1)
                                for c in range(4):
                                    ins = pe.transpose(SC[:, c * P:(c + 1) * P],
                                                       ob[:, 8 * j + 2 * c:8 * j + 2 * c + 2, :].rearrange("p h d -> p (h d)"),
                                                       ident[:])
                            if kind == "y":
                                pe.wait_ge(b_read, misc(SLOTS_B, ("turn_out", (arg, 1))))
                                for c in range(8):
                                    ins = pe.matmul(SC[:, 0:D], obt[:, c, :], wout[:, c, :], start=(c == 0), stop=(c == 7))
                            if kind is not None:
                                ins.then_inc(b_filled, 1)
                            u = unit(SLOTS_B, slot - 2)
                            if u is not None:
                                b_turn(u)
                            u = unit(SLOTS_B, slot - 4)
                            if u is not None:
                                b_pvs(u)
                        if n >= BM:
                            mix(BK, 3, n - BM)

                    run(front, back)

                @block.scalar
                def _(act):
                    order = Order(act, act_order)

                    def root(st, k):
                        act.wait_ge(st.var_ready, k)
                        order.done(act.activation(st.lnv[:], st.mv[:, :, 1], ACT.Ln, bias=epsb[:, 0:1]))
                        act.activation(st.rstd[:], st.lnv[:], ACT.Exp, scale=-0.5).then_inc(st.rstd_ready, 1)

                    def mix(st, k, n):
                        b0, b1, b2 = st.banks
                        if n == 1:
                            root(st, k)
                        if n == 4:
                            act.wait_ge(st.turned, k)
                            copy(st.xt[:, 1:1 + S], b0[:]).then_inc(st.f_xt, 1)
                        if n == 6:
                            act.wait_ge(st.f_k, 1)
                            act.activation(st.kr[:], b1[:], ACT.Relu).then_inc(st.f_relu, 1)
                            act.wait_ge(st.f_r, 1)
                            act.activation(st.ez[:], b2[:], ACT.Exp, scale=-1.0).then_inc(st.f_e, 1)
                        if n == 8:
                            act.wait_ge(st.f_e1, 1)
                            act.wait_ge(st.f_ka, 1)
                            order.done(act.activation(st.ez[:], st.ez[:], ACT.Ln))
                            act.activation(st.gate[:], st.ez[:], ACT.Exp, scale=-1.0).then_inc(st.f_gate, 1)

                    def front(n):
                        if n == 1:
                            root(FR, 1 + before)
                        if n == 4:
                            act.wait_ge(FR.turned, 1 + before)
                            copy(xh_a[:], SA[:]).then_inc(xh_ready, 1)
                        if 6 <= n < 14:
                            a = n - 6
                            act.wait_ge(a_proj, a + 1)
                            if a > 1:
                                act.wait_ge(a_stacked, a - 1)
                            copy(ht[:, a % 2, :], PROJ_A[a % 2][:]).then_inc(a_hi, 1)
                        if n == 13 and has_attention:
                            act.wait_ge(FR.f_done, 1)
                            if has_back:
                                act.wait_ge(b_added, T)
                            copy(x_f[:], x_next[:])
                        if n == 15:
                            act.wait_ge(va_proj, 1)
                            copy(vah[:, :, :, 0:DA].rearrange("p t h d -> p (t h) d"),
                                 SA[:].rearrange("p (t d) -> p t d", d=DA)).then_inc(va_hi, 1)
                        if A0 <= n < AM:
                            slot, sub = (n - A0) // 3, (n - A0) % 3
                            kind, arg = at(SLOTS_A, slot)
                            if sub == 0:
                                u = unit(SLOTS_A, slot - 1)
                                if u is not None:
                                    act.wait_ge(a_turned, u + 1)
                                    if u > 1:
                                        act.wait_ge(a_pv, u - 1)
                                    copy(pth_a[:, u % 2, :], TA[:]).then_inc(a_pthi, 1)
                            if sub == 1:
                                if kind == "turn_glob":
                                    ng = 2 * (arg - 1)
                                    act.wait_ge(a_filled, filled(SLOTS_A, (kind, arg)))
                                    if arg > 2:
                                        act.wait_ge(a_out, arg - 2)
                                    copy(pgh[0:ng * H, :], SA[0:ng * H, 0:P]).then_inc(a_ghi, 1)
                                if kind == "turn_out":
                                    act.wait_ge(a_filled, filled(SLOTS_A, (kind, arg)))
                                    copy(oat[:], SA[:, 0:P]).then_inc(a_read, 1)
                            if sub == 1 and kind == "unit":
                                i, h0, nh = UNITS_A[arg]
                                w = min(i + 1, 2) * P
                                act.wait_ge(a_bias, arg + 1)
                                if arg > 0:
                                    act.wait_ge(a_turned, arg)
                                for j in range(nh):
                                    s = slice(j * w, (j + 1) * w)
                                    ins = act.activation(prob_a[:, s], SA[:, s], ACT.Exp, scale=-C_A,
                                                         bias=abias[:, i % 2, h0 + j:h0 + j + 1])
                                ins.then_inc(a_exp, 1)
                                if h0 + nh == H and i >= 2:
                                    ng = 2 * (i - 1)
                                    act.wait_ge(a_gt, i - 1)
                                    act.activation(pg[:, 0:ng * H], gt[:, 0:ng * H], ACT.Exp).then_inc(a_gexp, 1)
                        if n >= AM:
                            mix(FR, 1, n - AM)

                    def b_root(kind):
                        act.wait_ge(b_clamped, kind + 1)
                        order.done(act.activation(rn[:], rn[:], ACT.Ln, scale=256.0))
                        act.activation(rn[:], rn[:], ACT.Exp, scale=-0.5, bias=epsb[0:96, 1:2]).then_inc(b_rn, 1)

                    def b_his(a):
                        act.wait_ge(b_norm, a + 1)
                        if a >= 4:
                            act.wait_ge(*spread(a // 2 - 2))
                        copy(nh[:, (a // 2) % 2, a % 2, :], raw[:, a % 8, :]).then_inc(b_nhi, 1)

                    def b_square(a):
                        j = a if a < 8 else a + 8
                        act.wait_ge(b_proj, a + 1)
                        if a > 1:
                            act.wait_ge(b_ss, a - 1)
                        act.activation(sq[:, a % 2, :], PROJ_B[j % 3][:], ACT.Square).then_inc(b_sq, 1)

                    def b_vhi(a):
                        t, hf = a // 2, a % 2
                        act.wait_ge(vb_proj, a + 1)
                        copy(vbh[:, t, 8 * hf:8 * hf + 8, :].rearrange("p h d -> p (h d)"),
                             PROJ_B[(a + 8) % 3][:]).then_inc(vb_hi, 1)

                    def back(n):
                        if n == 1:
                            root(BK, 1)
                        if n == 4:
                            root(BK, 2)
                            act.wait_ge(BK.turned, 1)
                            copy(xh_b[:], TR[0][:]).then_inc(b_xh, 1)
                        if n == 7:
                            act.wait_ge(BK.turned, 2)
                            order.done(act.activation(xq[:], TR[1][:], ACT.Identity, scale=cols[:, 0:1], bias=cols[:, 1:2]))
                            copy(xqh[:], xq[:]).then_inc(xq_hi, 1)
                        if K0 <= n < K0 + 8:
                            b_square(n - K0)
                        if n == V0 + 2:
                            b_root(0)
                        if V0 <= n < V0 + 8:
                            b_vhi(n - V0)
                        if FK0 + 1 < n <= FK0 + 11 and n not in (FK0 + 6, FK0 + 7):
                            b_his(n - FK0 - (2 if n < FK0 + 6 else 4))
                        if Q0 <= n < Q0 + 8:
                            b_square(8 + n - Q0)
                        if n == Q0 + 9:
                            b_root(1)
                        if FQ0 < n <= FQ0 + 4:
                            b_his(8 + 2 * (n - FQ0 - 1))
                            b_his(8 + 2 * (n - FQ0 - 1) + 1)
                        if B0 <= n < BM:
                            slot = n - B0
                            kind, arg = at(SLOTS_B, slot)
                            u = unit(SLOTS_B, slot - 3)
                            if u is not None:
                                w = UNITS_B[u][2] * (UNITS_B[u][0] + 1) * P
                                act.wait_ge(b_turned, u + 1)
                                if u > 2:
                                    act.wait_ge(b_pv, u - 2)
                                copy(pth[:, u % 3, 0:w], TR[u % 2][:, 0:w]).then_inc(b_pthi, 1)
                            if kind == "turn_null":
                                act.wait_ge(b_filled, filled(SLOTS_B, (kind, arg)))
                                if arg > 0:
                                    act.wait_ge(b_out, 2 * arg)
                                copy(pnh[:], SC[0:NN * H, 0:P]).then_inc(b_nhi2, 1)
                            if kind == "turn_out":
                                i, j = arg
                                act.wait_ge(b_filled, filled(SLOTS_B, (kind, arg)))
                                copy(obt[:, 4 * j:4 * j + 4, :].rearrange("p c q -> p (c q)"), SC[:]).then_inc(b_read, 1)
                            u = unit(SLOTS_B, slot - 1)
                            if u is not None:
                                i, h0, nh = UNITS_B[u]
                                w = (i + 1) * P
                                act.wait_ge(b_biased, u + 1)
                                if u > 1:
                                    act.wait_ge(b_turned, u - 1)
                                for j in range(nh):
                                    s, h = slice(j * w, (j + 1) * w), slice(h0 + j, h0 + j + 1)
                                    ins = act.activation(prob[:, u % 2, s], sbias[:, u % 2, s], ACT.Exp, scale=-1.0,
                                                         bias=bmin[:, i % 2, h], accum_out=bden[:, i % 2, h])
                                ins.then_inc(b_exp, 1)
                                if h0 + nh == H:
                                    act.wait_ge(b_nt, i + 1)
                                    if i > 0:
                                        act.wait_ge(b_normed, 2 * i)
                                    act.activation(pn[:], nt[:], ACT.Exp).then_inc(b_nexp, 1)
                        if n >= BM:
                            mix(BK, 3, n - BM)

                    run(front, back)

                @block.vector
                def _(v):
                    order = Order(v, vec_order)
                    done = order.done

                    def ln_stats(st, src):
                        for t in range(T):
                            ins = v.bn_stats(st.stats[:, t, :], src[:, t, :])
                        done(ins)
                        for t in range(T):
                            ins = v.bn_aggr(st.mv[:, t, :], st.stats[:, t, :])
                        ins.then_inc(st.var_ready, 1)

                    def ln_apply(st, k, src, dst):
                        v.wait_ge(st.var_ready, k)
                        v.wait_ge(st.rstd_ready, k)
                        for t in range(T):
                            ins = v.tensor_scalar(dst[:, t, :], src[:, t, :], st.mv[:, t, 0:1], st.rstd[:, t:t + 1],
                                                  ALU.subtract, ALU.mult)
                        ins.then_inc(st.ln_ready, 1)

                    def mix(st, k, n, src, dst):
                        b0, b1, b2 = st.banks
                        if n == 0:
                            ln_stats(st, src)
                        if n == 2:
                            ln_apply(st, k, src, st.xn)
                            v.memset(st.xt[:, 0:1], 0.0).then_inc(st.ln_ready, 1)
                        if n == 5:
                            v.wait_ge(st.f_xt, 1)
                            v.wait_ge(st.ln_ready, k + 1)
                            for j in (1, 0):
                                done(v.tensor_scalar(st.prev[:], st.xt[:, 0:S], colx[:, 1 + j:2 + j], None, ALU.mult))
                                v.scalar_tensor_tensor(out=st.mixed[:, j, :], in0=st.xt[:, 1:1 + S], scalar=cols[:, 4 + j:5 + j],
                                                       in1=st.prev[:], op0=ALU.mult, op1=ALU.add).then_inc(st.f_mixed, 1)
                                v.wait_ge(st.f_mixed, 2 - j)
                        if n == 7:
                            v.wait_ge(st.f_e, 1)
                            v.tensor_scalar(st.ez[:], st.ez[:], 1e18, 1.0, ALU.min, ALU.add).then_inc(st.f_e1, 1)
                            v.wait_ge(st.f_relu, 1)
                            v.scalar_tensor_tensor(out=st.ka[:], in0=b1[:], scalar=0.0, in1=st.kr[:],
                                                   op0=ALU.max, op1=ALU.mult).then_inc(st.f_ka, 1)
                        if n == 10:
                            v.wait_ge(st.f_gate, 1)
                            v.wait_ge(st.f_v, 1)
                            done(v.tensor_tensor(st.gv[:], b0[:], st.gate[:], ALU.mult))
                            dv, sv = dst[:].rearrange("p t d -> p (t d)"), src[:].rearrange("p t d -> p (t d)")
                            v.tensor_tensor(dv, st.gv[:], sv, ALU.add).then_inc(st.f_done, 1)

                    def a_min(u):
                        i, h0, nh = UNITS_A[u]
                        hs = slice(h0, h0 + nh)
                        v.wait_ge(a_filled, filled(SLOTS_A, ("unit", u)))
                        done(v.tensor_reduce(amin[:, hs], SA[:].rearrange("p (h k) -> p h k", h=nh), AX.X, ALU.min))
                        if i >= 2:
                            ins = v.scalar_tensor_tensor(out=abias[:, i % 2, hs], in0=amin[:, hs], scalar=C_A, in1=gmin[:, hs],
                                                         op0=ALU.mult, op1=ALU.min)
                        else:
                            ins = v.tensor_scalar(abias[:, i % 2, hs], amin[:, hs], C_A, None, ALU.mult)
                        ins.then_inc(a_bias, 1)
                        if h0 + nh == H and i >= 2:
                            ng = 2 * (i - 1)
                            v.wait_ge(a_bias, u + 1)
                            v.tensor_tensor(gt[:, 0:ng * H].rearrange("p (g h) -> p g h", h=H),
                                            abias[:, i % 2, :].unsqueeze(1).broadcast_to([P, ng, H]),
                                            sgs[:, 0:ng * H].rearrange("p (g h) -> p g h", h=H), ALU.subtract).then_inc(a_gt, 1)

                    def a_gmin(i):
                        ng = 2 * (i - 1)
                        if i > 2:
                            v.wait_ge(a_gt, i - 2)
                        v.wait_ge(a_filled, filled(SLOTS_A, ("glob", i)))
                        v.tensor_scalar(sgs[:, 0:ng * H], SA[:, 0:ng * H], C_A, None, ALU.mult).then_inc(a_read, 1)
                        v.wait_ge(a_read, misc(SLOTS_A, ("glob", i)))
                        done(v.tensor_reduce(gmin[:], sgs[:, 0:ng * H].rearrange("p (g h) -> p h g", h=H), AX.X, ALU.min))

                    def a_norm(i):
                        if i >= 2:
                            v.wait_ge(a_out, i - 1)
                        else:
                            v.wait_ge(a_pv, upto(UNITS_A, i))
                        if i >= 1:
                            v.wait_ge(a_filled, filled(SLOTS_A, ("turn_out", i - 1)))
                        o = OA[:, 0:H * (DA + 1)].rearrange("p (h d) -> p h d", d=DA + 1)
                        done(v.reciprocal(rden_a[:], o[:, :, DA]))
                        v.tensor_tensor(oa[:].rearrange("p (h d) -> p h d", d=DA), o[:, :, 0:DA],
                                        rden_a[:].unsqueeze(2).broadcast_to([P, H, DA]), ALU.mult).then_inc(a_normed, 1)

                    def front(n):
                        if n == 0:
                            if has_attention:
                                v.wait_ge(x_loaded, 16)
                            else:
                                v.wait_ge(x_first, 16)
                            ln_stats(FR, x_in)
                        if n == 2:
                            ln_apply(FR, 1 + before, x_in, FR.xn)
                        if n == 5:
                            v.wait_ge(xh_ready, 1)
                            v.tensor_tensor(xl_a[:], SA[:], xh_a[:], ALU.subtract).then_inc(xl_ready, 1)
                            v.wait_ge(xl_ready, 1)
                            for k, part in enumerate((xh_a, xl_a)):
                                ins = v.tensor_copy(xg[:, k, :].rearrange("p (g h) -> p g h", h=H),
                                                    part[:, 0:NG * STRIDE:STRIDE].unsqueeze(2).broadcast_to([P, NG, H]))
                            ins.then_inc(xg_ready, 1)
                        if 7 <= n < 15:
                            a = n - 7
                            kind, grp = 1 - a // 4, a % 4
                            v.wait_ge(a_hi, a + 1)
                            dst = ka4 if kind else qa4
                            v.scalar_tensor_tensor(out=dst[:, grp, :], in0=ht[:, a % 2, :], scalar=lo_rows[:, kind:kind + 1],
                                                   in1=PROJ_A[a % 2][:], op0=ALU.mult, op1=ALU.add).then_inc(a_stacked, 1)
                        if n == 15:
                            v.wait_ge(a_stacked, 8)
                            for r in range(GR):
                                v.tensor_scalar(qm[:, 0, r:H:GR, :], qa4[:, :, 0:P], head_rows[:, r:r + 1], None, ALU.mult)
                        if n == 16:
                            v.wait_ge(va_hi, 1)
                            v.tensor_tensor(val[:, :, :, 0:DA].rearrange("p t h d -> p (t h) d"),
                                            SA[:].rearrange("p (t d) -> p t d", d=DA),
                                            vah[:, :, :, 0:DA].rearrange("p t h d -> p (t h) d"), ALU.subtract).then_inc(va_ready, 1)
                            v.wait_ge(vg_proj, 1)
                            one = blk[0:NG * H, :].unsqueeze(2).broadcast_to([NG * H, H, DA])
                            done(v.scalar_tensor_tensor(out=vgt[:], in0=OA[0:NG * H, 0:D].rearrange("p (h d) -> p h d", d=DA),
                                                        scalar=1.0 / WS, in1=one, op0=ALU.mult, op1=ALU.mult))
                            done(v.tensor_copy(vgh[:, :, 0:DA], vgt[:]))
                            v.tensor_tensor(vgl[:, :, 0:DA], vgt[:], vgh[:, :, 0:DA], ALU.subtract).then_inc(vg_ready, 1)
                        if A0 <= n < AM:
                            slot, sub = (n - A0) // 3, (n - A0) % 3
                            kind, arg = at(SLOTS_A, slot)
                            if sub == 0 and kind == "unit":
                                a_min(arg)
                            if sub == 1:
                                u = unit(SLOTS_A, slot - 1)
                                if u is not None:
                                    v.wait_ge(a_pthi, u + 1)
                                    v.tensor_tensor(ptl_a[:, u % 2, :], TA[:], pth_a[:, u % 2, :], ALU.subtract
                                                    ).then_inc(a_ptlo, 1)
                                if kind == "glob":
                                    a_gmin(arg)
                                if kind == "y":
                                    v.wait_ge(a_filled, filled(SLOTS_A, (kind, arg)))
                                    v.tensor_tensor(x_a[:, arg, :], SA[:, 0:D], x_in[:, arg, :], ALU.add).then_inc(a_added, 1)
                            if sub == 2:
                                u = unit(SLOTS_A, slot - 2)
                                if u is not None and sum(UNITS_A[u][1:]) == H:
                                    a_norm(UNITS_A[u][0])
                                if kind == "turn_glob":
                                    ng = 2 * (arg - 1)
                                    v.wait_ge(a_ghi, arg - 1)
                                    v.tensor_tensor(pgl[0:ng * H, :], SA[0:ng * H, 0:P], pgh[0:ng * H, :], ALU.subtract
                                                    ).then_inc(a_read, 1)
                        if n == AM:
                            v.wait_ge(a_added, T)
                        if n >= AM:
                            mix(FR, 1, n - AM, x_a, x_next)

                    def b_rsplit(kind):
                        v.wait_ge(b_rn, kind + 1)
                        if kind:
                            v.wait_ge(b_fan, 8)
                        done(v.tensor_copy(rnh[:], rn[:]))
                        v.scalar_tensor_tensor(out=rns[:], in0=rnh[:], scalar=lo_rows[0:96, 2:3], in1=rn[:],
                                               op0=ALU.mult, op1=ALU.add).then_inc(b_rns, 1)

                    def b_save(a):
                        j = a if a < 8 else a + 8
                        v.wait_ge(b_sq, a + 1)
                        if a > 7:
                            v.wait_ge(b_nlo, a - 7)
                        v.tensor_copy(raw[:, a % 8, :], PROJ_B[j % 3][:]).then_inc(b_raw, 1)

                    def b_norms(a):
                        v.wait_ge(b_fan, a + 1)
                        v.wait_ge(b_raw, a + 1)
                        scale = cols[:, 3:4] if a < 8 else colx[:, 0:1]
                        v.scalar_tensor_tensor(out=raw[:, a % 8, :], in0=OB[a % 2][:], scalar=scale,
                                               in1=raw[:, a % 8, :], op0=ALU.mult, op1=ALU.mult).then_inc(b_norm, 1)

                    def b_vlo(a):
                        t, hf = a // 2, a % 2
                        v.wait_ge(vb_hi, a + 1)
                        v.tensor_tensor(vbl[:, t, 8 * hf:8 * hf + 8, :].rearrange("p h d -> p (h d)"), PROJ_B[(a + 8) % 3][:],
                                        vbh[:, t, 8 * hf:8 * hf + 8, :].rearrange("p h d -> p (h d)"),
                                        ALU.subtract).then_inc(vb_lo, 1)

                    def b_nullbias(i):
                        v.wait_ge(b_filled, filled(SLOTS_B, ("null", i)))
                        v.tensor_tensor(snb[:, i % 2].rearrange("p n h -> p (n h)"), SC[:, 0:NN * H],
                                        alibi_null[:, i].rearrange("p n h -> p (n h)"), ALU.add).then_inc(b_read, 1)
                        v.wait_ge(b_read, misc(SLOTS_B, ("null", i)))
                        done(v.tensor_tensor(nmin[:], snb[:, i % 2, 0, :], snb[:, i % 2, 1, :], ALU.min))

                    def b_bias(u):
                        i, h0, nh = UNITS_B[u]
                        w = (i + 1) * P
                        v.wait_ge(b_filled, filled(SLOTS_B, ("unit", u)))
                        if u > 1:
                            v.wait_ge(b_exp, u - 1)
                        for j in range(nh):
                            s, h = slice(j * w, (j + 1) * w), slice(h0 + j, h0 + j + 1)
                            ins = v.tensor_tensor_reduce(sbias[:, u % 2, s], SC[:, s], alibi[:, h0 + j, S - w:S],
                                                         1.0, nmin[:, h], ALU.add, ALU.min, bmin[:, i % 2, h])
                        ins.then_inc(b_biased, 1)

                    def b_normal(i):
                        v.wait_ge(b_exp, upto(UNITS_B, i))
                        v.wait_ge(b_nexp, i + 1)
                        if i >= 1:
                            v.wait_ge(b_filled, filled(SLOTS_B, ("turn_out", (i - 1, 1))))
                        done(v.tensor_tensor(den[:], bden[:, i % 2, :], pn[:, 0:H], ALU.add))
                        done(v.tensor_tensor(den[:], den[:], pn[:, H:2 * H], ALU.add))
                        done(v.reciprocal(rden_b[:], den[:]))
                        for k in range(2):
                            v.wait_ge(b_out, 2 * i + k + 1)
                            hs = slice(k * OBH, (k + 1) * OBH)
                            v.tensor_tensor(ob[:, hs, :], OB[k][:].rearrange("p (h d) -> p h d", d=DB),
                                            rden_b[:, hs].unsqueeze(2).broadcast_to([P, OBH, DB]), ALU.mult).then_inc(b_normed, 1)

                    def back(n):
                        if n == 0:
                            ln_stats(BK, x_f)
                        if n == 2:
                            ln_apply(BK, 1, x_f, BK.xn)
                        if n == 3:
                            v.wait_ge(BK.ln_ready, 1)
                            ln_stats(BK, BK.xn)
                        if n == 5:
                            ln_apply(BK, 2, BK.xn, xn2)
                            v.wait_ge(b_xh, 1)
                            v.tensor_tensor(xl_b[:], TR[0][:], xh_b[:], ALU.subtract).then_inc(b_xl, 1)
                        if n == 8:
                            v.wait_ge(xq_hi, 1)
                            v.tensor_tensor(xql[:], xq[:], xqh[:], ALU.subtract).then_inc(xq_lo, 1)
                        if K0 <= n < K0 + 8:
                            b_save(n - K0)
                        if Q0 <= n < Q0 + 8:
                            b_save(8 + n - Q0)
                        for kind, at_step in ((0, V0 + 1), (1, Q0 + 8)):
                            if n == at_step:
                                v.wait_ge(b_ss, 8 * kind + 8)
                                v.wait_ge(xq_lo, 1)
                                if kind > 0:
                                    v.wait_ge(b_rns, kind)
                                v.tensor_scalar(rn[:], OB[0][0:96, :], 4.096e-21, None, ALU.max).then_inc(b_clamped, 1)
                            if n == at_step + 2:
                                b_rsplit(kind)
                        if V0 < n <= V0 + 8:
                            b_vlo(n - V0 - 1)
                        if FK0 < n <= FK0 + 8:
                            b_norms(n - FK0 - 1)
                        if FQ0 <= n < FQ0 + 4:
                            b_norms(8 + 2 * (n - FQ0))
                            b_norms(8 + 2 * (n - FQ0) + 1)
                        if B0 <= n < BM:
                            slot = n - B0
                            kind, arg = at(SLOTS_B, slot)
                            u = unit(SLOTS_B, slot - 5)
                            if u is not None and sum(UNITS_B[u][1:]) == H:
                                b_normal(UNITS_B[u][0])
                            if kind == "unit":
                                b_bias(arg)
                                i, h0, nh = UNITS_B[arg]
                                if h0 + nh == H:
                                    v.wait_ge(b_biased, arg + 1)
                                    if i > 0:
                                        v.wait_ge(b_nexp, i)
                                    v.tensor_tensor(nt[:].rearrange("p (n h) -> p n h", h=H),
                                                    bmin[:, i % 2, :].unsqueeze(1).broadcast_to([P, NN, H]),
                                                    snb[:, i % 2], ALU.subtract).then_inc(b_nt, 1)
                            if kind == "null":
                                b_nullbias(arg)
                            if kind == "y":
                                v.wait_ge(b_filled, filled(SLOTS_B, (kind, arg)))
                                v.tensor_tensor(x_b[:, arg, :], SC[:, 0:D], x_f[:, arg, :], ALU.add).then_inc(b_added, 1)
                            u = unit(SLOTS_B, slot - 3)
                            if u is not None:
                                w = UNITS_B[u][2] * (UNITS_B[u][0] + 1) * P
                                v.wait_ge(b_pthi, u + 1)
                                v.tensor_tensor(ptl[:, u % 3, 0:w], TR[u % 2][:, 0:w], pth[:, u % 3, 0:w], ALU.subtract
                                                ).then_inc(b_ptlo, 1)
                            if kind == "turn_null":
                                v.wait_ge(b_nhi2, arg + 1)
                                v.tensor_tensor(pnl[:], SC[0:NN * H, 0:P], pnh[:], ALU.subtract).then_inc(b_read, 1)
                        if n == BM:
                            v.wait_ge(b_added, T)
                        if n >= BM:
                            mix(BK, 3, n - BM, x_b, x_b)

                    run(front, back)

            nc.all_engine_barrier(sems_to_clear=range(x_loaded.num, last_sem.num + 1))

        streams(PROJECT_ONLY, None)
        streams(FRONT_ONLY, None, load=x[1])
        with nc.Fori(0, NS - 1) as seq:
            streams(BOTH, seq, load=x[(seq + 2) % NS])
        streams(BACK_ONLY, NS - 1)


WLOADS = 17

_INS = ["L0_attn_a_x", "L0_attn_a_Wqkv", "L0_attn_a_Wproj", "L0_attn_b_norm_g", "L0_attn_b_norm_b",
        "L0_attn_b_Wq", "L0_attn_b_Wkv", "L0_attn_b_q_scale", "L0_attn_b_k_scale", "L0_attn_b_null_kv",
        "L0_attn_b_Wout", "L0_ffn_W_r", "L0_ffn_W_k", "L0_ffn_W_v", "L0_ffn_mu_r", "L0_ffn_mu_k"]


def kernel(**inputs):
    import numpy as _np
    import concourse.bacc as _bacc
    from concourse import mybir as _mybir
    from concourse.bass_utils import run_bass_kernel_spmd as _run

    nc = _bacc.Bacc("TRN2", target_bir_lowering=False, num_devices=1)
    arrays, args = {}, []
    for name in _INS:
        a = _np.ascontiguousarray(inputs[name])
        arrays[f"in_{name}"] = a
        args.append(nc.dram_tensor(f"in_{name}", a.shape, _mybir.dt.from_np(a.dtype), kind="ExternalInput").ap())
    shape = inputs["L0_attn_a_x"].shape
    args.append(nc.dram_tensor("out_0", shape, _mybir.dt.float32, kind="ExternalOutput").ap())
    program(nc, *args)
    r = _run(nc, [arrays], core_ids=[0])
    return r.results[0]["out_0"]
```
